# Optimizing a Trainium2 kernel written in Bass

```python
import numpy as np
import jax
import jax.numpy as jnp

def _softmax(x, axis=-1):
    return jax.nn.softmax(x, axis=axis)

def _gelu(x):
    return jax.nn.gelu(x, approximate=True)

def _silu(x):
    return jax.nn.silu(x)

def _sigmoid(x):
    return jax.nn.sigmoid(x)

def _layernorm(x, axis=-1, eps=1e-05):
    m = jnp.mean(x, axis=axis, keepdims=True)
    v = jnp.var(x, axis=axis, keepdims=True)
    return (x - m) / jnp.sqrt(v + eps)

def _scatter_add(tgt, idx, src, axis=0):
    return tgt.at[idx].add(src)

def _segment_sum(src, seg, n):
    return jax.ops.segment_sum(src, seg, n)
kernel_name = 'mk_adaln_attn_ffn_d2_seqx_r4_682ef0'

def setup_inputs(seed: int=0):
    np.random.seed(seed)
    _w = jnp.asarray

    def _rec_inputs():
        import jax
        import jax.numpy as jnp
        _rk = jax.random.key(seed)
        x = 7.22e-05 + 1 * jax.random.normal(jax.random.fold_in(_rk, 1), (2, 1024, 256), jnp.float32)
        _lenS = 1024 - jax.random.randint(jax.random.fold_in(_rk, 7), (2,), 0, max(1, 1024 // 4) + 1, jnp.int32)
        _lenS2 = 1024 - jax.random.randint(jax.random.fold_in(_rk, 8), (2,), 0, max(1, 1024 // 4) + 1, jnp.int32)
        cond_8 = jax.random.uniform(jax.random.fold_in(_rk, 11), (2, 8), jnp.float32, 0.0, 0.999837)
        return (x, cond_8)
    x, cond_8 = _rec_inputs()

    def _L0_cond_setup():
        import jax, jax.numpy as jnp
        import numpy as np
        key = jax.random.key(seed)
        k1, k2, k3, k4, k5 = jax.random.split(key, 5)
        B, N, T, O, G = (32, 64, 256, 256, 8)
        x = jax.random.normal(k1, (B, N, T), dtype=jnp.float32)
        y = jax.random.uniform(k2, (B, G), dtype=jnp.float32)
        weight = jax.random.normal(k3, (G, O, T), dtype=jnp.float32) * (1.0 / np.sqrt(T))
        mask = jax.random.uniform(k4, (O, T), dtype=jnp.float32)
        bias = jax.random.normal(k5, (O,), dtype=jnp.float32)
        return {'x': x, 'y': y, 'weight': weight, 'mask': mask, 'bias': bias}
    _L0_cond_all = _L0_cond_setup()
    _L0_cond_in = {k: v for k, v in _L0_cond_all.items() if k in ('weight', 'mask', 'bias')}
    del _L0_cond_all

    def _L0_attn_setup():
        import jax, jax.numpy as jnp
        import numpy as np
        B, T, DM = (2, 512, 256)
        DH = 128
        NH = DM // DH
        ROTARY_BASE = 10000.0

        def fractional_rope(x, base):
            dh = x.shape[-1]
            rot, skip = jnp.split(x, 2, axis=-1)
            width = rot.shape[-1]
            half = width // 2
            t = rot.shape[-2]
            positions = jnp.arange(t)[:, None]
            dims = jnp.arange(half)
            ang_freqs = jnp.power(base, -dims / half)[None, :]
            radians = positions * ang_freqs
            cos = jnp.cos(radians).astype(x.dtype)
            sin = jnp.sin(radians).astype(x.dtype)
            even, odd = jnp.split(rot, 2, axis=-1)
            r_even = even * cos - odd * sin
            r_odd = even * sin + odd * cos
            return jnp.concatenate([r_even, r_odd, skip], axis=-1)
        key = jax.random.key(seed)
        ks = jax.random.split(key, 5)
        scale = (1.0 / DM) ** 0.5
        x = jax.random.normal(ks[0], (B, T, DM), dtype=jnp.float32)
        wq = jax.random.normal(ks[1], (NH, DM, DH), dtype=jnp.float32) * scale
        wk = jax.random.normal(ks[2], (NH, DM, DH), dtype=jnp.float32) * scale
        wv = jax.random.normal(ks[3], (NH, DM, DH), dtype=jnp.float32) * scale
        wo = jax.random.normal(ks[4], (NH * DH, DM), dtype=jnp.float32) * (1.0 / (NH * DH)) ** 0.5
        return {'x': x, 'wq': wq, 'wk': wk, 'wv': wv, 'wo': wo}
    _L0_attn_all = _L0_attn_setup()
    _L0_attn_in = {k: v for k, v in _L0_attn_all.items() if k in ('wq', 'wk', 'wv', 'wo')}
    del _L0_attn_all

    def _L0_cond2_setup():
        import jax, jax.numpy as jnp
        import numpy as np
        B, S, D = (16, 512, 256)
        E, H = (8, 512)
        key = jax.random.key(seed)
        ks = jax.random.split(key, 8)
        scale = 0.02
        x = jax.random.normal(ks[0], (B, S, D), dtype=jnp.float32)
        opcode_onehot = jax.random.uniform(ks[1], (B, E), dtype=jnp.float32)
        W_up = jax.random.normal(ks[2], (E, H, D), dtype=jnp.float32) * scale
        b_up = jnp.zeros((E, H), dtype=jnp.float32)
        W_gate = jax.random.normal(ks[3], (E, H, D), dtype=jnp.float32) * scale
        b_gate = jnp.zeros((E, H), dtype=jnp.float32)
        W_down = jax.random.normal(ks[4], (E, D, H), dtype=jnp.float32) * scale
        b_down = jnp.zeros((E, D), dtype=jnp.float32)
        return {'x': x, 'opcode_onehot': opcode_onehot, 'W_up': W_up, 'b_up': b_up, 'W_gate': W_gate, 'b_gate': b_gate, 'W_down': W_down, 'b_down': b_down}
    _L0_cond2_all = _L0_cond2_setup()
    _L0_cond2_in = {k: v for k, v in _L0_cond2_all.items() if k in ('W_up', 'b_up', 'W_gate', 'b_gate', 'W_down', 'b_down')}
    del _L0_cond2_all

    def _L0_ffn_setup():
        import jax, jax.numpy as jnp
        import numpy as np
        B, C, D = (2, 512, 256)
        I = 512
        E, K = (8, 2)
        CF = 1.25
        key = jax.random.key(seed)
        k1, k2, k3, k4 = jax.random.split(key, 4)
        scale = 0.02
        return {'hidden_states': jax.random.normal(k1, (B, C, D), jnp.float32), 'Wg': jax.random.normal(k2, (E, D), jnp.float32) * scale, 'W1': jax.random.normal(k3, (E, D, 2 * I), jnp.float32) * scale, 'W2': jax.random.normal(k4, (E, I, D), jnp.float32) * scale}
    _L0_ffn_all = _L0_ffn_setup()
    _L0_ffn_in = {k: v for k, v in _L0_ffn_all.items() if k in ('Wg', 'W1', 'W2')}
    del _L0_ffn_all

    def _L1_cond_setup():
        import jax, jax.numpy as jnp
        import numpy as np
        TOP_K = 2
        NUM_MOE_LAYERS = 12

        def _gemma_mlp(x, gate_w, up_w, down_w):
            g = jnp.einsum('bsh,hi->bsi', x, gate_w)
            u = jnp.einsum('bsh,hi->bsi', x, up_w)
            return jnp.einsum('bsi,ih->bsh', jax.nn.gelu(g, approximate=True) * u, down_w)
        key = jax.random.key(seed)
        ks = jax.random.split(key, 8)
        B, S, H, I, E = (32, 64, 256, 1024, 8)
        std = 0.02
        return {'x': jax.random.normal(ks[0], (B, S, H), jnp.float32), 'router_logits': jax.random.normal(ks[1], (B, E), jnp.float32), 'skill_gate': jax.random.normal(ks[2], (E, H, I), jnp.float32) * std, 'skill_up': jax.random.normal(ks[3], (E, H, I), jnp.float32) * std, 'skill_down': jax.random.normal(ks[4], (E, I, H), jnp.float32) * std, 'shared_gate': jax.random.normal(ks[5], (H, I), jnp.float32) * std, 'shared_up': jax.random.normal(ks[6], (H, I), jnp.float32) * std, 'shared_down': jax.random.normal(ks[7], (I, H), jnp.float32) * std}
    _L1_cond_all = _L1_cond_setup()
    _L1_cond_in = {k: v for k, v in _L1_cond_all.items() if k in ('skill_gate', 'skill_up', 'skill_down', 'shared_gate', 'shared_up', 'shared_down')}
    del _L1_cond_all

    def _L1_attn_setup():
        import jax, jax.numpy as jnp
        import numpy as np
        B, L, D = (4, 2048, 256)

        def _mingru_scan(gates, candidates):

            def combine(e1, e2):
                a1, b1 = e1
                a2, b2 = e2
                return (a2 * a1, a2 * b1 + b2)
            _, h = jax.lax.associative_scan(combine, (gates, candidates), axis=1)
            return h
        key = jax.random.key(seed)
        kx, kg, kc = jax.random.split(key, 3)
        scale = 1.0 / np.sqrt(D)
        return {'x': jax.random.normal(kx, (B, L, D), dtype=jnp.float32), 'Wg': jax.random.normal(kg, (D, D), dtype=jnp.float32) * scale, 'bg': jnp.ones((D,), dtype=jnp.float32), 'Wc': jax.random.normal(kc, (D, D), dtype=jnp.float32) * scale, 'bc': jnp.zeros((D,), dtype=jnp.float32)}
    _L1_attn_all = _L1_attn_setup()
    _L1_attn_in = {k: v for k, v in _L1_attn_all.items() if k in ('Wg', 'bg', 'Wc', 'bc')}
    del _L1_attn_all

    def _L1_cond2_setup():
        import jax, jax.numpy as jnp
        import numpy as np
        R = 16
        ALPHA = 32.0
        SCALING = ALPHA / R
        key = jax.random.key(seed)
        ks = jax.random.split(key, 6)
        B, T, C, O, E = (16, 375, 256, 256, 8)
        x = jax.random.normal(ks[0], (B, T, C), dtype=jnp.float32)
        w = jax.random.uniform(ks[1], (B, E), dtype=jnp.float32)
        W_base = jax.random.normal(ks[2], (O, C), dtype=jnp.float32) * 0.02
        b_base = jax.random.normal(ks[3], (O,), dtype=jnp.float32) * 0.02
        As = jax.random.normal(ks[4], (E, R, C), dtype=jnp.float32) * 0.02
        Bs = jax.random.normal(ks[5], (E, O, R), dtype=jnp.float32) * 0.02
        return {'x': x, 'w': w, 'W_base': W_base, 'b_base': b_base, 'As': As, 'Bs': Bs}
    _L1_cond2_all = _L1_cond2_setup()
    _L1_cond2_in = {k: v for k, v in _L1_cond2_all.items() if k in ('W_base', 'b_base', 'As', 'Bs')}
    del _L1_cond2_all

    def _L1_ffn_setup():
        import jax, jax.numpy as jnp
        import numpy as np
        EMB = 256
        FF = 4 * EMB

        def _ternary(w):
            scale = jnp.maximum(jnp.mean(jnp.abs(w)), 1e-08)
            w_t = jnp.clip(jnp.round(w / scale), -1.0, 1.0)
            return w + jax.lax.stop_gradient(w_t - w)
        key = jax.random.key(seed)
        kx, k1, k2, kb1, kb2 = jax.random.split(key, 5)
        x = jax.random.normal(kx, (4, 512, EMB), dtype=jnp.float32)
        lim1 = 1.0 / np.sqrt(EMB)
        lim2 = 1.0 / np.sqrt(FF)
        W1 = jax.random.uniform(k1, (FF, EMB), jnp.float32, -lim1, lim1)
        b1 = jax.random.uniform(kb1, (FF,), jnp.float32, -lim1, lim1)
        W2 = jax.random.uniform(k2, (EMB, FF), jnp.float32, -lim2, lim2)
        b2 = jax.random.uniform(kb2, (EMB,), jnp.float32, -lim2, lim2)
        return {'x': x, 'W1': W1, 'b1': b1, 'W2': W2, 'b2': b2}
    _L1_ffn_all = _L1_ffn_setup()
    _L1_ffn_in = {k: v for k, v in _L1_ffn_all.items() if k in ('W1', 'b1', 'W2', 'b2')}
    del _L1_ffn_all
    return {'x': x, 'cond_8': cond_8, 'L0_cond_weight': _L0_cond_in['weight'], 'L0_cond_mask': _L0_cond_in['mask'], 'L0_cond_bias': _L0_cond_in['bias'], 'L0_attn_wq': _L0_attn_in['wq'], 'L0_attn_wk': _L0_attn_in['wk'], 'L0_attn_wv': _L0_attn_in['wv'], 'L0_attn_wo': _L0_attn_in['wo'], 'L0_cond2_W_up': _L0_cond2_in['W_up'], 'L0_cond2_b_up': _L0_cond2_in['b_up'], 'L0_cond2_W_gate': _L0_cond2_in['W_gate'], 'L0_cond2_b_gate': _L0_cond2_in['b_gate'], 'L0_cond2_W_down': _L0_cond2_in['W_down'], 'L0_cond2_b_down': _L0_cond2_in['b_down'], 'L0_ffn_Wg': _L0_ffn_in['Wg'], 'L0_ffn_W1': _L0_ffn_in['W1'], 'L0_ffn_W2': _L0_ffn_in['W2'], 'L1_cond_skill_gate': _L1_cond_in['skill_gate'], 'L1_cond_skill_up': _L1_cond_in['skill_up'], 'L1_cond_skill_down': _L1_cond_in['skill_down'], 'L1_cond_shared_gate': _L1_cond_in['shared_gate'], 'L1_cond_shared_up': _L1_cond_in['shared_up'], 'L1_cond_shared_down': _L1_cond_in['shared_down'], 'L1_attn_Wg': _L1_attn_in['Wg'], 'L1_attn_bg': _L1_attn_in['bg'], 'L1_attn_Wc': _L1_attn_in['Wc'], 'L1_attn_bc': _L1_attn_in['bc'], 'L1_cond2_W_base': _L1_cond2_in['W_base'], 'L1_cond2_b_base': _L1_cond2_in['b_base'], 'L1_cond2_As': _L1_cond2_in['As'], 'L1_cond2_Bs': _L1_cond2_in['Bs'], 'L1_ffn_W1': _L1_ffn_in['W1'], 'L1_ffn_b1': _L1_ffn_in['b1'], 'L1_ffn_W2': _L1_ffn_in['W2'], 'L1_ffn_b2': _L1_ffn_in['b2']}

def reference(x, cond_8, L0_cond_weight, L0_cond_mask, L0_cond_bias, L0_attn_wq, L0_attn_wk, L0_attn_wv, L0_attn_wo, L0_cond2_W_up, L0_cond2_b_up, L0_cond2_W_gate, L0_cond2_b_gate, L0_cond2_W_down, L0_cond2_b_down, L0_ffn_Wg, L0_ffn_W1, L0_ffn_W2, L1_cond_skill_gate, L1_cond_skill_up, L1_cond_skill_down, L1_cond_shared_gate, L1_cond_shared_up, L1_cond_shared_down, L1_attn_Wg, L1_attn_bg, L1_attn_Wc, L1_attn_bc, L1_cond2_W_base, L1_cond2_b_base, L1_cond2_As, L1_cond2_Bs, L1_ffn_W1, L1_ffn_b1, L1_ffn_W2, L1_ffn_b2):
    import jax
    import jax.numpy as jnp

    def _L0_cond_ref(x, y, weight, mask, bias):
        import jax, jax.numpy as jnp
        import numpy as np
        masked_w = weight * mask[None, :, :]
        w_bot = jnp.einsum('bg,got->bot', y, masked_w)
        return jnp.einsum('bnt,bot->bno', x, w_bot) + bias

    def _L0_attn_ref(x, wq, wk, wv, wo):
        import jax, jax.numpy as jnp
        import numpy as np
        B, T, DM = (2, 512, 256)
        DH = 128
        NH = DM // DH
        ROTARY_BASE = 10000.0

        def fractional_rope(x, base):
            dh = x.shape[-1]
            rot, skip = jnp.split(x, 2, axis=-1)
            width = rot.shape[-1]
            half = width // 2
            t = rot.shape[-2]
            positions = jnp.arange(t)[:, None]
            dims = jnp.arange(half)
            ang_freqs = jnp.power(base, -dims / half)[None, :]
            radians = positions * ang_freqs
            cos = jnp.cos(radians).astype(x.dtype)
            sin = jnp.sin(radians).astype(x.dtype)
            even, odd = jnp.split(rot, 2, axis=-1)
            r_even = even * cos - odd * sin
            r_odd = even * sin + odd * cos
            return jnp.concatenate([r_even, r_odd, skip], axis=-1)
        b, t, dm = x.shape
        q = jnp.einsum('btd,hdk->bhtk', x, wq)
        k = jnp.einsum('btd,hdk->bhtk', x, wk)
        v = jnp.einsum('btd,hdk->bhtk', x, wv)
        q = fractional_rope(q, ROTARY_BASE)
        k = fractional_rope(k, ROTARY_BASE)
        inv_sqrt_dh = DH ** (-0.5)
        q = q * inv_sqrt_dh
        k = k * inv_sqrt_dh
        s = jnp.einsum('bhik,bhjk->bhij', q, k)
        i = jnp.arange(t)[:, None]
        j = jnp.arange(t)[None, :]
        mask = jnp.less(i, j).astype(s.dtype)
        s = s - 1e+30 * mask
        p = jax.nn.softmax(s, axis=-1)
        o = jnp.einsum('bhij,bhjv->bihv', p, v)
        o = jnp.reshape(o, (b, t, NH * DH))
        return jnp.einsum('bto,od->btd', o, wo)

    def _L0_cond2_ref(x, opcode_onehot, W_up, b_up, W_gate, b_gate, W_down, b_down):
        import jax, jax.numpy as jnp
        import numpy as np
        B, S, D = (16, 512, 256)
        E, H = (8, 512)
        expert = jnp.argmax(opcode_onehot, axis=-1)
        wu, bu = (W_up[expert], b_up[expert])
        wg, bg = (W_gate[expert], b_gate[expert])
        wd, bd = (W_down[expert], b_down[expert])
        up = jnp.einsum('bsd,bhd->bsh', x, wu) + bu[:, None, :]
        gate = jnp.einsum('bsd,bhd->bsh', x, wg) + bg[:, None, :]
        hidden = jax.nn.silu(up) * gate
        out = jnp.einsum('bsh,bdh->bsd', hidden, wd) + bd[:, None, :]
        return out

    def _L0_ffn_ref(hidden_states, Wg, W1, W2):
        import jax, jax.numpy as jnp
        import numpy as np
        B, C, D = (2, 512, 256)
        I = 512
        E, K = (8, 2)
        CF = 1.25
        Bx, Cx, d = hidden_states.shape
        N = Bx * Cx
        cap = int(N * K * CF / E)
        x = hidden_states.reshape(N, d)
        logits = x @ Wg.T
        top_v, top_i = jax.lax.top_k(logits, K)
        gates = jax.nn.softmax(top_v, axis=-1)
        flat_e = top_i.reshape(N * K)
        gates_f = gates.reshape(N * K)
        tok = jnp.repeat(jnp.arange(N), K)
        onehot = jax.nn.one_hot(flat_e, E, dtype=jnp.int32)
        pos = jnp.cumsum(onehot, axis=0) - 1
        pos_f = jnp.take_along_axis(pos, flat_e[:, None], axis=1)[:, 0]
        keep = pos_f < cap
        pos_safe = jnp.where(keep, pos_f, cap)
        exp_batches = jnp.zeros((E, cap, d), x.dtype).at[flat_e, pos_safe].set(x[tok], mode='drop')
        h = jnp.einsum('ecd,edf->ecf', exp_batches, W1)
        inp, gate = jnp.split(h, 2, axis=-1)
        h = jax.nn.gelu(inp, approximate=False) * gate
        exp_out = jnp.einsum('eci,eid->ecd', h, W2)
        gathered = exp_out[flat_e, jnp.minimum(pos_safe, cap - 1)]
        contrib = jnp.where(keep, gates_f, 0.0)[:, None] * gathered
        out = jax.ops.segment_sum(contrib, tok, num_segments=N)
        return out.reshape(Bx, Cx, d)

    def _L1_cond_ref(x, router_logits, skill_gate, skill_up, skill_down, shared_gate, shared_up, shared_down):
        import jax, jax.numpy as jnp
        import numpy as np
        TOP_K = 2
        NUM_MOE_LAYERS = 12

        def _gemma_mlp(x, gate_w, up_w, down_w):
            g = jnp.einsum('bsh,hi->bsi', x, gate_w)
            u = jnp.einsum('bsh,hi->bsi', x, up_w)
            return jnp.einsum('bsi,ih->bsh', jax.nn.gelu(g, approximate=True) * u, down_w)
        B = x.shape[0]
        E = skill_gate.shape[0]
        rw = jax.nn.softmax(router_logits.astype(jnp.float32), axis=-1)
        w, sel = jax.lax.top_k(rw, TOP_K)
        w = w / w.sum(axis=-1, keepdims=True)
        w = w.astype(x.dtype)
        scale = 1.0 / NUM_MOE_LAYERS
        w = scale * w + (1.0 - scale) * jax.lax.stop_gradient(w)
        dense_w = jnp.zeros((B, E), x.dtype).at[jnp.arange(B)[:, None], sel].add(w)

        def step(acc, params):
            g, u, d, we = params
            return (acc + we[:, None, None] * _gemma_mlp(x, g, u, d), None)
        out, _ = jax.lax.scan(step, jnp.zeros_like(x), (skill_gate, skill_up, skill_down, dense_w.T))
        out = out + _gemma_mlp(x, shared_gate, shared_up, shared_down)
        return out

    def _L1_attn_ref(x, Wg, bg, Wc, bc):
        import jax, jax.numpy as jnp
        import numpy as np
        B, L, D = (4, 2048, 256)

        def _mingru_scan(gates, candidates):

            def combine(e1, e2):
                a1, b1 = e1
                a2, b2 = e2
                return (a2 * a1, a2 * b1 + b2)
            _, h = jax.lax.associative_scan(combine, (gates, candidates), axis=1)
            return h
        gates = jax.nn.sigmoid(jnp.einsum('bld,ed->ble', x, Wg) + bg)
        candidates = jnp.tanh(jnp.einsum('bld,ed->ble', x, Wc) + bc)
        return _mingru_scan(gates, candidates)

    def _L1_cond2_ref(x, w, W_base, b_base, As, Bs):
        import jax, jax.numpy as jnp
        import numpy as np
        R = 16
        ALPHA = 32.0
        SCALING = ALPHA / R
        out = jnp.einsum('btc,oc->bto', x, W_base) + b_base
        h = jnp.einsum('btc,erc->bter', x, As)
        lora = jnp.einsum('bter,eor,be->bto', h, Bs, w)
        return out + lora * SCALING

    def _L1_ffn_ref(x, W1, b1, W2, b2):
        import jax, jax.numpy as jnp
        import numpy as np
        EMB = 256
        FF = 4 * EMB

        def _ternary(w):
            scale = jnp.maximum(jnp.mean(jnp.abs(w)), 1e-08)
            w_t = jnp.clip(jnp.round(w / scale), -1.0, 1.0)
            return w + jax.lax.stop_gradient(w_t - w)
        h = jnp.einsum('bsd,fd->bsf', x, _ternary(W1)) + b1
        h = jax.nn.gelu(h, approximate=False)
        out = jnp.einsum('bsf,df->bsd', h, _ternary(W2)) + b2
        return out
    x = x + _L0_attn_ref(_L0_cond_ref(x, cond_8, L0_cond_weight, L0_cond_mask, L0_cond_bias), L0_attn_wq, L0_attn_wk, L0_attn_wv, L0_attn_wo)
    x = x + _L0_ffn_ref(_L0_cond2_ref(x, cond_8, L0_cond2_W_up, L0_cond2_b_up, L0_cond2_W_gate, L0_cond2_b_gate, L0_cond2_W_down, L0_cond2_b_down), L0_ffn_Wg, L0_ffn_W1, L0_ffn_W2)
    x = x + _L1_attn_ref(_L1_cond_ref(x, cond_8, L1_cond_skill_gate, L1_cond_skill_up, L1_cond_skill_down, L1_cond_shared_gate, L1_cond_shared_up, L1_cond_shared_down), L1_attn_Wg, L1_attn_bg, L1_attn_Wc, L1_attn_bc)
    x = x + _L1_ffn_ref(_L1_cond2_ref(x, cond_8, L1_cond2_W_base, L1_cond2_b_base, L1_cond2_As, L1_cond2_Bs), L1_ffn_W1, L1_ffn_b1, L1_ffn_W2, L1_ffn_b2)
    return x

_drawn_inputs = setup_inputs


def setup_inputs(seed=0):
    import zlib

    import numpy as np

    out = dict(_drawn_inputs(seed))
    spreads = {'L0_cond2_b_up': (0.0, 0.1),
     'L0_cond2_b_gate': (0.0, 0.1),
     'L0_cond2_b_down': (0.0, 0.1),
     'L1_attn_bg': (1.0, 0.2),
     'L1_attn_bc': (0.0, 0.1)}
    factors = {}
    for name, (base, spread) in spreads.items():
        noise = np.random.default_rng([zlib.crc32(name.encode()), seed]).standard_normal(out[name].shape)
        drawn = base * np.exp(spread * noise) if base else spread * noise
        out[name] = jnp.asarray(drawn.astype(out[name].dtype))
    for name, factor in factors.items():
        out[name] = (out[name] * factor).astype(out[name].dtype)
    return out
```

```python
import numpy as np
import concourse.bass as bass
from concourse import mybir
from concourse.alu_op_type import AluOpType as ALU

F32 = mybir.dt.float32
F32R = mybir.dt.float32r
BF16 = mybir.dt.bfloat16
I32 = mybir.dt.int32
ACT = mybir.ActivationFunctionType
AX = mybir.AxisListType

P = 128
B, T, D = 2, 1024, 256
N = B * T
KD = D // P
CH = 512
NCH = N // CH
CPB = T // CH
G = 8
NH, DH = 2, 128
HR = 32
H0 = 512
I0 = 512
CAP = int(N * 2 * 1.25 / 8)
ST = CAP // P
HALF = CAP // 2
NT = N // P
TPB = T // P
I1 = 1024
R = 16
FF = 4 * D
LOW = 32
HIGH = CAP // LOW
MASK = -1.0e30 * DH
PK0 = 2 * KD * H0 + (H0 // P) * D + 2 * (H0 // P)
PKF = KD * 2 * I0 + (I0 // P) * D
PK1 = 2 * KD * I1 + (I1 // P) * D


class Event:

    def __init__(self, nc, name, by=1):
        self.sem, self.count, self.by = nc.alloc_semaphore(name), 0, by

    def mark(self, ins):
        ins.then_inc(self.sem, self.by)
        self.count += self.by
        return (self, self.count)


def wait(eng, *marks):
    for m in marks:
        if m is not None:
            eng.wait_ge(m[0].sem, m[1])


class Ring:

    def __init__(self, slots):
        self.slots, self.free, self.at = slots, [() for _ in slots], -1

    def take(self, eng):
        self.at = (self.at + 1) % len(self.slots)
        wait(eng, *self.free[self.at])
        return self.at, self.slots[self.at]

    def release(self, i, *marks):
        self.free[i] = marks


def program(nc, A, out):
    pe, act, dve, pool, sp = nc.tensor, nc.scalar, nc.vector, nc.gpsimd, nc.sync

    def f(ap):
        return ap.bitcast(F32)

    base0 = (nc.sbuf_base + 63) // 64 * 64
    top = [base0]
    serial = [0]

    def sb(name, shape, dt=F32):
        size = int(np.prod(shape[1:])) * (2 if dt == BF16 else 4)
        serial[0] += 1
        t = nc.alloc_sbuf_tensor_at(f"{name}_{serial[0]}", shape, dt, offset=top[0])
        top[0] += (size + 31) // 32 * 32
        assert top[0] <= nc.sbuf_usable_end, (name, top[0])
        return t

    banks = nc.alloc_psum_tensor("banks", [P, 8, CH], F32)

    def dma_event(name):
        return Event(nc, name, 16)

    xT = sb("residual", [P, KD, N])
    inH = sb("input_hi", [P, KD, N], F32R)
    inL = sb("input_lo", [P, KD, N], F32R)
    stage = sb("weight_stage", [P, 6160])
    ident = sb("identity", [P, P])
    ident16 = sb("identity_bf16", [P, P], BF16)
    causal = sb("causal_mask", [P, P], BF16)
    before = sb("earlier_token", [P, P], BF16)
    ones16 = sb("ones_bf16", [P, P], BF16)
    ones32 = sb("ones", [P, P])
    rev = sb("eight_minus_expert", [P, G])
    cond = sb("conditioning", [P, B, G])
    dyn0 = sb("rows_of_L0_cond2", [P, B], I32)
    dynb = sb("expert_of_L0_cond2", [P, B], I32)
    dyn1 = sb("rows_of_L1_cond", [P, B * 2], I32)
    wsel = sb("L1_expert_weight", [P, B, 2])
    lane = sb("partition_number", [P, 1])
    bias_c = sb("cond_bias", [P, KD])
    bias_g = sb("gru_biases", [P, 2, KD])
    bias_b = sb("base_bias", [P, KD])
    bias_1 = sb("ffn_bias_1", [P, FF // P])
    bias_2 = sb("ffn_bias_2", [P, KD])
    tiny = sb("tiny", [P, 512])
    phase_top = top[0]

    rows_in = nc.dram_tensor("routed_input", [N, D], F32, kind="Internal").ap()
    rows_out = nc.dram_tensor("expert_output", [G * CAP, D], F32, kind="Internal").ap()

    e_phase = Event(nc, "phase_end")
    e_const = Event(nc, "constants")
    e_vec = Event(nc, "dve_small_step")
    e_acs = Event(nc, "act_small_step")
    e_hi = Event(nc, "hi_written")
    e_lo = Event(nc, "lo_written")
    e_wlo = Event(nc, "weight_lo_by_pool")
    e_mm = Event(nc, "product_in_psum")

    def v_step(ins):
        m = e_vec.mark(ins)
        wait(dve, m)
        return m

    def phase_end(*stores):
        wait(dve, *stores)
        for eng in (pe, act, dve, pool):
            m = e_phase.mark(eng.drain())
        for eng in (pe, act, dve, pool, sp):
            wait(eng, m)
        top[0] = phase_top

    def products(bank, terms):
        n = len(terms)
        for i, (wh, wl, dh, dl) in enumerate(terms):
            pe.matmul(bank, wh, dh, start=(i == 0), stop=False)
            pe.matmul(bank, wh, dl, start=False, stop=False)
            last = pe.matmul(bank, wl, dh, start=False, stop=(i == n - 1))
        return last

    def split_weights(hi, lo, src, ready, lo_eng=None, lo_event=None):
        lo_eng = lo_eng or pool
        lo_event = lo_event or (e_wlo if lo_eng is pool else e_lo)
        wait(act, *ready)
        h = e_hi.mark(act.copy(hi, src))
        wait(lo_eng, h)
        return lo_event.mark(lo_eng.tensor_tensor(lo, src, f(hi), ALU.subtract))

    def evacuate(hi, lo, bank, bias, ready, free):
        wait(act, ready, *free)
        if bias is None:
            h = e_hi.mark(act.copy(hi, bank))
        else:
            h = e_hi.mark(act.activation(hi, bank, ACT.Identity, bias=bias))
        wait(dve, h)
        if bias is None:
            return e_lo.mark(dve.tensor_tensor(lo, bank, f(hi), ALU.subtract))
        return e_lo.mark(dve.scalar_tensor_tensor(lo, bank, bias, f(hi), ALU.add, ALU.subtract))

    def split_rows(hi, lo, src, ready):
        wait(act, *ready)
        h = e_hi.mark(act.copy(hi, src))
        wait(dve, h)
        return e_lo.mark(dve.tensor_tensor(lo, src, f(hi), ALU.subtract))

    def load(eng, dst, src, name, *after):
        wait(eng, *after)
        ev = dma_event(name)
        return ev.mark(eng.dma_start(dst, src))

    ld_cond = load(act, cond[:, :, :], A["cond_8"].rearrange("b g -> (b g)").rearrange("(a n) -> a n", a=1).broadcast_to((P, B * G)).rearrange("p (b g) -> p b g", b=B), "ld_cond")
    cw_st = stage[:, 0:2048].rearrange("p (g o) -> p g o", g=G)

    for t, v in ((ident, 0.0), (ident16, 0.0), (causal, 0.0), (before, 1.0), (ones16, 1.0), (ones32, 1.0)):
        c0 = e_const.mark(pool.memset(t[:, :], v))
    wait(pool, c0)
    pool.affine_select(out=ident[:, :], in_=ident[:, :], compare_op=ALU.not_equal, fill=1.0, base=0, pattern=[[-1, P]], channel_multiplier=1)
    pool.affine_select(out=ident16[:, :], in_=ident16[:, :], compare_op=ALU.not_equal, fill=1.0, base=0, pattern=[[-1, P]], channel_multiplier=1)
    pool.affine_select(out=causal[:, :], in_=causal[:, :], compare_op=ALU.is_ge, fill=MASK, base=0, pattern=[[-1, P]], channel_multiplier=1)
    pool.affine_select(out=before[:, :], in_=before[:, :], compare_op=ALU.is_gt, fill=0.0, base=0, pattern=[[1, P]], channel_multiplier=-1)
    pool.iota(rev[:, :], [[-1, G]], base=G, channel_multiplier=0, allow_small_or_imprecise_dtypes=True)
    consts = e_const.mark(pool.iota(lane[:, :], [[0, 1]], base=0, channel_multiplier=1, allow_small_or_imprecise_dtypes=True))
    wait(dve, consts)
    wait(pe, consts)

    def first_max(vals, groups, m, onehot, tmp, tmp1):
        def wide(ap):
            return ap.rearrange("p (g a) -> p g a", a=1).broadcast_to((P, groups, G))
        revb = rev[:, :].rearrange("p (a g) -> p a g", a=1).broadcast_to((P, groups, G))
        v_step(dve.tensor_reduce(m, vals, AX.X, ALU.max))
        v_step(dve.tensor_tensor(tmp, vals, wide(m), ALU.is_equal))
        v_step(dve.tensor_tensor(tmp, tmp, revb, ALU.mult))
        v_step(dve.tensor_reduce(tmp1, tmp, AX.X, ALU.max))
        v_step(dve.tensor_tensor(onehot, revb, wide(tmp1), ALU.is_equal))

    def second_input(dst, vals, onehot):
        v_step(dve.scalar_tensor_tensor(dst, onehot, -3.0e38, vals, ALU.mult, ALU.add))

    def expert_number(dst, onehot, groups, tmp):
        revb = rev[:, :].rearrange("p (a g) -> p a g", a=1).broadcast_to((P, groups, G))
        v_step(dve.tensor_tensor(tmp, onehot, revb, ALU.mult))
        v_step(dve.tensor_reduce(dst, tmp, AX.X, ALU.add))
        v_step(dve.tensor_scalar(dst, dst, -1.0, float(G), ALU.mult, ALU.add))

    def t3(at, g):
        return tiny[:, at:at + g * G].rearrange("p (g e) -> p g e", e=G)
    v0, oh, tm, sm, rw, v2 = (t3(16 * i, B) for i in range(6))
    m1, m2, s1, ex = (tiny[:, 96 + 2 * i:98 + 2 * i] for i in range(4))
    wait(dve, ld_cond)
    wait(act, ld_cond)
    first_max(cond[:, :, :], B, m1, oh, tm, s1)
    expert_number(ex, oh, B, tm)
    v_step(dve.tensor_copy(dynb[:, :], ex))
    picked = v_step(dve.tensor_scalar(dyn0[:, :], ex, float(P), lane[:, 0:1], ALU.mult, ALU.add))
    m1w = m1.rearrange("p (g a) -> p g a", a=1).broadcast_to((P, B, G))
    d0 = v_step(dve.tensor_tensor(v0, cond[:, :, :], m1w, ALU.subtract))
    wait(act, d0)
    x0 = e_acs.mark(act.activation(rw, v0, ACT.Exp))
    wait(dve, x0)
    v_step(dve.tensor_reduce(s1, rw, AX.X, ALU.add))
    v_step(dve.reciprocal(s1, s1))
    v_step(dve.tensor_tensor(rw, rw, s1.rearrange("p (g a) -> p g a", a=1).broadcast_to((P, B, G)), ALU.mult))
    first_max(rw, B, m1, oh, tm, s1)
    expert_number(ex, oh, B, tm)
    d1 = dyn1[:, :].rearrange("p (b k) -> p b k", k=2)
    v_step(dve.tensor_scalar(d1[:, :, 0], ex, float(P), lane[:, 0:1], ALU.mult, ALU.add))
    second_input(v2, rw, oh)
    first_max(v2, B, m2, oh, tm, s1)
    expert_number(ex, oh, B, tm)
    v_step(dve.tensor_scalar(d1[:, :, 1], ex, float(P), lane[:, 0:1], ALU.mult, ALU.add))
    v_step(dve.tensor_tensor(s1, m1, m2, ALU.add))
    v_step(dve.reciprocal(s1, s1))
    a0, a1 = tiny[:, 104:106], tiny[:, 106:108]
    for k, m in enumerate((m1, m2)):
        v_step(dve.tensor_tensor(a0, m, s1, ALU.mult))
        v_step(dve.tensor_scalar(a1, a0, 1.0 - 1.0 / 12, None, ALU.mult))
        picked1 = v_step(dve.scalar_tensor_tensor(wsel[:, :, k], a0, 1.0 / 12, a1, ALU.mult, ALU.add))

    cwH = sb("cond_weight_hi", [P, KD, D], F32R)
    cwL = sb("cond_weight_lo", [P, KD, D], F32R)
    cwF = sb("cond_weight", [P, KD, D])
    cmask = sb("cond_mask", [P, KD, D])
    aW = sb("attention_weights_hi", [P, 4, KD, D], F32R)
    aWl = sb("attention_weights_lo", [P, 4, KD, D], F32R)
    kH = sb("key_hi", [P, NH, T], F32R)
    kL = sb("key_lo", [P, NH, T], F32R)
    qH = sb("query_hi", [P, NH, CH], F32R)
    qL = sb("query_lo", [P, NH, CH], F32R)
    vH = sb("value_hi", [P, TPB, D], F32R)
    vL = sb("value_lo", [P, TPB, D], F32R)
    ptH = [sb("probT_hi", [P, CH // P * (c + 1), CH], F32R) for c in range(CPB)]
    ptL = [sb("probT_lo", [P, CH // P * (c + 1), CH], F32R) for c in range(CPB)]
    prob = [sb("prob", [P, T]) for _ in range(2)]
    ropeC = sb("rope_cos", [P, T])
    ropeS = sb("rope_sin", [2 * HR, T])
    cross = sb("rope_cross", [2 * HR, CH])
    stat = sb("softmax_stats", [P, 4 * 16])

    ld_x = [load(sp, xT[:, :, c * CH:(c + 1) * CH], A["xT"][:, :, c * CH:(c + 1) * CH], f"ld_x{c}") for c in range(1)]
    ld_mask = load(sp, cmask[:, :, :], A["cond_mask"], "ld_cmask")
    cw_ld = [load(sp, stage[:, 2048 * k:2048 * (k + 1)].rearrange("p (g o) -> p g o", g=G), A["cond_w"][:, k], f"ld_cw{k}") for k in range(KD)]
    aw_st = stage[:, 4096:6144]
    ld_x += [load(sp, xT[:, :, c * CH:(c + 1) * CH], A["xT"][:, :, c * CH:(c + 1) * CH], f"ld_x{c}") for c in range(1, NCH)]
    ld_small = Event(nc, "ld_small", 16)
    for dst, src in ((bias_c, "cond_bias"), (bias_b, "base_bias"), (bias_1, "ffn_b1"), (bias_2, "ffn_b2")):
        small = ld_small.mark(act.dma_start(dst[:, :], A[src]))
    small = ld_small.mark(act.dma_start(bias_g[:, :, :], A["gru_b"]))
    small = ld_small.mark(act.dma_start(ropeC[:, :], A["ropeC"]))
    small = ld_small.mark(act.dma_start(ropeS[:, :], A["ropeS"]))
    aw_ld = load(act, aw_st.rearrange("p (w k o) -> p w k o", w=4, k=KD), A["attn_w"], "ld_attn_w")
    wait(act, small)
    wait(dve, small)
    attn_w = split_weights(aW[:, :, :, :], aWl[:, :, :, :], aw_st.rearrange("p (w k o) -> p w k o", w=4, k=KD), (aw_ld,))
    in_x = [None] * NCH

    def split_input(c, ready):
        s = slice(c * CH, (c + 1) * CH)
        return split_rows(inH[:, :, s], inL[:, :, s], xT[:, :, s], (ready,))

    b_score = Ring([banks[:, 0:2, :], banks[:, 2:4, :]])
    b_turn = Ring([banks[:, 4, :], banks[:, 5, :]])
    b_out = Ring([banks[:, 6, :], banks[:, 7, :]])
    r_prob = Ring(prob)
    e_s = Event(nc, "scores")
    e_t = Event(nc, "probs_turned")
    e_exp = Event(nc, "exponentials")
    e_norm = Event(nc, "probs_normed")
    e_rope = Event(nc, "rope_by_pool")
    e_x = Event(nc, "residual_updated")
    x_done = [None] * NCH
    turned_free = [()] * CPB
    cross_free = None
    q_free = k_free = v_free = ()
    cw_free = ()
    tile = 0

    def conditioned_weights(b):
        nonlocal cw_free
        wait(dve, *cw_ld)
        wait(dve, ld_mask)
        for k in range(KD):
            st = stage[:, 2048 * k:2048 * (k + 1)].rearrange("p (g o) -> p g o", g=G)
            v_step(dve.tensor_scalar(cwF[:, k, :], st[:, 0, :], cond[:, b, 0:1], None, ALU.mult))
            for g in range(1, G):
                v_step(dve.scalar_tensor_tensor(cwF[:, k, :], st[:, g, :], cond[:, b, g:g + 1], cwF[:, k, :], ALU.mult, ALU.add))
        m = v_step(dve.tensor_tensor(cwF[:, :, :], cwF[:, :, :], cmask[:, :, :], ALU.mult))
        wait(dve, *cw_free)
        return split_rows(cwH[:, :, :], cwL[:, :, :], cwF[:, :, :], (m, *cw_free))

    def linear(c, wh, wl, bias, ready):
        s = slice(c * CH, (c + 1) * CH)
        got = []
        wait(pe, *ready)
        for m in range(KD):
            i, bank = b_out.take(pe)
            t = e_mm.mark(products(bank, [(wh[:, k, m * P:(m + 1) * P], wl[:, k, m * P:(m + 1) * P], inH[:, k, s], inL[:, k, s]) for k in range(KD)]))
            got.append((i, bank, t))
        for m, (i, bank, t) in enumerate(got):
            lo = evacuate(inH[:, m, s], inL[:, m, s], bank, bias[:, m:m + 1], t, (got[-1][2],))
            b_out.release(i, lo)
        return lo

    for b in range(B):
        chunks = [b * CPB + c for c in range(CPB)]
        for c in chunks:
            in_x[c] = split_input(c, ld_x[c])
        cw = conditioned_weights(b)
        for c in chunks:
            in_x[c] = linear(c, cwH, cwL, bias_c, (cw, in_x[c]))
        cw_free = ((e_mm, e_mm.count),)
        wait(pe, attn_w)

        def rotated(w, h, c, hi, lo, free):
            nonlocal cross_free
            s = slice(c * CH, (c + 1) * CH)
            pos = slice((c % CPB) * CH, (c % CPB + 1) * CH)
            wait(pe, in_x[c])
            i, bank = b_out.take(pe)
            hs = slice(h * DH, (h + 1) * DH)
            t = e_mm.mark(products(bank, [(aW[:, w, k, hs], aWl[:, w, k, hs], inH[:, k, s], inL[:, k, s]) for k in range(KD)]))
            wait(dve, t)
            j, r = r_prob.take(dve)
            r = r[:, 0:CH]
            wait(dve, cross_free)
            dve.tensor_tensor(r, bank, ropeC[:, pos], ALU.mult)
            dve.tensor_tensor(cross[0:HR, :], bank[HR:2 * HR, :], ropeS[HR:2 * HR, pos], ALU.mult)
            u = e_vec.mark(dve.tensor_tensor(cross[HR:2 * HR, :], bank[0:HR, :], ropeS[0:HR, pos], ALU.mult))
            b_out.release(i, u)
            wait(pool, u)
            v = e_rope.mark(pool.tensor_tensor(r[0:2 * HR, :], r[0:2 * HR, :], cross[:, :], ALU.add))
            cross_free = v
            wait(act, *free)
            lo_m = split_rows(hi, lo, r, (v,))
            r_prob.release(j, lo_m)
            return lo_m

        k_ready = None
        for c in range(CPB):
            for h in range(NH):
                s = slice(c * CH, (c + 1) * CH)
                k_ready = rotated(1, h, chunks[c], kH[:, h, s], kL[:, h, s], k_free)
        for t in range(TPB):
            ts = slice(b * T + t * P, b * T + (t + 1) * P)
            i, bank = b_out.take(pe)
            m = e_mm.mark(products(bank[:, 0:D], [(inH[:, k, ts], inL[:, k, ts], aW[:, 2, k, :], aWl[:, 2, k, :]) for k in range(KD)]))
            v_ready = evacuate(vH[:, t, :], vL[:, t, :], bank[:, 0:D], None, m, v_free)
            b_out.release(i, v_ready)

        for c in range(CPB):
            for h in range(NH):
                q_ready = rotated(0, h, chunks[c], qH[:, h, :], qL[:, h, :], q_free)
            att = []
            for h in range(NH):
                tiles = []

                def scores(i):
                    nonlocal tile
                    qt = c * (CH // P) + i
                    width = (qt + 1) * P
                    qs = slice(i * P, (i + 1) * P)
                    wait(pe, q_ready, k_ready)
                    si, sc = b_score.take(pe)
                    flat = sc.rearrange("p a n -> p (a n)")
                    for n0 in range(0, width, CH):
                        n1 = min(n0 + CH, width)
                        o = flat[:, n0:n1]
                        pe.matmul(o, qH[:, h, qs], kH[:, h, n0:n1], start=True, stop=False)
                        pe.matmul(o, qH[:, h, qs], kL[:, h, n0:n1], start=False, stop=False)
                        last = pe.matmul(o, qL[:, h, qs], kH[:, h, n0:n1], start=False, stop=(n1 < width))
                    m = e_s.mark(pe.matmul(flat[:, width - P:width], ident16[:, :], causal[:, :], start=False, stop=True))
                    so = 4 * (tile % 16)
                    tile += 1
                    mx, nb, l, r = (stat[:, so + a:so + a + 1] for a in range(4))
                    wait(dve, m)
                    v_step(dve.tensor_reduce(mx, flat[:, 0:width], AX.X, ALU.max))
                    u = v_step(dve.tensor_scalar(nb, mx, -1.0 / DH, None, ALU.mult))
                    pi, pr = r_prob.take(act)
                    wait(act, u)
                    x = e_exp.mark(act.activation(pr[:, 0:width], flat[:, 0:width], ACT.Exp, bias=nb, scale=1.0 / DH, accum_out=l))
                    b_score.release(si, x)
                    wait(dve, x)
                    u = v_step(dve.reciprocal(r, l))
                    wait(pool, u, x)
                    n = e_norm.mark(pool.tensor_scalar(pr[:, 0:width], pr[:, 0:width], r, None, ALU.mult))
                    return (i, qt, pi, pr, n)

                def turn(i, qt, pi, pr, n):
                    wait(pe, n)
                    for k0 in range(0, qt + 1, 4):
                        k1 = min(k0 + 4, qt + 1)
                        ti, bank = b_turn.take(pe)
                        for k in range(k0, k1):
                            last = pe.transpose(bank[:, (k - k0) * P:(k - k0 + 1) * P], pr[:, k * P:(k + 1) * P], ident[:, :])
                        m = e_t.mark(last)
                        src = bank[:, 0:(k1 - k0) * P].rearrange("p (k q) -> p k q", q=P)
                        lo = evacuate(ptH[c][:, k0:k1, i * P:(i + 1) * P], ptL[c][:, k0:k1, i * P:(i + 1) * P], src, None, m, turned_free[c])
                        b_turn.release(ti, lo)
                    r_prob.release(pi, m)
                    return lo

                pend = [scores(0)]
                for i in range(1, CH // P):
                    pend.append(scores(i))
                    turn(*pend.pop(0))
                lo = turn(*pend.pop(0))
                wait(pe, lo, v_ready)
                oi, bank = b_out.take(pe)
                hs = slice(h * DH, (h + 1) * DH)
                nk = (c + 1) * (CH // P)
                for k in range(nk):
                    q0 = max(0, k - c * (CH // P)) * P
                    a, p_h, p_l = bank[:, q0:CH], ptH[c][:, k, q0:CH], ptL[c][:, k, q0:CH]
                    pe.matmul(a, vH[:, k, hs], p_h, start=(k == 0), stop=False)
                    pe.matmul(a, vH[:, k, hs], p_l, start=False, stop=False)
                    last = pe.matmul(a, vL[:, k, hs], p_h, start=False, stop=(k == nk - 1))
                m = e_mm.mark(last)
                turned_free[c] = (m,)
                s = slice(chunks[c] * CH, (chunks[c] + 1) * CH)
                lo = evacuate(inH[:, h, s], inL[:, h, s], bank, None, m, ())
                b_out.release(oi, lo)
            q_free = ((e_s, e_s.count),)
            s = slice(chunks[c] * CH, (chunks[c] + 1) * CH)
            wait(pe, lo)
            for m_ in range(KD):
                oi, bank = b_out.take(pe)
                ms = slice(m_ * P, (m_ + 1) * P)
                m = e_mm.mark(products(bank, [(aW[:, 3, k, ms], aWl[:, 3, k, ms], inH[:, k, s], inL[:, k, s]) for k in range(KD)]))
                wait(dve, m)
                x = e_x.mark(dve.tensor_tensor(xT[:, m_, s], bank, xT[:, m_, s], ALU.add))
                b_out.release(oi, x)
            x_done[chunks[c]] = x
            wait(act, m)
            in_x[chunks[c]] = split_input(chunks[c], x)
        k_free = q_free
        v_free = turned_free[CPB - 1]
    phase_end()
    gates = sb("route_gates", [P, 2, NT])
    rows = sb("route_rows", [P, 2, NT], I32)
    slot_token = sb("token_of_slot", [P, G * ST], I32)
    routed_top = top[0]
    HT = H0 // P
    wBh = [sb("expert0_hi", [P, PK0 - 2 * HT], F32R) for _ in range(B)]
    wBl = [sb("expert0_lo", [P, PK0 - 2 * HT], F32R) for _ in range(B)]
    bB = [sb("expert0_biases", [P, 2, HT]) for _ in range(B)]
    downB = [sb("expert0_bias_down", [P, D]) for _ in range(B)]
    wgT = sb("router_weights", [P, KD, G])
    act_out = [sb("silu", [P, CH]) for _ in range(2)]
    prod = [sb("hidden", [P, CH]) for _ in range(2)]
    hidH = [sb("hidden_hi", [P, HT, CH], F32R) for _ in range(2)]
    hidL = [sb("hidden_lo", [P, HT, CH], F32R) for _ in range(2)]
    xrow = [sb("x_rows", [P, D]) for _ in range(4)]
    xcol = [sb("x_columns", [P, KD, P]) for _ in range(2)]

    def parts(ap, n):
        return (ap[:, 0:KD * n].rearrange("p (k n) -> p k n", k=KD), ap[:, KD * n:2 * KD * n].rearrange("p (k n) -> p k n", k=KD),
                ap[:, 2 * KD * n:2 * KD * n + (n // P) * D].rearrange("p (k n) -> p k n", n=D))

    wait(pool, picked)
    w_ready = []
    for b in range(B):
        st = stage[:, b * PK0:(b + 1) * PK0]
        ev = dma_event(f"ld_pack0_{b}")
        a = ev.mark(pool.indirect_dma_start(st, None, A["pack0"], bass.IndirectOffsetOnAxis(ap=dyn0[:, b:b + 1], axis=0)))
        ev2 = dma_event(f"ld_bdown_{b}")
        a2 = ev2.mark(pool.indirect_dma_start(downB[b][:, :], None, A["b_down"], bass.IndirectOffsetOnAxis(ap=dynb[:, b:b + 1], axis=0)))
        n = PK0 - 2 * HT
        w_ready.append((split_weights(wBh[b][:, :], wBl[b][:, :], st[:, 0:n], (a,), dve), a2, a))
    ld_wg = load(sp, wgT[:, :, :], A["WgT"], "ld_wg")
    wait(pe, ld_wg)

    b_pair = Ring([(banks[:, 0, :], banks[:, 1, :]), (banks[:, 2, :], banks[:, 3, :])])
    b_down = Ring([banks[:, 4, :], banks[:, 5, :]])
    b_turn = Ring([banks[:, 6, :]])
    logit_bank = banks[:, 7, 0:NT * G]
    r_act, r_prod, r_hid = Ring(act_out), Ring(prod), Ring([0, 1])
    r_xrow, r_xcol = Ring(xrow), Ring(xcol)
    e_act = Event(nc, "activated")
    e_prod = Event(nc, "hidden_product")
    e_row = Event(nc, "x_row_written")
    e_col = Event(nc, "x_column_written")
    st_x = [dma_event(f"st_x{i}") for i in range(4)]

    def gated_unit(pair, func, bias, scale, gate_bias, width, hi, lo, ready, free):
        pi, (b0, b1) = pair
        ai, s = r_act.take(act)
        wait(act, ready)
        x = e_act.mark(act.activation(s[:, 0:width], b0, func, bias=bias))
        hi_, h = r_prod.take(dve)
        wait(dve, x)
        if gate_bias is not None:
            y = e_prod.mark(dve.scalar_tensor_tensor(h[:, 0:width], b1, gate_bias, s[:, 0:width], ALU.add, ALU.mult))
        elif scale is not None:
            y = e_prod.mark(dve.scalar_tensor_tensor(h[:, 0:width], b1, scale, s[:, 0:width], ALU.mult, ALU.mult))
        else:
            y = e_prod.mark(dve.tensor_tensor(h[:, 0:width], b1, s[:, 0:width], ALU.mult))
        b_pair.release(pi, y)
        r_act.release(ai, y)
        wait(act, *free)
        z = split_rows(hi, lo, h[:, 0:width], (y,))
        r_prod.release(hi_, z)
        return z

    def up_chunk(c):
        b = c // CPB
        s = slice(c * CH, (c + 1) * CH)
        uh, gh, _ = parts(wBh[b], H0)
        ul, gl, _ = parts(wBl[b], H0)
        wait(pe, in_x[c], w_ready[b][0])
        wait(act, w_ready[b][2])
        hi_, _ = r_hid.take(act)
        for i in range(HT):
            pi, pair = b_pair.take(pe)
            ms = slice(i * P, (i + 1) * P)
            products(pair[0], [(uh[:, k, ms], ul[:, k, ms], inH[:, k, s], inL[:, k, s]) for k in range(KD)])
            m = e_mm.mark(products(pair[1], [(gh[:, k, ms], gl[:, k, ms], inH[:, k, s], inL[:, k, s]) for k in range(KD)]))
            if i == 0:
                wait(act, *bias_copied[b])
            z = gated_unit((pi, pair), ACT.Silu, bB[b][:, 0, i:i + 1], None, bB[b][:, 1, i:i + 1], CH,
                           hidH[hi_][:, i, :], hidL[hi_][:, i, :], m, ())
        return c, hi_, z

    bias_copied = []
    for b in range(B):
        wait(act, w_ready[b][2])
        o = b * PK0 + PK0 - 2 * HT
        bias_copied.append((e_acs.mark(act.copy(bB[b][:, :, :], stage[:, o:o + 2 * HT].rearrange("p (a h) -> p a h", a=2))),))

    def down_chunk(c, hi_, z):
        b = c // CPB
        dh, dl = parts(wBh[b], H0)[2], parts(wBl[b], H0)[2]
        wait(pe, z)
        wait(dve, w_ready[b][1])
        todo = []
        for t in range(CH // P):
            ts = slice(t * P, (t + 1) * P)
            bi, bank = b_down.take(pe)
            m = e_mm.mark(products(bank[:, 0:D], [(hidH[hi_][:, k, ts], hidL[hi_][:, k, ts], dh[:, k, :], dl[:, k, :]) for k in range(HT)]))
            xi, xr = r_xrow.take(dve)
            wait(dve, m)
            y = e_row.mark(dve.tensor_tensor(xr[:, :], bank[:, 0:D], downB[b][:, :], ALU.add))
            b_down.release(bi, y)
            tt = c * (CH // P) + t
            wait(sp, y)
            stored = st_x[xi].mark(sp.dma_start(rows_in[tt * P:(tt + 1) * P, :], xr[:, :]))
            todo.append((tt, xi, xr, y, stored))
            if len(todo) > 1:
                route_tile(*todo.pop(0))
        r_hid.release(hi_, m)
        route_tile(*todo.pop(0))

    def route_tile(tt, xi, xr, y, stored):
        wait(pe, y)
        ti, bank = b_turn.take(pe)
        for k in range(KD):
            last = pe.transpose(bank[:, k * P:(k + 1) * P], xr[:, k * P:(k + 1) * P], ident[:, :])
        m = e_t.mark(last)
        r_xrow.release(xi, m, stored)
        ci, xc = r_xcol.take(act)
        wait(act, m)
        y = e_col.mark(act.copy(xc[:, :, :], bank[:, 0:D].rearrange("p (k t) -> p k t", k=KD)))
        b_turn.release(ti, y)
        wait(pe, y)
        for k in range(KD):
            last = pe.matmul(logit_bank[:, tt * G:(tt + 1) * G], xc[:, k, :], wgT[:, k, :], start=(k == 0), stop=(k == KD - 1))
        m = e_mm.mark(last)
        r_xcol.release(ci, m)
        return m

    pend = None
    for c in range(NCH):
        now = up_chunk(c)
        if pend:
            down_chunk(*pend)
        pend = now
    down_chunk(*pend)
    logits_ready = (e_mm, e_mm.count)
    phase_end(*[(ev, ev.count) for ev in st_x])

    top[0] = routed_top
    W = NT * G
    lg, lg2, oh1, oh2, tmp, pos, Ttot, scan, keep8 = (sb(n, [P, NT, G]) for n in
        ("logits", "logits2", "onehot1", "onehot2", "route_tmp", "position", "tile_totals", "tile_scan", "routed"))
    reset = sb("scan_reset", [P, G, NT])
    M16 = sb("routed_bf16", [P, NT, G], BF16)
    m1, m2, t1, t2, kp, ek, pk = (sb(n, [P, NT]) for n in ("max1", "max2", "rt1", "rt2", "kept", "expert", "place"))
    posi, hii, loi = (sb(n, [P, NT, G], I32) for n in ("position_int", "high_int", "low_int"))
    hif, lof = (sb(n, [P, NT, G]) for n in ("high", "low"))
    ramp = sb("ramp", [P, LOW])
    tok = sb("token_number", [P, NT])
    oneA = sb("token_at_high", [P, NT, G, HIGH], F32R)
    tmpA = sb("at_high", [P, NT, G, HIGH])
    oneB = sb("at_low", [P, NT, G, P // LOW, LOW], F32R)

    def wide(ap, n=G):
        return ap.rearrange("p (g a) -> p g a", a=1).broadcast_to((P, NT, n))

    pool.memset(reset[:, :, :], 1.0)
    pool.iota(ramp[:, :], [[1, LOW]], base=0, channel_multiplier=0, allow_small_or_imprecise_dtypes=True)
    c1 = e_const.mark(pool.iota(tok[:, :], [[P, NT]], base=0, channel_multiplier=1, allow_small_or_imprecise_dtypes=True))
    wait(pool, c1)
    c1 = e_const.mark(pool.memset(reset[:, :, 0:1], 0.0))
    wait(dve, logits_ready)
    v_step(dve.tensor_copy(lg[:, :, :], logit_bank.rearrange("p (t e) -> p t e", e=G)))
    first_max(lg[:, :, :], NT, m1[:, :], oh1[:, :, :], tmp[:, :, :], t1[:, :])
    second_input(lg2[:, :, :], lg[:, :, :], oh1[:, :, :])
    first_max(lg2[:, :, :], NT, m2[:, :], oh2[:, :, :], tmp[:, :, :], t1[:, :])
    v_step(dve.tensor_tensor(keep8[:, :, :], oh1[:, :, :], oh2[:, :, :], ALU.add))
    r_m = v_step(dve.tensor_copy(M16[:, :, :], keep8[:, :, :]))
    d = v_step(dve.tensor_tensor(t1[:, :], m2[:, :], m1[:, :], ALU.subtract))
    wait(act, d)
    x = e_acs.mark(act.activation(t2[:, :], t1[:, :], ACT.Exp))
    wait(pe, r_m)
    bpos, btot = banks[:, 0, 0:W], banks[:, 1, 0:W]
    flatM = M16[:, :, :].rearrange("p t e -> p (t e)")
    pe.matmul(bpos, before[:, :], flatM, start=True, stop=True)
    mt = e_mm.mark(pe.matmul(btot, ones16[:, :], flatM, start=True, stop=True))
    wait(dve, mt, c1, x)
    et = Ttot[:, :, :].rearrange("p t e -> p (t e)").rearrange("p (e t) -> p e t", t=NT)
    sc = scan[:, :, :].rearrange("p t e -> p (t e)").rearrange("p (e t) -> p e t", t=NT)
    v_step(dve.tensor_copy(et, btot.rearrange("p (t e) -> p e t", e=G)))
    v_step(dve.tensor_tensor_scan(scan[:, :, :].rearrange("p t e -> p (t e)"), reset[:, :, :].rearrange("p e t -> p (e t)"),
                                  Ttot[:, :, :].rearrange("p t e -> p (t e)"), 0.0, ALU.mult, ALU.add))
    v_step(dve.tensor_tensor(sc, sc, et, ALU.subtract))
    v_step(dve.tensor_tensor(pos[:, :, :], bpos.rearrange("p (t e) -> p t e", e=G), sc.rearrange("p e t -> p t e"), ALU.add))
    v_step(dve.tensor_copy(posi[:, :, :], pos[:, :, :]))
    v_step(dve.tensor_single_scalar(hii[:, :, :], posi[:, :, :], 5, ALU.logical_shift_right))
    v_step(dve.tensor_single_scalar(loi[:, :, :], posi[:, :, :], LOW - 1, ALU.bitwise_and))
    v_step(dve.tensor_copy(hif[:, :, :], hii[:, :, :]))
    v_step(dve.tensor_copy(lof[:, :, :], loi[:, :, :]))
    v_step(dve.scalar_tensor_tensor(hif[:, :, :], hif[:, :, :], 1.0, keep8[:, :, :], ALU.add, ALU.mult))
    v_step(dve.tensor_scalar(hif[:, :, :], hif[:, :, :], -1.0, None, ALU.add))

    def four(ap, n):
        return ap.rearrange("p t e -> p (t e)").rearrange("p (x a) -> p x a", a=1).broadcast_to((P, W, n))

    def ramped(n):
        return ramp[:, 0:n].rearrange("p (a n) -> p a n", a=1).broadcast_to((P, W, n))
    tA = tmpA[:, :, :, :].rearrange("p t e h -> p (t e) h")
    v_step(dve.tensor_tensor(tA, four(hif[:, :, :], HIGH), ramped(HIGH), ALU.is_equal))
    v_step(dve.tensor_tensor(oneA[:, :, :, :].rearrange("p t e h -> p t (e h)"), tmpA[:, :, :, :].rearrange("p t e h -> p t (e h)"),
                             wide(tok[:, :], G * HIGH), ALU.mult))
    oB = oneB[:, :, :, :, :].rearrange("p t e q l -> p (t e) q l")
    first = v_step(dve.tensor_tensor(oB[:, :, 0, :], four(lof[:, :, :], LOW), ramped(LOW), ALU.is_equal))
    wait(act, first)
    for q in range(1, P // LOW):
        cp = e_acs.mark(act.copy(oB[:, :, q, :], f(oB[:, :, 0, :])))
    wait(pe, first, cp)
    inv = banks[:, 2, 0:G * HIGH].rearrange("p (e h) -> p e h", e=G)
    for e in range(G):
        for t in range(NT):
            last = pe.matmul(inv[:, e, :], oneB[:, t, e, :, :].rearrange("p q l -> p (q l)"), oneA[:, t, e, :], start=(t == 0), stop=(t == NT - 1))
    mi = e_mm.mark(last)
    wait(act, mi)
    for q in range(P // LOW):
        qs = slice(q * LOW, (q + 1) * LOW)
        slots_ready = e_acs.mark(act.copy(slot_token[qs, :].rearrange("p (e j) -> p e j", e=G),
                                          inv[qs, :, :].rearrange("p e (j q) -> p e j q", q=P // LOW)[:, :, :, q]))
    v_step(dve.tensor_scalar(t1[:, :], t2[:, :], 1.0, None, ALU.add))
    v_step(dve.reciprocal(t1[:, :], t1[:, :]))
    v_step(dve.tensor_tensor(t2[:, :], t2[:, :], t1[:, :], ALU.mult))
    for k, (o, gate) in enumerate(((oh1, t1), (oh2, t2))):
        v_step(dve.tensor_tensor(tmp[:, :, :], o[:, :, :], pos[:, :, :], ALU.mult))
        v_step(dve.tensor_reduce(pk[:, :], tmp[:, :, :], AX.X, ALU.add))
        expert_number(ek[:, :], o[:, :, :], NT, tmp[:, :, :])
        v_step(dve.tensor_scalar(kp[:, :], pk[:, :], float(CAP), None, ALU.is_lt))
        v_step(dve.tensor_tensor(gates[:, k, :], kp[:, :], gate[:, :], ALU.mult))
        v_step(dve.tensor_scalar(pk[:, :], pk[:, :], float(CAP - 1), None, ALU.min))
        rows_ready = v_step(dve.scalar_tensor_tensor(rows[:, k, :], ek[:, :], float(CAP), pk[:, :], ALU.mult, ALU.add))
    phase_end()

    top[0] = routed_top
    IT = I0 // P
    w1H = [sb("ffn_w1_hi", [P, KD, 2 * I0], F32R) for _ in range(2)]
    w1L = [sb("ffn_w1_lo", [P, KD, 2 * I0], F32R) for _ in range(2)]
    w2H = [sb("ffn_w2_hi", [P, IT, D], F32R) for _ in range(2)]
    w2L = [sb("ffn_w2_lo", [P, IT, D], F32R) for _ in range(2)]
    got = [sb("gathered", [P, D]) for _ in range(2 * ST)]
    xeH = [sb("expert_in_hi", [P, KD, CAP], F32R) for _ in range(2)]
    xeL = [sb("expert_in_lo", [P, KD, CAP], F32R) for _ in range(2)]
    heH = [sb("expert_hidden_hi", [P, IT, CAP], F32R) for _ in range(1)]
    heL = [sb("expert_hidden_lo", [P, IT, CAP], F32R) for _ in range(1)]
    act_out = [sb("gelu", [P, HALF]) for _ in range(2)]
    prod = [sb("hidden", [P, HALF]) for _ in range(2)]
    yrow = [sb("y_rows", [P, D]) for _ in range(4)]
    r_act, r_prod = Ring(act_out), Ring(prod)
    b_pair = Ring([(banks[:, 0, :], banks[:, 1, :]), (banks[:, 2, :], banks[:, 3, :])])
    b_turn = Ring([banks[:, 4, :], banks[:, 5, :]])
    b_down = Ring([banks[:, 6, :], banks[:, 7, :]])
    r_got, r_xe, r_he, r_y = Ring(got), Ring([0, 1]), Ring([0]), Ring(yrow)
    ld_got = [dma_event(f"gather{i}") for i in range(2 * ST)]
    ld_f = [dma_event(f"ld_packF{i}") for i in range(2)]
    st_y = [dma_event(f"st_y{i}") for i in range(4)]
    w1_free, w2_free, stage_free = [(), ()], [(), ()], [(), ()]
    e_y = Event(nc, "y_row_written")
    wait(pool, slots_ready, rows_ready)
    for i in range(4):
        wait(pool, (st_x[i], st_x[i].count))

    def fetch_weights(e):
        s = e % 2
        wait(sp, *stage_free[s])
        return ld_f[s].mark(sp.dma_start(stage[:, s * PK0:s * PK0 + PKF], A["packF"][e]))

    def split_expert(e, loaded):
        s = e % 2
        st = stage[:, s * PK0:s * PK0 + PKF]
        n1 = KD * 2 * I0
        marks = []
        for k in range(KD):
            a = 2 * I0
            marks.append(split_weights(w1H[s][:, k, :], w1L[s][:, k, :], st[:, k * a:(k + 1) * a], (loaded, *w1_free[s])))
        marks.append(split_weights(w2H[s][:, :, :], w2L[s][:, :, :], st[:, n1:PKF].rearrange("p (k n) -> p k n", n=D), (loaded, *w2_free[s])))
        stage_free[s] = (marks[-1],)
        return marks

    def gather(e):
        res = []
        for j in range(ST):
            gi, g = r_got.take(pool)
            n = e * ST + j
            res.append((gi, g, ld_got[gi].mark(pool.indirect_dma_start(g[:, :], None, rows_in, bass.IndirectOffsetOnAxis(ap=slot_token[:, n:n + 1], axis=0)))))
        return res

    def turn_in(e, tiles):
        xi, _ = r_xe.take(act)
        for j, (gi, g, m) in enumerate(tiles):
            wait(pe, m)
            ti, bank = b_turn.take(pe)
            for k in range(KD):
                last = pe.transpose(bank[:, k * P:(k + 1) * P], g[:, k * P:(k + 1) * P], ident[:, :])
            t = e_t.mark(last)
            r_got.release(gi, t)
            js = slice(j * P, (j + 1) * P)
            lo = evacuate(xeH[xi][:, :, js], xeL[xi][:, :, js], bank[:, 0:D].rearrange("p (k t) -> p k t", k=KD), None, t, ())
            b_turn.release(ti, lo)
        return xi, lo

    def up_expert(e, xi, ready, wm):
        s = e % 2
        hi_, _ = r_he.take(act)
        wait(pe, ready, *wm[0:KD])
        for h in range(2):
            hs = slice(h * HALF, (h + 1) * HALF)
            for i in range(IT):
                pi, pair = b_pair.take(pe)
                cut = [bk[:, 0:HALF] for bk in pair]
                for part in range(2):
                    ms = slice(part * I0 + i * P, part * I0 + (i + 1) * P)
                    last = products(cut[part], [(w1H[s][:, k, ms], w1L[s][:, k, ms], xeH[xi][:, k, hs], xeL[xi][:, k, hs]) for k in range(KD)])
                m = e_mm.mark(last)
                z = gated_unit((pi, cut), ACT.Gelu, 0.0, None, None, HALF, heH[hi_][:, i, hs], heL[hi_][:, i, hs], m, ())
        w1_free[s] = (m,)
        r_xe.release(xi, m)
        return hi_, z

    def down_expert(e, hi_, ready, wm):
        s = e % 2
        wait(pe, ready, wm[KD])
        for j in range(ST):
            js = slice(j * P, (j + 1) * P)
            bi, bank = b_down.take(pe)
            m = e_mm.mark(products(bank[:, 0:D], [(heH[hi_][:, k, js], heL[hi_][:, k, js], w2H[s][:, k, :], w2L[s][:, k, :]) for k in range(IT)]))
            yi, y = r_y.take(dve)
            wait(dve, m)
            c = e_y.mark(dve.tensor_copy(y[:, :], bank[:, 0:D]))
            b_down.release(bi, c)
            wait(sp, c)
            r0 = e * CAP + j * P
            r_y.release(yi, st_y[yi].mark(sp.dma_start(rows_out[r0:r0 + P, :], y[:, :])))
        w2_free[s] = (m,)
        r_he.release(hi_, m)

    loaded = [fetch_weights(0), fetch_weights(1)]
    tiles = gather(0)
    wm = split_expert(0, loaded[0])
    turned = turn_in(0, tiles)
    for e in range(G):
        if e + 1 < G:
            tiles = gather(e + 1)
        hid = up_expert(e, *turned, wm)
        if e + 1 < G:
            wm_next = split_expert(e + 1, loaded[e + 1])
            if e + 2 < G:
                loaded.append(fetch_weights(e + 2))
            turned = turn_in(e + 1, tiles)
        down_expert(e, *hid, wm)
        wm = wm_next
    phase_end(*[(ev, ev.count) for ev in st_y])

    top[0] = routed_top
    IT1 = I1 // P
    wDh = [sb("mlp_hi", [P, PK1], F32R) for _ in range(2)]
    wDl = [sb("mlp_lo", [P, PK1], F32R) for _ in range(2)]
    y1 = [sb("y_first", [P, D]) for _ in range(3)]
    y2 = [sb("y_second", [P, D]) for _ in range(3)]
    act_out = [sb("gelu", [P, CH]) for _ in range(2)]
    prod = [sb("hidden", [P, CH]) for _ in range(2)]
    hiD = [sb("hidden_hi", [P, CH], F32R) for _ in range(4)]
    loD = [sb("hidden_lo", [P, CH], F32R) for _ in range(4)]
    r_act, r_prod, r_y12, r_h = Ring(act_out), Ring(prod), Ring([0, 1, 2]), Ring([0, 1, 2, 3])
    b_pair = Ring([(banks[:, 0, :], banks[:, 1, :]), (banks[:, 2, :], banks[:, 3, :])])
    ld_y1 = [dma_event(f"ld_y1_{i}") for i in range(3)]
    ld_y2 = [dma_event(f"ld_y2_{i}") for i in range(3)]
    ld_d = dma_event("ld_mlp")
    stD_free, wD_free = (), [(), ()]
    e_comb = Event(nc, "rows_combined")

    def fetch_mlp(b, j):
        if j < 2:
            n = 2 * b + j
            wait(pool, picked1, *stD_free)
            return ld_dyn.mark(pool.indirect_dma_start(stage[:, 0:PK1], None, A["pack1"], bass.IndirectOffsetOnAxis(ap=dyn1[:, n:n + 1], axis=0)))
        wait(sp, *stD_free)
        return ld_d.mark(sp.dma_start(stage[:, 0:PK1], A["shared"]))

    ld_dyn = dma_event("ld_picked_mlp")

    def split_mlp(n, loaded, pieces):
        nonlocal stD_free
        s = n % 2
        wait(act, *wD_free[s])
        for q in pieces:
            a = PK1 // 8
            m = split_weights(wDh[s][:, q * a:(q + 1) * a], wDl[s][:, q * a:(q + 1) * a], stage[:, q * a:(q + 1) * a], (loaded,))
        stD_free = (m,)
        return m

    loaded = fetch_mlp(0, 0)
    for i in range(4):
        wait(pool, (st_y[i], st_y[i].count))

    def combine_chunk(c):
        tiles = []
        for t in range(CH // P):
            tt = c * (CH // P) + t
            i, _ = r_y12.take(pool)
            for k, (buf, ev) in enumerate(((y1, ld_y1), (y2, ld_y2))):
                got = ev[i].mark(pool.indirect_dma_start(buf[i][:, :], None, rows_out, bass.IndirectOffsetOnAxis(ap=rows[:, k, tt:tt + 1], axis=0)))
                wait(dve, got)
            g0 = v_step(dve.tensor_scalar(y1[i][:, :], y1[i][:, :], gates[:, 0, tt:tt + 1], None, ALU.mult))
            a = e_comb.mark(dve.scalar_tensor_tensor(y1[i][:, :], y2[i][:, :], gates[:, 1, tt:tt + 1], y1[i][:, :], ALU.mult, ALU.add))
            if t == 0:
                pi, pair = b_pair.take(pe)
            wait(pe, a)
            for k in range(KD):
                last = pe.transpose(pair[k][:, t * P:(t + 1) * P], y1[i][:, k * P:(k + 1) * P], ident[:, :])
            m = e_t.mark(last)
            r_y12.release(i, m)
        wait(dve, m)
        s = slice(c * CH, (c + 1) * CH)
        for k in range(KD):
            x = e_x.mark(dve.tensor_tensor(xT[:, k, s], pair[k], xT[:, k, s], ALU.add))
        b_pair.release(pi, x)
        return split_input(c, x)

    for c in range(CPB):
        in_x[c] = combine_chunk(c)
    w_m = split_mlp(0, loaded, range(8))
    acc_free = ()
    n = 0
    for b in range(B):
        pend = []

        def down_unit(j, c, i, hi_, z, s):
            wait(pe, z)
            dh, dl = parts(wDh[s], I1)[2], parts(wDl[s], I1)[2]
            first, final = (j == 0 and i == 0), (j == 2 and i == IT1 - 1)
            for m in range(KD):
                ms = slice(m * P, (m + 1) * P)
                o = banks[:, 4 + 2 * c + m, :]
                pe.matmul(o, dh[:, i, ms], hiD[hi_][:, :], start=first, stop=False)
                pe.matmul(o, dh[:, i, ms], loD[hi_][:, :], start=False, stop=False)
                last = pe.matmul(o, dl[:, i, ms], hiD[hi_][:, :], start=False, stop=final)
            m = e_mm.mark(last)
            r_h.release(hi_, m)
            return m

        for j in range(3):
            s = n % 2
            nxt = (b, j + 1) if j < 2 else (b + 1, 0)
            more = nxt[0] < B
            if more:
                loaded = fetch_mlp(*nxt)
            uh, gh, _ = parts(wDh[s], I1)[1], parts(wDh[s], I1)[0], None
            ul, gl, _ = parts(wDl[s], I1)[1], parts(wDl[s], I1)[0], None
            wait(pe, w_m, *acc_free)
            for c in range(CPB):
                cc = b * CPB + c
                ts = slice(cc * CH, (cc + 1) * CH)
                wait(pe, in_x[cc])
                for i in range(IT1):
                    pi, pair = b_pair.take(pe)
                    ms = slice(i * P, (i + 1) * P)
                    products(pair[0], [(gh[:, k, ms], gl[:, k, ms], inH[:, k, ts], inL[:, k, ts]) for k in range(KD)])
                    m = e_mm.mark(products(pair[1], [(uh[:, k, ms], ul[:, k, ms], inH[:, k, ts], inL[:, k, ts]) for k in range(KD)]))
                    hi_, _ = r_h.take(act)
                    wsc = wsel[:, b, j:j + 1] if j < 2 else None
                    z = gated_unit((pi, pair), ACT.Gelu_apprx_tanh, 0.0, wsc, None, CH, hiD[hi_][:, :], loD[hi_][:, :], m, ())
                    pend.append((j, c, i, hi_, z, s))
                    if len(pend) > 2:
                        m = down_unit(*pend.pop(0))
                    u = c * IT1 + i
                    if u == 2:
                        wD_free[(n + 1) % 2] = (m,)
                    if more and u >= 7 and u < 15:
                        w_next = split_mlp(n + 1, loaded, [u - 7])
                    if b == 0 and j == 0 and u in (3, 7):
                        cn = CPB + (u == 7)
                        in_x[cn] = combine_chunk(cn)
            w_m = w_next
            n += 1
        while pend:
            m = down_unit(*pend.pop(0))
        for c in range(CPB):
            cc = b * CPB + c
            ts = slice(cc * CH, (cc + 1) * CH)
            for k in range(KD):
                lo = evacuate(inH[:, k, ts], inL[:, k, ts], banks[:, 4 + 2 * c + k, :], None, m, ())
            in_x[cc] = lo
        acc_free = (lo,)
    phase_end()

    top[0] = routed_top
    FT = FF // P
    gw = sb("gru_weights", [P, 2, KD, D])
    gwH = sb("gru_weights_hi", [P, 2, KD, D], F32R)
    gwL = sb("gru_weights_lo", [P, 2, KD, D], F32R)
    bw = sb("base_weights", [P, KD, D])
    la = sb("lora_a", [P, D])
    lb = sb("lora_b", [P, D])
    lbw = [sb("lora_b_weighted", [P, D]) for _ in range(B)]
    crep = sb("conditioning_rows", [P, B])
    bwF = [sb("adapted_weights", [P, KD, D]) for _ in range(B)]
    bwH = [sb("adapted_weights_hi", [P, KD, D], F32R) for _ in range(B)]
    bwL = [sb("adapted_weights_lo", [P, KD, D], F32R) for _ in range(B)]
    t1w = sb("ternary_w1", [P, KD, FF], F32R)
    t2w = sb("ternary_w2", [P, FT, D], F32R)
    below = sb("below_minus_half", [P, 2048])
    gate_t = [sb("gates", [P, CH]) for _ in range(2)]
    cand_t = [sb("candidates", [P, CH]) for _ in range(2)]
    state = [sb("state", [P, CH]) for _ in range(4)]
    act_out = [sb("gelu", [P, CH]) for _ in range(3)]
    hiE = [sb("hidden_hi", [P, CH], F32R) for _ in range(4)]
    loE = [sb("hidden_lo", [P, CH], F32R) for _ in range(4)]
    outb = [sb("out", [P, CH]) for _ in range(4)]

    ld_tw = [load(sp, stage[:, 2048 * i:2048 * (i + 1)], A[k].rearrange("p k n -> p (k n)"), f"ld_{k}") for i, k in enumerate(("ffn_w1", "ffn_w2"))]
    ld_gw = load(act, gw[:, :, :, :], A["gru_w"], "ld_gru_w")
    ld_e = Event(nc, "ld_adapter", 16)
    for dst, src in ((bw[:, :, :], "base_w"), (la[:, :], "lora_a"), (lb[:, :], "lora_b"), (crep[:, :], "cond_rep")):
        ld_em = ld_e.mark(act.dma_start(dst, A[src]))
    gru_w = split_weights(gwH[:, :, :, :], gwL[:, :, :, :], gw[:, :, :, :], (ld_gw,), dve)
    b_any = Ring([banks[:, i, :] for i in range(6)])
    wait(dve, ld_em)
    wait(pe, ld_em)
    base_w = []
    for b in range(B):
        m = v_step(dve.tensor_scalar(lbw[b][:, :], lb[:, :], crep[:, b:b + 1], 2.0, ALU.mult, ALU.mult))
        wait(pe, m)
        for k in range(KD):
            i, bank = b_any.take(pe)
            t = e_mm.mark(pe.matmul(bank[:, 0:D], la[:, k * P:(k + 1) * P], lbw[b][:, :], start=True, stop=True))
            wait(dve, t)
            t = v_step(dve.tensor_tensor(bwF[b][:, k, :], bank[:, 0:D], bw[:, k, :], ALU.add))
            b_any.release(i, t)
        base_w.append(split_rows(bwH[b][:, :, :], bwL[b][:, :, :], bwF[b][:, :, :], (t,)))

    tern = []
    for n, (tw, ld) in enumerate(((t1w, ld_tw[0]), (t2w, ld_tw[1]))):
        st = stage[:, 2048 * n:2048 * (n + 1)]
        sm, half_, neg = (tiny[:, 200 + 4 * n + a:201 + 4 * n + a] for a in range(3))
        wait(dve, ld)
        v_step(dve.scalar_tensor_tensor(below[:, :], st, -1.0, st, ALU.mult, ALU.max))
        m = v_step(dve.tensor_reduce(sm, below[:, :], AX.X, ALU.add))
        wait(pe, m)
        i, bank = b_any.take(pe)
        t = e_mm.mark(pe.matmul(bank[:, 0:1], ones32[:, :], sm, start=True, stop=True))
        wait(dve, t)
        v_step(dve.tensor_scalar(half_, bank[:, 0:1], 1.0 / (FF * D), 1e-8, ALU.mult, ALU.max))
        t = v_step(dve.tensor_scalar(neg, half_, -0.5, None, ALU.mult))
        b_any.release(i, t)
        v_step(dve.tensor_scalar(half_, half_, 0.5, None, ALU.mult))
        v_step(dve.tensor_scalar(below[:, :], st, neg, None, ALU.is_lt))
        tern.append(v_step(dve.scalar_tensor_tensor(tw[:, :, :].rearrange("p k n -> p (k n)"), st, half_, below[:, :], ALU.is_gt, ALU.subtract)))

    r_gate, r_state = Ring([0, 1]), Ring(state)
    e_gate = Event(nc, "gru_gates")
    e_scan = Event(nc, "gru_states")
    wait(pe, gru_w)

    def gru_chunk(c, carry):
        s = slice(c * CH, (c + 1) * CH)
        wait(pe, in_x[c])
        new = []
        for m_ in range(KD):
            ms = slice(m_ * P, (m_ + 1) * P)
            gi, _ = r_gate.take(act)
            for w, (dst, func) in enumerate(((gate_t[gi], ACT.Sigmoid), (cand_t[gi], ACT.Tanh))):
                i, bank = b_any.take(pe)
                t = e_mm.mark(products(bank, [(gwH[:, w, k, ms], gwL[:, w, k, ms], inH[:, k, s], inL[:, k, s]) for k in range(KD)]))
                wait(act, t)
                a = e_gate.mark(act.activation(dst[:, :], bank, func, bias=bias_g[:, w, m_:m_ + 1]))
                b_any.release(i, a)
            si, st = r_state.take(dve)
            wait(dve, a)
            init = 0.0 if carry is None else carry[m_]
            h = e_scan.mark(dve.tensor_tensor_scan(st[:, :], gate_t[gi][:, :], cand_t[gi][:, :], init, ALU.mult, ALU.add))
            r_gate.release(gi, h)
            new.append(st[:, CH - 1:CH])
            wait(dve, h)
            x = e_x.mark(dve.tensor_tensor(xT[:, m_, s], st[:, :], xT[:, m_, s], ALU.add))
            r_state.release(si, x)
        wait(act, t)
        in_x[c] = split_input(c, x)
        return new

    b_out = b_any
    r_gelu, r_he2 = Ring(act_out), Ring([0, 1, 2, 3])
    r_outb = Ring(outb)
    st_out = [dma_event(f"st_out{i}") for i in range(4)]
    acc_free = ()

    def ffn_chunk(c):
        nonlocal acc_free
        s = slice(c * CH, (c + 1) * CH)
        wait(pe, in_x[c], *tern)
        pend = []

        def down(i, hi_, z):
            wait(pe, z)
            if i == 0:
                wait(pe, *acc_free)
            for m in range(KD):
                ms = slice(m * P, (m + 1) * P)
                pe.matmul(banks[:, 6 + m, :], t2w[:, i, ms], hiE[hi_][:, :], start=(i == 0), stop=False)
                last = pe.matmul(banks[:, 6 + m, :], t2w[:, i, ms], loE[hi_][:, :], start=False, stop=(i == FT - 1))
            m = e_mm.mark(last)
            r_he2.release(hi_, m)
            return m

        for i in range(FT):
            bi, bank = b_any.take(pe)
            ms = slice(i * P, (i + 1) * P)
            for k in range(KD):
                pe.matmul(bank, t1w[:, k, ms], inH[:, k, s], start=(k == 0), stop=False)
                last = pe.matmul(bank, t1w[:, k, ms], inL[:, k, s], start=False, stop=(k == KD - 1))
            m = e_mm.mark(last)
            ai, a = r_gelu.take(act)
            wait(act, m)
            x = e_act.mark(act.activation(a[:, :], bank, ACT.Gelu, bias=bias_1[:, i:i + 1]))
            b_any.release(bi, x)
            hi_, _ = r_he2.take(act)
            z = split_rows(hiE[hi_][:, :], loE[hi_][:, :], a[:, :], (x,))
            r_gelu.release(ai, z)
            pend.append((i, hi_, z))
            if len(pend) > 2:
                down(*pend.pop(0))
        while pend:
            m = down(*pend.pop(0))
        wait(dve, m)
        for k in range(KD):
            oi, o = r_outb.take(dve)
            y = e_x.mark(dve.scalar_tensor_tensor(o[:, :], banks[:, 6 + k, :], bias_2[:, k:k + 1], xT[:, k, s], ALU.add, ALU.add))
            wait(sp, y)
            r_outb.release(oi, st_out[oi].mark(sp.dma_start(out[:, k, s], o[:, :])))
        acc_free = (y,)

    carry = None
    for b in range(B):
        carry = None
        for c in range(CPB):
            carry = gru_chunk(b * CPB + c, carry)
    for c in range(NCH):
        in_x[c] = linear(c, bwH[c // CPB], bwL[c // CPB], bias_b, (base_w[c // CPB], in_x[c]))
    for c in range(NCH):
        ffn_chunk(c)
    for ev in st_out:
        wait(sp, (ev, ev.count))


def kernel(**inputs):
    import concourse.bacc as _bacc
    from concourse.bass_utils import run_bass_kernel_spmd as _run
    a = {k: np.asarray(v) for k, v in inputs.items()}

    def cols(w, k):
        return w.reshape(k, P, -1).transpose(1, 0, 2)

    def heads(w):
        return w.transpose(1, 0, 2).reshape(D, NH * DH)

    half = HR
    freq = np.power(np.float32(10000.0), (-np.arange(half).astype(np.float32) / np.float32(half)))
    rad = freq[:, None] * np.arange(T, dtype=np.float32)[None, :]
    cos, sin = np.cos(rad), np.sin(rad)
    arrays = {
        "xT": a["x"].reshape(N, D).T.reshape(KD, P, N).transpose(1, 0, 2),
        "cond_8": a["cond_8"],
        "cond_w": a["L0_cond_weight"].transpose(2, 0, 1).reshape(KD, P, G, D).transpose(1, 0, 2, 3),
        "cond_mask": cols(a["L0_cond_mask"].T, KD),
        "cond_bias": a["L0_cond_bias"].reshape(KD, P).T,
        "attn_w": np.stack([cols(heads(a["L0_attn_wq"]), KD), cols(heads(a["L0_attn_wk"]), KD),
                            cols(heads(a["L0_attn_wv"]), KD), cols(a["L0_attn_wo"], KD)], axis=1),
        "ropeC": np.concatenate([cos, cos, np.ones((P - 2 * HR, T), np.float32)]),
        "ropeS": np.concatenate([sin, -sin]),
        "cond_rep": np.repeat(a["cond_8"].T, R, axis=0),
        "pack0": np.concatenate([
            a["L0_cond2_W_up"].transpose(0, 2, 1).reshape(G, KD, P, H0).transpose(0, 2, 1, 3).reshape(G, P, -1),
            a["L0_cond2_W_gate"].transpose(0, 2, 1).reshape(G, KD, P, H0).transpose(0, 2, 1, 3).reshape(G, P, -1),
            a["L0_cond2_W_down"].transpose(0, 2, 1).reshape(G, H0 // P, P, D).transpose(0, 2, 1, 3).reshape(G, P, -1),
            a["L0_cond2_b_up"].reshape(G, H0 // P, P).transpose(0, 2, 1),
            a["L0_cond2_b_gate"].reshape(G, H0 // P, P).transpose(0, 2, 1)], axis=2).reshape(G * P, PK0),
        "b_down": a["L0_cond2_b_down"],
        "WgT": cols(a["L0_ffn_Wg"].T, KD),
        "packF": np.concatenate([
            a["L0_ffn_W1"].reshape(G, KD, P, 2 * I0).transpose(0, 2, 1, 3).reshape(G, P, -1),
            a["L0_ffn_W2"].reshape(G, I0 // P, P, D).transpose(0, 2, 1, 3).reshape(G, P, -1)], axis=2),
        "pack1": np.concatenate([
            a["L1_cond_skill_gate"].reshape(G, KD, P, I1).transpose(0, 2, 1, 3).reshape(G, P, -1),
            a["L1_cond_skill_up"].reshape(G, KD, P, I1).transpose(0, 2, 1, 3).reshape(G, P, -1),
            a["L1_cond_skill_down"].reshape(G, I1 // P, P, D).transpose(0, 2, 1, 3).reshape(G, P, -1)], axis=2).reshape(G * P, PK1),
        "shared": np.concatenate([cols(a["L1_cond_shared_gate"], KD).reshape(P, -1), cols(a["L1_cond_shared_up"], KD).reshape(P, -1),
                                  cols(a["L1_cond_shared_down"], I1 // P).reshape(P, -1)], axis=1),
        "gru_w": np.stack([cols(a["L1_attn_Wg"].T, KD), cols(a["L1_attn_Wc"].T, KD)], axis=1),
        "gru_b": np.stack([a["L1_attn_bg"].reshape(KD, P).T, a["L1_attn_bc"].reshape(KD, P).T], axis=1),
        "base_w": cols(a["L1_cond2_W_base"].T, KD),
        "base_bias": a["L1_cond2_b_base"].reshape(KD, P).T,
        "lora_a": a["L1_cond2_As"].reshape(G * R, D),
        "lora_b": a["L1_cond2_Bs"].transpose(0, 2, 1).reshape(G * R, D),
        "ffn_w1": cols(a["L1_ffn_W1"].T, KD),
        "ffn_b1": a["L1_ffn_b1"].reshape(FF // P, P).T,
        "ffn_w2": cols(a["L1_ffn_W2"].T, FF // P),
        "ffn_b2": a["L1_ffn_b2"].reshape(KD, P).T,
    }
    arrays = {k: np.ascontiguousarray(v) for k, v in arrays.items()}
    nc = _bacc.Bacc("TRN2", target_bir_lowering=False, num_devices=1)
    A = {k: nc.dram_tensor(f"in_{k}", v.shape, mybir.dt.from_np(v.dtype), kind="ExternalInput").ap() for k, v in arrays.items()}
    out = nc.dram_tensor("out_xT", (P, KD, N), F32, kind="ExternalOutput").ap()
    program(nc, A, out)
    r = _run(nc, [{f"in_{k}": v for k, v in arrays.items()}], core_ids=[0])
    got = r.results[0]["out_xT"]
    return np.ascontiguousarray(got.transpose(1, 0, 2).reshape(D, N).T.reshape(B, T, D))
```

```python
import numpy as np
import concourse.bass as bass
from concourse import mybir
from concourse.alu_op_type import AluOpType as ALU

F32 = mybir.dt.float32
F32R = mybir.dt.float32r
BF16 = mybir.dt.bfloat16
I32 = mybir.dt.int32
ACT = mybir.ActivationFunctionType
AX = mybir.AxisListType

P = 128
B, T, D = 2, 1024, 256
N = B * T
KD = D // P
CH = 512
NCH = N // CH
CPB = T // CH
G = 8
NH, DH = 2, 128
HR = 32
H0 = 512
I0 = 512
CAP = int(N * 2 * 1.25 / 8)
ST = CAP // P
HALF = CAP // 2
NT = N // P
TPB = T // P
I1 = 1024
R = 16
FF = 4 * D
LOW = 32
HIGH = CAP // LOW
MASK = -1.0e30 * DH
PK0 = 2 * KD * H0 + (H0 // P) * D + 2 * (H0 // P)
PKF = KD * 2 * I0 + (I0 // P) * D
PK1 = 2 * KD * I1 + (I1 // P) * D


class Event:

    def __init__(self, nc, name, by=1):
        self.sem, self.count, self.by = nc.alloc_semaphore(name), 0, by

    def mark(self, ins):
        ins.then_inc(self.sem, self.by)
        self.count += self.by
        return (self, self.count)


def wait(eng, *marks):
    for m in marks:
        if m is not None:
            eng.wait_ge(m[0].sem, m[1])


class Ring:

    def __init__(self, slots):
        self.slots, self.free, self.at = slots, [() for _ in slots], -1

    def take(self, eng):
        self.at = (self.at + 1) % len(self.slots)
        wait(eng, *self.free[self.at])
        return self.at, self.slots[self.at]

    def release(self, i, *marks):
        self.free[i] = marks


def run_all(steps):
    while True:
        try:
            next(steps)
        except StopIteration as end:
            return end.value


def interleave(main, side, every=1, per=1):
    n, live = 0, True
    result = None
    while True:
        try:
            next(main)
        except StopIteration as end:
            result = end.value
            break
        n += 1
        if live and n % every == 0:
            for _ in range(per):
                try:
                    next(side)
                except StopIteration:
                    live = False
                    break
    if live:
        for _ in side:
            pass
    return result


def program(nc, A, out):
    pe, act, dve, pool, sp = nc.tensor, nc.scalar, nc.vector, nc.gpsimd, nc.sync

    def f(ap):
        return ap.bitcast(F32)

    base0 = (nc.sbuf_base + 63) // 64 * 64
    top = [base0]
    serial = [0]

    def sb(name, shape, dt=F32):
        size = int(np.prod(shape[1:])) * (2 if dt == BF16 else 4)
        serial[0] += 1
        t = nc.alloc_sbuf_tensor_at(f"{name}_{serial[0]}", shape, dt, offset=top[0])
        top[0] += (size + 31) // 32 * 32
        assert top[0] <= nc.sbuf_usable_end, (name, top[0])
        return t

    banks = nc.alloc_psum_tensor("banks", [P, 8, CH], F32)

    def dma_event(name):
        return Event(nc, name, 16)

    xT = sb("residual", [P, KD, N])
    inH = sb("input_hi", [P, KD, N], F32R)
    inL = sb("input_lo", [P, KD, N], F32R)
    stage = sb("weight_stage", [P, 6160])
    ident = sb("identity", [P, P])
    ident16 = sb("identity_bf16", [P, P], BF16)
    causal = sb("causal_mask", [P, P], BF16)
    before = sb("earlier_token", [P, P], BF16)
    ones16 = sb("ones_bf16", [P, P], BF16)
    ones32 = sb("ones", [P, P])
    rev = sb("eight_minus_expert", [P, G])
    cond = sb("conditioning", [P, B, G])
    dyn0 = sb("rows_of_L0_cond2", [P, B], I32)
    dynb = sb("expert_of_L0_cond2", [P, B], I32)
    dyn1 = sb("rows_of_L1_cond", [P, B * 2], I32)
    wsel = sb("L1_expert_weight", [P, B, 2])
    lane = sb("partition_number", [P, 1])
    bias_c = sb("cond_bias", [P, KD])
    bias_g = sb("gru_biases", [P, 2, KD])
    bias_b = sb("base_bias", [P, KD])
    bias_1 = sb("ffn_bias_1", [P, FF // P])
    bias_2 = sb("ffn_bias_2", [P, KD])
    tiny = sb("tiny", [P, 512])
    phase_top = top[0]

    rows_in = nc.dram_tensor("routed_input", [N, D], F32, kind="Internal").ap()
    rows_out = nc.dram_tensor("expert_output", [G * CAP, D], F32, kind="Internal").ap()

    e_phase = Event(nc, "phase_end")
    e_const = Event(nc, "constants")
    e_vec = Event(nc, "dve_small_step")
    e_acs = Event(nc, "act_small_step")
    e_hi = Event(nc, "hi_written")
    e_lo = Event(nc, "lo_written")
    e_wlo = Event(nc, "weight_lo_by_pool")
    e_mm = Event(nc, "product_in_psum")

    def v_step(ins):
        m = e_vec.mark(ins)
        wait(dve, m)
        return m

    def phase_end(*stores):
        wait(dve, *stores)
        for eng in (pe, act, dve, pool):
            m = e_phase.mark(eng.drain())
        for eng in (pe, act, dve, pool, sp):
            wait(eng, m)
        top[0] = phase_top

    def products(bank, terms):
        n = len(terms)
        for i, (wh, wl, dh, dl) in enumerate(terms):
            pe.matmul(bank, wh, dh, start=(i == 0), stop=False)
            pe.matmul(bank, wh, dl, start=False, stop=False)
            last = pe.matmul(bank, wl, dh, start=False, stop=(i == n - 1))
        return last

    def split_weights(hi, lo, src, ready, lo_eng=None, lo_event=None):
        lo_eng = lo_eng or pool
        lo_event = lo_event or (e_wlo if lo_eng is pool else e_lo)
        wait(act, *ready)
        h = e_hi.mark(act.copy(hi, src))
        wait(lo_eng, h)
        return lo_event.mark(lo_eng.tensor_tensor(lo, src, f(hi), ALU.subtract))

    def evacuate(hi, lo, bank, bias, ready, free):
        wait(act, ready, *free)
        if bias is None:
            h = e_hi.mark(act.copy(hi, bank))
        else:
            h = e_hi.mark(act.activation(hi, bank, ACT.Identity, bias=bias))
        wait(dve, h)
        if bias is None:
            return e_lo.mark(dve.tensor_tensor(lo, bank, f(hi), ALU.subtract))
        return e_lo.mark(dve.scalar_tensor_tensor(lo, bank, bias, f(hi), ALU.add, ALU.subtract))

    def split_rows(hi, lo, src, ready):
        wait(act, *ready)
        h = e_hi.mark(act.copy(hi, src))
        wait(dve, h)
        return e_lo.mark(dve.tensor_tensor(lo, src, f(hi), ALU.subtract))

    def load(eng, dst, src, name, *after):
        wait(eng, *after)
        ev = dma_event(name)
        return ev.mark(eng.dma_start(dst, src))

    ld_cond = load(act, cond[:, :, :], A["cond_8"].rearrange("b g -> (b g)").rearrange("(a n) -> a n", a=1).broadcast_to((P, B * G)).rearrange("p (b g) -> p b g", b=B), "ld_cond")
    cw_st = stage[:, 0:2048].rearrange("p (g o) -> p g o", g=G)

    for t, v in ((ident, 0.0), (ident16, 0.0), (causal, 0.0), (before, 1.0), (ones16, 1.0), (ones32, 1.0)):
        c0 = e_const.mark(pool.memset(t[:, :], v))
    wait(pool, c0)
    pool.affine_select(out=ident[:, :], in_=ident[:, :], compare_op=ALU.not_equal, fill=1.0, base=0, pattern=[[-1, P]], channel_multiplier=1)
    pool.affine_select(out=ident16[:, :], in_=ident16[:, :], compare_op=ALU.not_equal, fill=1.0, base=0, pattern=[[-1, P]], channel_multiplier=1)
    pool.affine_select(out=causal[:, :], in_=causal[:, :], compare_op=ALU.is_ge, fill=MASK, base=0, pattern=[[-1, P]], channel_multiplier=1)
    pool.affine_select(out=before[:, :], in_=before[:, :], compare_op=ALU.is_gt, fill=0.0, base=0, pattern=[[1, P]], channel_multiplier=-1)
    pool.iota(rev[:, :], [[-1, G]], base=G, channel_multiplier=0, allow_small_or_imprecise_dtypes=True)
    consts = e_const.mark(pool.iota(lane[:, :], [[0, 1]], base=0, channel_multiplier=1, allow_small_or_imprecise_dtypes=True))
    wait(dve, consts)
    wait(pe, consts)

    def first_max(vals, groups, m, onehot, tmp, tmp1):
        def wide(ap):
            return ap.rearrange("p (g a) -> p g a", a=1).broadcast_to((P, groups, G))
        revb = rev[:, :].rearrange("p (a g) -> p a g", a=1).broadcast_to((P, groups, G))
        v_step(dve.tensor_reduce(m, vals, AX.X, ALU.max))
        v_step(dve.tensor_tensor(tmp, vals, wide(m), ALU.is_equal))
        v_step(dve.tensor_tensor(tmp, tmp, revb, ALU.mult))
        v_step(dve.tensor_reduce(tmp1, tmp, AX.X, ALU.max))
        v_step(dve.tensor_tensor(onehot, revb, wide(tmp1), ALU.is_equal))

    def second_input(dst, vals, onehot):
        v_step(dve.scalar_tensor_tensor(dst, onehot, -3.0e38, vals, ALU.mult, ALU.add))

    def expert_number(dst, onehot, groups, tmp):
        revb = rev[:, :].rearrange("p (a g) -> p a g", a=1).broadcast_to((P, groups, G))
        v_step(dve.tensor_tensor(tmp, onehot, revb, ALU.mult))
        v_step(dve.tensor_reduce(dst, tmp, AX.X, ALU.add))
        v_step(dve.tensor_scalar(dst, dst, -1.0, float(G), ALU.mult, ALU.add))

    def pick_experts():
        def t3(at, g):
            return tiny[:, at:at + g * G].rearrange("p (g e) -> p g e", e=G)
        v0, oh, tm, sm, rw, v2 = (t3(16 * i, B) for i in range(6))
        m1, m2, s1, ex = (tiny[:, 96 + 2 * i:98 + 2 * i] for i in range(4))
        wait(dve, ld_cond)
        wait(act, ld_cond)
        first_max(cond[:, :, :], B, m1, oh, tm, s1)
        expert_number(ex, oh, B, tm)
        v_step(dve.tensor_copy(dynb[:, :], ex))
        picked = v_step(dve.tensor_scalar(dyn0[:, :], ex, float(P), lane[:, 0:1], ALU.mult, ALU.add))
        m1w = m1.rearrange("p (g a) -> p g a", a=1).broadcast_to((P, B, G))
        d0 = v_step(dve.tensor_tensor(v0, cond[:, :, :], m1w, ALU.subtract))
        wait(act, d0)
        x0 = e_acs.mark(act.activation(rw, v0, ACT.Exp))
        wait(dve, x0)
        v_step(dve.tensor_reduce(s1, rw, AX.X, ALU.add))
        v_step(dve.reciprocal(s1, s1))
        v_step(dve.tensor_tensor(rw, rw, s1.rearrange("p (g a) -> p g a", a=1).broadcast_to((P, B, G)), ALU.mult))
        first_max(rw, B, m1, oh, tm, s1)
        expert_number(ex, oh, B, tm)
        d1 = dyn1[:, :].rearrange("p (b k) -> p b k", k=2)
        v_step(dve.tensor_scalar(d1[:, :, 0], ex, float(P), lane[:, 0:1], ALU.mult, ALU.add))
        second_input(v2, rw, oh)
        first_max(v2, B, m2, oh, tm, s1)
        expert_number(ex, oh, B, tm)
        v_step(dve.tensor_scalar(d1[:, :, 1], ex, float(P), lane[:, 0:1], ALU.mult, ALU.add))
        v_step(dve.tensor_tensor(s1, m1, m2, ALU.add))
        v_step(dve.reciprocal(s1, s1))
        a0, a1 = tiny[:, 104:106], tiny[:, 106:108]
        for k, m in enumerate((m1, m2)):
            v_step(dve.tensor_tensor(a0, m, s1, ALU.mult))
            v_step(dve.tensor_scalar(a1, a0, 1.0 - 1.0 / 12, None, ALU.mult))
            picked1 = v_step(dve.scalar_tensor_tensor(wsel[:, :, k], a0, 1.0 / 12, a1, ALU.mult, ALU.add))
        return picked, picked1

    cwH = [sb("cond_weight_hi", [P, KD, D], F32R) for _ in range(B)]
    cwL = [sb("cond_weight_lo", [P, KD, D], F32R) for _ in range(B)]
    cwF = sb("cond_weight", [P, KD, D])
    cmask = sb("cond_mask", [P, KD, D])
    aW = sb("attention_weights_hi", [P, 4, KD, D], F32R)
    aWl = sb("attention_weights_lo", [P, 4, KD, D], F32R)
    kH = sb("key_hi", [P, NH, T], F32R)
    kL = sb("key_lo", [P, NH, T], F32R)
    qH = sb("query_hi", [P, NH, CH], F32R)
    qL = sb("query_lo", [P, NH, CH], F32R)
    vH = sb("value_hi", [P, TPB, D], F32R)
    vL = sb("value_lo", [P, TPB, D], F32R)
    QT = CH // P
    ptH = [sb("probT_hi", [P, QT * (c + 1), CH], F32R) for c in range(CPB)]
    ptL = [sb("probT_lo", [P, QT * (c + 1), CH], F32R) for c in range(CPB)]
    prob = [stage[:, PK0 + T * i:PK0 + T * (i + 1)] for i in range(3)]
    ropeC = sb("rope_cos", [P, T])
    ropeS = sb("rope_sin", [2 * HR, T])
    cross = sb("rope_cross", [2 * HR, CH])
    rot = [sb("rotated", [P, CH]) for _ in range(2)]
    stat = sb("softmax_stats", [P, 4 * 16])

    cond_stage = stage[:, 0:2048 * KD].rearrange("p (k g o) -> p k g o", k=KD, g=G)
    aw_st = stage[:, 4096:6144].rearrange("p (w k o) -> p w k o", w=4, k=KD)

    def load_x(c):
        return load(sp, xT[:, :, c * CH:(c + 1) * CH], A["xT"][:, :, c * CH:(c + 1) * CH], f"ld_x{c}")
    ld_x = [load_x(0)]
    ld_cw = load(sp, cond_stage, A["cond_w"], "ld_cond_w")
    ld_mask = load(sp, cmask[:, :, :], A["cond_mask"], "ld_cond_mask")
    ld_small = Event(nc, "ld_small", 16)
    small = ld_small.mark(act.dma_start(bias_c[:, :], A["cond_bias"]))
    ld_aw = load(act, aw_st, A["attn_w"], "ld_attn_w")
    small = ld_small.mark(act.dma_start(ropeC[:, :], A["ropeC"]))
    small = ld_small.mark(act.dma_start(ropeS[:, :], A["ropeS"]))
    for dst, src in ((bias_b, "base_bias"), (bias_1, "ffn_b1"), (bias_2, "ffn_b2")):
        small = ld_small.mark(act.dma_start(dst[:, :], A[src]))
    small = ld_small.mark(act.dma_start(bias_g[:, :, :], A["gru_b"]))
    ld_x += [load_x(c) for c in range(1, NCH)]

    def split_input(c, ready):
        s = slice(c * CH, (c + 1) * CH)
        return split_rows(inH[:, :, s], inL[:, :, s], xT[:, :, s], (ready,))

    def conditioned_weights(b):
        v_step(dve.tensor_scalar(cwF[:, :, :], cond_stage[:, :, 0, :], cond[:, b, 0:1], None, ALU.mult))
        for g in range(1, G):
            v_step(dve.scalar_tensor_tensor(cwF[:, :, :], cond_stage[:, :, g, :], cond[:, b, g:g + 1], cwF[:, :, :], ALU.mult, ALU.add))
        wait(dve, ld_mask)
        m = v_step(dve.tensor_tensor(cwF[:, :, :], cwF[:, :, :], cmask[:, :, :], ALU.mult))
        return split_rows(cwH[b][:, :, :], cwL[b][:, :, :], cwF[:, :, :], (m,))

    in_x = [None] * NCH
    wait(dve, ld_cond, ld_cw)
    in_x[0] = split_input(0, ld_x[0])
    cw = [conditioned_weights(0)]
    attn_w = split_weights(aW[:, :, :, :], aWl[:, :, :, :], aw_st, (ld_aw,))
    in_x[1] = split_input(1, ld_x[1])
    wait(dve, cw[0])
    cw.append(conditioned_weights(1))
    in_x[2] = split_input(2, ld_x[2])
    in_x[3] = split_input(3, ld_x[3])
    wait(act, small)
    wait(dve, small)
    wait(act, cw[1], attn_w)

    b_score = Ring([banks[:, 0:2, :], banks[:, 2:4, :]])
    b_turn = Ring([banks[:, 4, :], banks[:, 5, :]])
    b_out = Ring([banks[:, 6, :], banks[:, 7, :]])
    r_prob = Ring(prob)
    r_rot = Ring(rot)
    e_s = Event(nc, "scores")
    e_t = Event(nc, "probs_turned")
    e_exp = Event(nc, "exponentials")
    e_norm = Event(nc, "probs_normed")
    e_rope = Event(nc, "rope_by_pool")
    e_x = Event(nc, "residual_updated")
    turned_free = [()] * CPB
    cross_free = None
    q_free = k_free = v_free = ()
    k_ready, v_ready, q_ready = [None] * NCH, [None] * NT, [None] * NCH
    tile = 0

    def linear(c, wh, wl, bias, ready):
        s = slice(c * CH, (c + 1) * CH)
        got = []
        wait(pe, *ready)
        for m in range(KD):
            i, bank = b_out.take(pe)
            t = e_mm.mark(products(bank, [(wh[:, k, m * P:(m + 1) * P], wl[:, k, m * P:(m + 1) * P], inH[:, k, s], inL[:, k, s]) for k in range(KD)]))
            got.append((i, bank, t))
        for m, (i, bank, t) in enumerate(got):
            lo = evacuate(inH[:, m, s], inL[:, m, s], bank, bias[:, m:m + 1], t, (got[-1][2],))
            b_out.release(i, lo)
        return lo

    def conditioned(c):
        in_x[c] = linear(c, cwH[c // CPB], cwL[c // CPB], bias_c, (cw[c // CPB], in_x[c]))
        yield

    def rotated(w, h, c, hi, lo, free):
        nonlocal cross_free
        s = slice(c * CH, (c + 1) * CH)
        pos = slice((c % CPB) * CH, (c % CPB + 1) * CH)
        wait(pe, in_x[c], attn_w)
        i, bank = b_out.take(pe)
        hs = slice(h * DH, (h + 1) * DH)
        t = e_mm.mark(products(bank, [(aW[:, w, k, hs], aWl[:, w, k, hs], inH[:, k, s], inL[:, k, s]) for k in range(KD)]))
        yield
        wait(dve, t)
        j, r = r_rot.take(dve)
        dve.tensor_tensor(r[:, :], bank, ropeC[:, pos], ALU.mult)
        wait(dve, cross_free)
        dve.tensor_tensor(cross[0:HR, :], bank[HR:2 * HR, :], ropeS[HR:2 * HR, pos], ALU.mult)
        u = e_vec.mark(dve.tensor_tensor(cross[HR:2 * HR, :], bank[0:HR, :], ropeS[0:HR, pos], ALU.mult))
        b_out.release(i, u)
        wait(pool, u)
        v = cross_free = e_rope.mark(pool.tensor_tensor(r[0:2 * HR, :], r[0:2 * HR, :], cross[:, :], ALU.add))
        yield
        wait(act, *free)
        m = split_rows(hi, lo, r[:, :], (v,))
        r_rot.release(j, m)
        return m

    def keys(c):
        s = slice((c % CPB) * CH, (c % CPB + 1) * CH)
        for h in range(NH):
            k_ready[c] = yield from rotated(1, h, c, kH[:, h, s], kL[:, h, s], k_free)

    def values(c):
        for t in range(QT):
            tt = (c % CPB) * QT + t
            ts = slice(c * CH + t * P, c * CH + (t + 1) * P)
            wait(pe, in_x[c], attn_w)
            i, bank = b_out.take(pe)
            m = e_mm.mark(products(bank[:, 0:D], [(inH[:, k, ts], inL[:, k, ts], aW[:, 2, k, :], aWl[:, 2, k, :]) for k in range(KD)]))
            yield
            v_ready[c] = evacuate(vH[:, tt, :], vL[:, tt, :], bank[:, 0:D], None, m, v_free)
            b_out.release(i, v_ready[c])

    def queries(c):
        for h in range(NH):
            q_ready[c] = yield from rotated(0, h, c, qH[:, h, :], qL[:, h, :], q_free)

    def scores(c, h, i):
        nonlocal tile
        qt = (c % CPB) * QT + i
        width = (qt + 1) * P
        qs = slice(i * P, (i + 1) * P)
        wait(pe, q_ready[c], k_ready[c])
        si, sc = b_score.take(pe)
        flat = sc.rearrange("p a n -> p (a n)")
        for n0 in range(0, width, CH):
            n1 = min(n0 + CH, width)
            o = flat[:, n0:n1]
            pe.matmul(o, qH[:, h, qs], kH[:, h, n0:n1], start=True, stop=False)
            pe.matmul(o, qH[:, h, qs], kL[:, h, n0:n1], start=False, stop=False)
            pe.matmul(o, qL[:, h, qs], kH[:, h, n0:n1], start=False, stop=(n1 < width))
        m = e_s.mark(pe.matmul(flat[:, width - P:width], ident16[:, :], causal[:, :], start=False, stop=True))
        so = 4 * (tile % 16)
        tile += 1
        mx, nb, l, r = (stat[:, so + a:so + a + 1] for a in range(4))
        wait(dve, m)
        v_step(dve.tensor_reduce(mx, flat[:, 0:width], AX.X, ALU.max))
        u = e_vec.mark(dve.tensor_scalar(nb, mx, -1.0 / DH, None, ALU.mult))
        pi, pr = r_prob.take(act)
        wait(act, u)
        x = e_exp.mark(act.activation(pr[:, 0:width], flat[:, 0:width], ACT.Exp, bias=nb, scale=1.0 / DH, accum_out=l))
        b_score.release(si, x)
        return (c, h, i, qt, pi, pr, x, l, r)

    def norm(c, h, i, qt, pi, pr, x, l, r):
        width = (qt + 1) * P
        wait(dve, x)
        u = e_vec.mark(dve.reciprocal(r, l))
        wait(pool, u)
        n = e_norm.mark(pool.tensor_scalar(pr[:, 0:width], pr[:, 0:width], r, 1.0, ALU.mult, ALU.mult))
        return (c, h, i, qt, pi, pr, n)

    def turn(c, h, i, qt, pi, pr, n):
        cb = c % CPB
        wait(pe, n)
        for k0 in range(0, qt + 1, 4):
            k1 = min(k0 + 4, qt + 1)
            ti, bank = b_turn.take(pe)
            for k in range(k0, k1):
                last = pe.transpose(bank[:, (k - k0) * P:(k - k0 + 1) * P], pr[:, k * P:(k + 1) * P], ident[:, :])
            m = e_t.mark(last)
            src = bank[:, 0:(k1 - k0) * P].rearrange("p (k q) -> p k q", q=P)
            lo = evacuate(ptH[cb][:, k0:k1, i * P:(i + 1) * P], ptL[cb][:, k0:k1, i * P:(i + 1) * P], src, None, m, turned_free[cb])
            b_turn.release(ti, lo)
        r_prob.release(pi, m)
        return lo

    def weighted(c, h, ready):
        cb = c % CPB
        wait(pe, ready, v_ready[c])
        oi, bank = b_out.take(pe)
        hs = slice(h * DH, (h + 1) * DH)
        nk = (cb + 1) * QT
        for k in range(nk):
            q0 = max(0, k - cb * QT) * P
            a, p_h, p_l = bank[:, q0:CH], ptH[cb][:, k, q0:CH], ptL[cb][:, k, q0:CH]
            pe.matmul(a, vH[:, k, hs], p_h, start=(k == 0), stop=False)
            pe.matmul(a, vH[:, k, hs], p_l, start=False, stop=False)
            last = pe.matmul(a, vL[:, k, hs], p_h, start=False, stop=(k == nk - 1))
        m = e_mm.mark(last)
        turned_free[cb] = (m,)
        s = slice(c * CH, (c + 1) * CH)
        lo = evacuate(inH[:, h, s], inL[:, h, s], bank, None, m, ())
        b_out.release(oi, lo)
        return lo

    def project_out(c, ready):
        s = slice(c * CH, (c + 1) * CH)
        wait(pe, *ready)
        for m_ in range(KD):
            oi, bank = b_out.take(pe)
            ms = slice(m_ * P, (m_ + 1) * P)
            m = e_mm.mark(products(bank, [(aW[:, 3, k, ms], aWl[:, 3, k, ms], inH[:, k, s], inL[:, k, s]) for k in range(KD)]))
            wait(dve, m)
            x = e_x.mark(dve.tensor_tensor(xT[:, m_, s], bank, xT[:, m_, s], ALU.add))
            b_out.release(oi, x)
        wait(act, m)
        in_x[c] = split_input(c, x)

    normed, summed, todo, project = [], {}, [], []

    def attention(c):
        nonlocal q_free
        for h in range(NH):
            for i in range(QT):
                t = scores(c, h, i)
                yield
                yield from advance()
                normed.append(norm(*t))
        q_free = ((e_s, e_s.count),)

    def advance(least=1):
        if todo:
            c, h, lo = todo.pop(0)
            summed[c, h] = weighted(c, h, lo)
            if h == NH - 1:
                project.append(c)
            yield
        if len(normed) > least:
            t = normed.pop(0)
            lo = turn(*t)
            if t[2] == QT - 1:
                todo.append((t[0], t[1], lo))
            yield
        if project:
            c = project.pop(0)
            project_out(c, [summed[c, h] for h in range(NH)])
            yield

    def flush():
        while normed or todo:
            yield from advance(0)

    def chain(*steps):
        for s in steps:
            yield from s

    run_all(chain(conditioned(0), conditioned(1), keys(0), queries(0), values(0)))
    picked, picked1 = pick_experts()
    wait(pool, picked, cw[1])
    ld_pack0 = [dma_event("ld_pack0_0").mark(pool.indirect_dma_start(
        stage[:, 0:PK0], None, A["pack0"], bass.IndirectOffsetOnAxis(ap=dyn0[:, 0:1], axis=0)))]
    interleave(attention(0), chain(keys(1), values(1), conditioned(2)), every=2)
    run_all(queries(1))
    interleave(attention(1), conditioned(3), every=4)
    k_free = q_free
    run_all(chain(keys(2), queries(2)))
    run_all(flush())
    v_free = turned_free[CPB - 1]
    run_all(values(2))
    interleave(attention(2), chain(keys(3), values(3)), every=2)
    run_all(queries(3))
    run_all(attention(3))
    run_all(flush())
    phase_end()

    gates = sb("route_gates", [P, 2, NT])
    rows = sb("route_rows", [P, 2, NT], I32)
    slot_token = sb("token_of_slot", [P, G * ST], I32)
    routed_top = top[0]
    HT = H0 // P
    wBh = [sb("expert0_hi", [P, PK0 - 2 * HT], F32R) for _ in range(B)]
    wBl = [sb("expert0_lo", [P, PK0 - 2 * HT], F32R) for _ in range(B)]
    bB = [sb("expert0_biases", [P, 2, HT]) for _ in range(B)]
    downB = [sb("expert0_bias_down", [P, D]) for _ in range(B)]
    wgT = sb("router_weights", [P, KD, G])
    act_out = [sb("silu", [P, CH]) for _ in range(2)]
    prod = [sb("hidden", [P, CH]) for _ in range(2)]
    hidH = [sb("hidden_hi", [P, HT, CH], F32R) for _ in range(2)]
    hidL = [sb("hidden_lo", [P, HT, CH], F32R) for _ in range(2)]
    xrow = [sb("x_rows", [P, D]) for _ in range(6)]
    xcol = [sb("x_columns", [P, KD, P]) for _ in range(2)]
    GH = G * HIGH
    lg, lg2, oh1, oh2, tmp, pos, keep8 = (sb(n, [P, QT, G]) for n in
        ("logits", "logits2", "onehot1", "onehot2", "route_tmp", "position", "routed"))
    M16 = [sb("routed_bf16", [P, QT, G], BF16) for _ in range(2)]
    counts = [sb("routed_before", [P, G]) for _ in range(2)]
    m1, m2, t1, t2, kp, ek = (sb(n, [P, QT]) for n in ("max1", "max2", "rt1", "rt2", "kept", "expert"))
    pk = sb("place", [P, 2, QT])
    ihi, ilo = (sb(n, [P, 2, QT], I32) for n in ("high_int", "low_int"))
    column, low = (sb(n, [P, 2, QT]) for n in ("column", "low"))
    ramp = sb("ramp", [P, GH])
    ramp_low = sb("ramp_low", [P, P // LOW, LOW])
    tok = sb("token_number", [P, NT])
    at_col = [sb("token_at_column", [P, GH], F32R) for _ in range(2 * QT)]
    at_low = [sb("at_low", [P, P], F32R) for _ in range(2 * QT)]

    def parts(ap, n):
        return (ap[:, 0:KD * n].rearrange("p (k n) -> p k n", k=KD), ap[:, KD * n:2 * KD * n].rearrange("p (k n) -> p k n", k=KD),
                ap[:, 2 * KD * n:2 * KD * n + (n // P) * D].rearrange("p (k n) -> p k n", n=D))

    e_cst2 = Event(nc, "route_constants")
    e_cst2.mark(pool.memset(counts[0][:, :], 0.0))
    e_cst2.mark(pool.iota(ramp[:, :], [[1, GH]], base=0, channel_multiplier=0, allow_small_or_imprecise_dtypes=True))
    e_cst2.mark(pool.iota(ramp_low[:, :, :], [[0, P // LOW], [1, LOW]], base=0, channel_multiplier=0, allow_small_or_imprecise_dtypes=True))
    ramps = e_cst2.mark(pool.iota(tok[:, :], [[P, NT]], base=0, channel_multiplier=1, allow_small_or_imprecise_dtypes=True))

    wait(pool, picked)
    w_ready = []
    for b in range(B):
        st = stage[:, b * PK0:(b + 1) * PK0]
        n = PK0 - 2 * HT
        a = ld_pack0[b] if b == 0 else dma_event("ld_pack0_1").mark(pool.indirect_dma_start(
            st, None, A["pack0"], bass.IndirectOffsetOnAxis(ap=dyn0[:, b:b + 1], axis=0)))
        a2 = dma_event(f"ld_bdown_{b}").mark(pool.indirect_dma_start(
            downB[b][:, :], None, A["b_down"], bass.IndirectOffsetOnAxis(ap=dynb[:, b:b + 1], axis=0)))
        w_ready.append([None, a2, a])

    def prepare0(b):
        a = w_ready[b][2]
        st = stage[:, b * PK0:(b + 1) * PK0]
        n = PK0 - 2 * HT
        for q in range(3):
            qs = slice(q * n // 3, (q + 1) * n // 3)
            m = split_weights(wBh[b][:, qs], wBl[b][:, qs], st[:, qs], (a,), dve)
            if q < 2:
                yield
        w_ready[b][0] = m
        w_ready[b][2] = e_acs.mark(act.copy(bB[b][:, :, :], st[:, n:n + 2 * HT].rearrange("p (a h) -> p a h", a=2)))
        yield

    ld_wg = load(sp, wgT[:, :, :], A["WgT"], "ld_wg")
    wait(pe, ld_wg)

    b_work = Ring([banks[:, i, :] for i in range(3)])
    b_down = Ring([banks[:, 3, :], banks[:, 4, :]])
    b_turn = Ring([banks[:, 5, :], banks[:, 6, :]])
    inverse = banks[:, 7, 0:GH]
    r_act, r_prod, r_hid = Ring(act_out), Ring(prod), Ring([0, 1])
    r_xrow, r_xcol, r_at = Ring(xrow), Ring(xcol), Ring(list(range(2 * QT)))
    e_act = Event(nc, "activated")
    e_prod = Event(nc, "hidden_product")
    e_row = Event(nc, "x_row_written")
    e_col = Event(nc, "x_column_written")
    e_log = Event(nc, "logits_in_psum")
    e_cnt = Event(nc, "counts_in_psum")
    e_inv = Event(nc, "slots_in_psum")
    e_at = Event(nc, "slot_onehots")
    st_x = [dma_event(f"st_x{i}") for i in range(6)]

    def gated_unit(first, second, func, bias, scale, gate_bias, width, hi, lo):
        i0, b0, ready0 = first
        i1, b1, ready1 = second
        ai, s = r_act.take(act)
        wait(act, ready0)
        x = e_act.mark(act.activation(s[:, 0:width], b0, func, bias=bias))
        b_work.release(i0, x)
        hi_, h = r_prod.take(dve)
        wait(dve, x, ready1)
        if gate_bias is not None:
            y = e_prod.mark(dve.scalar_tensor_tensor(h[:, 0:width], b1, gate_bias, s[:, 0:width], ALU.add, ALU.mult))
        elif scale is not None:
            y = e_prod.mark(dve.scalar_tensor_tensor(h[:, 0:width], b1, scale, s[:, 0:width], ALU.mult, ALU.mult))
        else:
            y = e_prod.mark(dve.tensor_tensor(h[:, 0:width], b1, s[:, 0:width], ALU.mult))
        b_work.release(i1, y)
        r_act.release(ai, y)
        z = split_rows(hi, lo, h[:, 0:width], (y,))
        r_prod.release(hi_, z)
        return z

    def work(width, terms):
        i, bank = b_work.take(pe)
        return i, bank[:, 0:width], e_mm.mark(products(bank[:, 0:width], terms))

    hidden = {}

    def up_chunk(c):
        b = c // CPB
        s = slice(c * CH, (c + 1) * CH)
        uh, gh, _ = parts(wBh[b], H0)
        ul, gl, _ = parts(wBl[b], H0)
        wait(pe, in_x[c], w_ready[b][0])
        wait(act, w_ready[b][2])
        hi_, _ = r_hid.take(act)
        for i in range(HT):
            ms = slice(i * P, (i + 1) * P)
            up = work(CH, [(uh[:, k, ms], ul[:, k, ms], inH[:, k, s], inL[:, k, s]) for k in range(KD)])
            yield
            gate = work(CH, [(gh[:, k, ms], gl[:, k, ms], inH[:, k, s], inL[:, k, s]) for k in range(KD)])
            z = gated_unit(up, gate, ACT.Silu, bB[b][:, 0, i:i + 1], None, bB[b][:, 1, i:i + 1], CH,
                           hidH[hi_][:, i, :], hidL[hi_][:, i, :])
            hidden[c] = (hi_, z)
            yield

    x_rows = {}

    def down_chunk(c):
        b = c // CPB
        hi_, z = hidden[c]
        dh, dl = parts(wBh[b], H0)[2], parts(wBl[b], H0)[2]
        wait(pe, z)
        wait(dve, w_ready[b][1])
        for t in range(QT):
            ts = slice(t * P, (t + 1) * P)
            bi, bank = b_down.take(pe)
            m = e_mm.mark(products(bank[:, 0:D], [(hidH[hi_][:, k, ts], hidL[hi_][:, k, ts], dh[:, k, :], dl[:, k, :]) for k in range(HT)]))
            xi, xr = r_xrow.take(dve)
            wait(dve, m)
            y = e_row.mark(dve.tensor_tensor(xr[:, :], bank[:, 0:D], downB[b][:, :], ALU.add))
            b_down.release(bi, y)
            tt = c * QT + t
            wait(sp, y)
            stored = st_x[xi].mark(sp.dma_start(rows_in[tt * P:(tt + 1) * P, :], xr[:, :]))
            x_rows[tt] = (xi, xr, y, stored)
            yield
        r_hid.release(hi_, m)

    def route_chunk(c):
        nonlocal rows_ready, slot_mark
        columns = None

        def logits(t, xc, ci, y):
            wait(pe, y)
            ti, bank = b_turn.take(pe)
            for k in range(KD):
                last = pe.matmul(bank[:, 0:G], xc[:, k, :], wgT[:, k, :], start=(k == 0), stop=(k == KD - 1))
            m = e_log.mark(last)
            r_xcol.release(ci, m)
            wait(dve, m)
            y = e_vec.mark(dve.tensor_copy(lg[:, t, :], bank[:, 0:G]))
            b_turn.release(ti, y)
            return y

        for t in range(QT):
            tt = c * QT + t
            while tt not in x_rows:
                yield
            xi, xr, y, stored = x_rows[tt]
            wait(pe, y)
            ti, bank = b_turn.take(pe)
            for k in range(KD):
                last = pe.transpose(bank[:, k * P:(k + 1) * P], xr[:, k * P:(k + 1) * P], ident[:, :])
            m = e_t.mark(last)
            r_xrow.release(xi, m, stored)
            ci, xc = r_xcol.take(act)
            wait(act, m)
            y = e_col.mark(act.copy(xc[:, :, :], bank[:, 0:D].rearrange("p (k t) -> p k t", k=KD)))
            b_turn.release(ti, y)
            if columns:
                logits(*columns)
            columns = (t, xc, ci, y)
            yield
        y = logits(*columns)
        yield
        wait(dve, y)
        first_max(lg[:, :, :], QT, m1[:, :], oh1[:, :, :], tmp[:, :, :], t1[:, :])
        second_input(lg2[:, :, :], lg[:, :, :], oh1[:, :, :])
        first_max(lg2[:, :, :], QT, m2[:, :], oh2[:, :, :], tmp[:, :, :], t1[:, :])
        v_step(dve.tensor_tensor(keep8[:, :, :], oh1[:, :, :], oh2[:, :, :], ALU.add))
        r_m = v_step(dve.tensor_copy(M16[c % 2][:, :, :], keep8[:, :, :]))
        d = v_step(dve.tensor_tensor(t1[:, :], m2[:, :], m1[:, :], ALU.subtract))
        wait(act, d)
        x = e_acs.mark(act.activation(t2[:, :], t1[:, :], ACT.Exp))
        yield
        wait(pe, r_m)
        ti, bank = b_turn.take(pe)
        for t in range(QT):
            ranks = bank[:, t * G:(t + 1) * G]
            for u in range(t):
                pe.matmul(ranks, ones16[:, :], M16[c % 2][:, u, :], start=(u == 0), stop=False)
            pe.matmul(ranks, before[:, :], M16[c % 2][:, t, :], start=(t == 0), stop=True)
        for u in range(QT):
            last = pe.matmul(bank[:, QT * G:(QT + 1) * G], ones16[:, :], M16[c % 2][:, u, :], start=(u == 0), stop=(u == QT - 1))
        mt = e_cnt.mark(last)
        yield
        wait(dve, mt)
        cnt = counts[c % 2][:, :].rearrange("p (a g) -> p a g", a=1).broadcast_to((P, QT, G))
        v_step(dve.tensor_tensor(pos[:, :, :], bank[:, 0:QT * G].rearrange("p (t e) -> p t e", e=G), cnt, ALU.add))
        y = v_step(dve.tensor_tensor(counts[1 - c % 2][:, :], bank[:, QT * G:(QT + 1) * G], counts[c % 2][:, :], ALU.add))
        b_turn.release(ti, y)
        experts = []
        for k, o in enumerate((oh1, oh2)):
            v_step(dve.tensor_tensor(tmp[:, :, :], o[:, :, :], pos[:, :, :], ALU.mult))
            v_step(dve.tensor_reduce(pk[:, k, :], tmp[:, :, :], AX.X, ALU.add))
        v_step(dve.tensor_copy(ihi[:, :, :], pk[:, :, :]))
        v_step(dve.tensor_single_scalar(ilo[:, :, :], ihi[:, :, :], LOW - 1, ALU.bitwise_and))
        v_step(dve.tensor_single_scalar(ihi[:, :, :], ihi[:, :, :], 5, ALU.logical_shift_right))
        v_step(dve.tensor_copy(low[:, :, :], ilo[:, :, :]))
        v_step(dve.tensor_copy(column[:, :, :], ihi[:, :, :]))
        tk = slice(c * QT, (c + 1) * QT)
        wait(dve, x)
        v_step(dve.tensor_scalar(t1[:, :], t2[:, :], 1.0, None, ALU.add))
        v_step(dve.reciprocal(t1[:, :], t1[:, :]))
        v_step(dve.tensor_tensor(t2[:, :], t2[:, :], t1[:, :], ALU.mult))
        for k, (o, gate) in enumerate(((oh1, t1), (oh2, t2))):
            expert_number(ek[:, :], o[:, :, :], QT, tmp[:, :, :])
            v_step(dve.tensor_scalar(kp[:, :], pk[:, k, :], float(CAP), None, ALU.is_lt))
            v_step(dve.tensor_tensor(gates[:, k, tk], kp[:, :], gate[:, :], ALU.mult))
            v_step(dve.tensor_scalar(kp[:, :], kp[:, :], -4.0 * N, 4.0 * N, ALU.mult, ALU.add))
            v_step(dve.scalar_tensor_tensor(kp[:, :], ek[:, :], float(HIGH), kp[:, :], ALU.mult, ALU.add))
            v_step(dve.tensor_tensor(column[:, k, :], column[:, k, :], kp[:, :], ALU.add))
            v_step(dve.tensor_scalar(kp[:, :], pk[:, k, :], float(CAP - 1), None, ALU.min))
            rows_ready = v_step(dve.scalar_tensor_tensor(rows[:, k, tk], ek[:, :], float(CAP), kp[:, :], ALU.mult, ALU.add))
            yield
        for k in range(2):
            ready = []
            for t in range(QT):
                ai, _ = r_at.take(dve)
                tt = c * QT + t
                dve.tensor_scalar(at_col[ai][:, :], ramp[:, :], column[:, k, t:t + 1], tok[:, tt:tt + 1], ALU.is_equal, ALU.mult)
                ready.append((ai, t, e_at.mark(dve.tensor_scalar(at_low[ai][:, :], ramp_low[:, :, :].rearrange("p q l -> p (q l)"),
                                                                 low[:, k, t:t + 1], None, ALU.is_equal))))
            yield
            for ai, t, y in ready:
                wait(pe, y)
                slot_mark = e_inv.mark(pe.matmul(inverse, at_low[ai][:, :], at_col[ai][:, :], start=(c == 0 and k == 0 and t == 0),
                                                 stop=(c == NCH - 1 and k == 1 and t == QT - 1)))
                r_at.release(ai, slot_mark)

    rows_ready = slot_mark = None
    wait(dve, ramps)
    run_all(prepare0(0))
    interleave(up_chunk(0), prepare0(1))
    for c in range(NCH):
        nxt = up_chunk(c + 1) if c + 1 < NCH else iter(())
        before_it = route_chunk(c - 1) if c else iter(())
        interleave(chain(nxt, down_chunk(c)), before_it)
    run_all(route_chunk(NCH - 1))
    wait(act, slot_mark)
    inv = inverse.rearrange("p (e h) -> p e h", e=G)
    for q in range(P // LOW):
        qs = slice(q * LOW, (q + 1) * LOW)
        slots_ready = e_acs.mark(act.copy(slot_token[qs, :].rearrange("p (e j) -> p e j", e=G),
                                          inv[qs, :, :].rearrange("p e (j q) -> p e j q", q=P // LOW)[:, :, :, q]))
    phase_end(*[(ev, ev.count) for ev in st_x])

    top[0] = routed_top
    IT = I0 // P
    IT1 = I1 // P
    w1H, w1L, w2H, w2L = [], [], [], []
    for _ in range(2):
        w1H.append(sb("ffn_w1_hi", [P, KD, 2 * I0], F32R))
        w1L.append(sb("ffn_w1_lo", [P, KD, 2 * I0], F32R))
        w2H.append(sb("ffn_w2_hi", [P, IT, D], F32R))
        w2L.append(sb("ffn_w2_lo", [P, IT, D], F32R))
    heH, heL = sb("expert_hidden_hi", [P, IT, CAP], F32R), sb("expert_hidden_lo", [P, IT, CAP], F32R)
    xeH = [sb("expert_in_hi", [P, KD, CAP], F32R) for _ in range(2)]
    xeL = [sb("expert_in_lo", [P, KD, CAP], F32R) for _ in range(2)]
    got_at = top[0]
    got = [sb("gathered", [P, D]) for _ in range(ST + 1)]
    act_out = [sb("gelu", [P, CH]) for _ in range(2)]
    prod = [sb("hidden", [P, CH]) for _ in range(2)]
    yrow = [sb("y_rows", [P, D]) for _ in range(4)]
    last_top = nc.sbuf_usable_end // 32 * 32 - 4 * PK1
    assert top[0] <= last_top
    top[0] = last_top
    wDl = [sb("mlp_lo", [P, PK1], F32R)]
    top[0] = routed_top
    wDh = [sb("mlp_hi", [P, PK1], F32R) for _ in range(2)]
    wDl.append(sb("mlp_lo", [P, PK1], F32R))
    hiD = [sb("hidden_hi", [P, CH], F32R) for _ in range(4)]
    loD = [sb("hidden_lo", [P, CH], F32R) for _ in range(4)]
    assert top[0] <= got_at
    top[0] = got_at
    y1 = [sb("y_first", [P, D]) for _ in range(3)]
    y2 = [sb("y_second", [P, D]) for _ in range(3)]
    r_act, r_prod = Ring(act_out), Ring(prod)
    b_work = Ring([banks[:, i, :] for i in range(4)])
    b_turn = Ring([banks[:, 4, :], banks[:, 5, :]])
    b_down = Ring([banks[:, 6, :], banks[:, 7, :]])
    r_got, r_xe, r_he, r_y = Ring(got), Ring([0, 1]), Ring([0]), Ring(yrow)
    ld_got = [dma_event(f"gather{i}") for i in range(ST + 1)]
    ld_f = [dma_event(f"ld_packF{i}") for i in range(2)]
    st_y = [dma_event(f"st_y{i}") for i in range(4)]
    w1_free, w2_free, stage_free = [(), ()], [(), ()], [(), ()]
    e_y = Event(nc, "y_row_written")
    wait(pool, slots_ready, rows_ready)
    for i in range(6):
        wait(pool, (st_x[i], st_x[i].count))

    def fetch_weights(e):
        s = e % 2
        wait(sp, *stage_free[s])
        return ld_f[s].mark(sp.dma_start(stage[:, s * PK0:s * PK0 + PKF], A["packF"][e]))

    def split_expert(e, loaded):
        s = e % 2
        st = stage[:, s * PK0:s * PK0 + PKF]
        n1 = KD * 2 * I0
        for k in range(KD):
            for part in range(2):
                ps, a = slice(part * I0, (part + 1) * I0), (2 * k + part) * I0
                m1_ = split_weights(w1H[s][:, k, ps], w1L[s][:, k, ps], st[:, a:a + I0], (loaded, *w1_free[s]))
                yield
        for k in range(0, IT, 2):
            a = n1 + k * D
            m2_ = split_weights(w2H[s][:, k:k + 2, :], w2L[s][:, k:k + 2, :], st[:, a:a + 2 * D].rearrange("p (k n) -> p k n", n=D), (loaded, *w2_free[s]))
            if k + 2 < IT:
                yield
        stage_free[s] = (m2_,)
        return m1_, m2_

    def gather(e):
        res = []
        for j in range(ST):
            gi, g = r_got.take(pool)
            n = e * ST + j
            res.append((gi, g, ld_got[gi].mark(pool.indirect_dma_start(g[:, :], None, rows_in, bass.IndirectOffsetOnAxis(ap=slot_token[:, n:n + 1], axis=0)))))
        return res

    def turn_in(e, tiles):
        xi, _ = r_xe.take(act)
        for j, (gi, g, m) in enumerate(tiles):
            wait(pe, m)
            ti, bank = b_turn.take(pe)
            for k in range(KD):
                last = pe.transpose(bank[:, k * P:(k + 1) * P], g[:, k * P:(k + 1) * P], ident[:, :])
            t = e_t.mark(last)
            r_got.release(gi, t)
            js = slice(j * P, (j + 1) * P)
            lo = evacuate(xeH[xi][:, :, js], xeL[xi][:, :, js], bank[:, 0:D].rearrange("p (k t) -> p k t", k=KD), None, t, ())
            b_turn.release(ti, lo)
            yield
        return xi, lo

    def coming_expert(e):
        weights = yield from split_expert(e, loaded[e])
        if e + 2 < G:
            loaded.append(fetch_weights(e + 2))
        elif e + 1 == G:
            loaded.append(fetch_mlp(0, 0, *stage_free[0], *stage_free[1]))
        yield
        rows_turned = yield from turn_in(e, tiles)
        coming[e] = (*rows_turned, weights)

    def up_expert(e, xi, ready, wm):
        s = e % 2
        hi_, _ = r_he.take(act)
        wait(pe, ready, wm[0])
        halves = []
        for h in range(2):
            hs = slice(h * HALF, (h + 1) * HALF)
            for i in range(IT):
                both = []
                for part in range(2):
                    ms = slice(part * I0 + i * P, part * I0 + (i + 1) * P)
                    both.append(work(HALF, [(w1H[s][:, k, ms], w1L[s][:, k, ms], xeH[xi][:, k, hs], xeL[xi][:, k, hs]) for k in range(KD)]))
                m = both[1][2]
                z = gated_unit(*both, ACT.Gelu, 0.0, None, None, HALF, heH[:, i, hs], heL[:, i, hs])
                yield
            halves.append(z)
        w1_free[s] = (m,)
        r_xe.release(xi, m)
        return hi_, halves

    def down_expert(e, hi_, ready, wm):
        s = e % 2
        wait(pe, wm[1])
        for j in range(ST):
            wait(pe, ready[0 if (j + 1) * P <= HALF else 1])
            js = slice(j * P, (j + 1) * P)
            bi, bank = b_down.take(pe)
            m = e_mm.mark(products(bank[:, 0:D], [(heH[:, k, js], heL[:, k, js], w2H[s][:, k, :], w2L[s][:, k, :]) for k in range(IT)]))
            yi, y = r_y.take(dve)
            wait(dve, m)
            c = e_y.mark(dve.tensor_copy(y[:, :], bank[:, 0:D]))
            b_down.release(bi, c)
            wait(sp, c)
            r0 = e * CAP + j * P
            r_y.release(yi, st_y[yi].mark(sp.dma_start(rows_out[r0:r0 + P, :], y[:, :])))
            yield
        w2_free[s] = (m,)
        r_he.release(hi_, m)

    ld_d, ld_dyn = dma_event("ld_mlp"), dma_event("ld_picked_mlp")
    stD_free = ()
    PIECES = 8
    PIECE = PK1 // PIECES

    def fetch_mlp(b, j, *free):
        if j < 2:
            n = 2 * b + j
            wait(pool, picked1, *free)
            return ld_dyn.mark(pool.indirect_dma_start(stage[:, 0:PK1], None, A["pack1"], bass.IndirectOffsetOnAxis(ap=dyn1[:, n:n + 1], axis=0)))
        wait(sp, *free)
        return ld_d.mark(sp.dma_start(stage[:, 0:PK1], A["shared"]))

    def split_mlp(n, ready, free):
        nonlocal stD_free, w_next
        s = n % 2
        wait(act, *free)
        for q in range(PIECES):
            qs = slice(q * PIECE, (q + 1) * PIECE)
            w_next = split_weights(wDh[s][:, qs], wDl[s][:, qs], stage[:, qs], (ready,), dve if n == 1 else pool)
            stD_free = (w_next,)
            yield

    w_next = None
    loaded = [fetch_weights(0), fetch_weights(1)]
    tiles = gather(0)
    coming = {}
    run_all(coming_expert(0))

    def expert(e):
        xi, ready, weights = coming[e]
        hid = yield from up_expert(e, xi, ready, weights)
        yield from down_expert(e, *hid, weights)

    for e in range(G):
        if e + 1 < G:
            tiles = gather(e + 1)
            interleave(expert(e), coming_expert(e + 1))
        else:
            interleave(expert(e), split_mlp(0, loaded[G], (*w1_free[0], *w2_free[0])))

    r_y12, r_h = Ring([0, 1, 2]), Ring([0, 1, 2, 3])
    ld_y1 = [dma_event(f"ld_y1_{i}") for i in range(3)]
    ld_y2 = [dma_event(f"ld_y2_{i}") for i in range(3)]
    e_comb = Event(nc, "rows_combined")
    for i in range(4):
        wait(pool, (st_y[i], st_y[i].count))

    middle_top = routed_top + 4 * PK1
    top[0] = routed_top
    t1w = sb("ternary_w1", [P, KD, FF], F32R)
    t2w = sb("ternary_w2", [P, FF // P, D], F32R)
    below = sb("below_minus_half", [P, KD * FF])
    assert top[0] <= middle_top
    top[0] = last_top
    gwH = sb("gru_weights_hi", [P, 2, KD, D], F32R)
    gwL = sb("gru_weights_lo", [P, 2, KD, D], F32R)
    lbw = [sb("lora_b_weighted", [P, D]) for _ in range(B)]
    bwF = [sb("adapted_weights", [P, KD, D]) for _ in range(B)]
    bwH = [sb("adapted_weights_hi", [P, KD, D], F32R) for _ in range(B)]
    bwL = [sb("adapted_weights_lo", [P, KD, D], F32R) for _ in range(B)]
    ld_tail = [dma_event(f"ld_{k}") for k in ("ffn_w1", "ffn_w2", "gru_w", "base_w", "lora_a", "lora_b", "cond_rep")]
    tern, base_w, gru_w = [], [], []

    def tail_weights(free, place_free):
        W = KD * FF
        views, at = [], 0
        for k in ("ffn_w1", "ffn_w2", "gru_w", "base_w", "lora_a", "lora_b", "cond_rep"):
            src = A[k]
            n = int(np.prod(src.shape[1:]))
            views.append((stage[:, at:at + n], src))
            at += n
        loads = []
        wait(sp, *free)
        for i in (4, 5, 6, 3, 2, 0, 1):
            dst, src = views[i]
            if len(src.shape) == 3:
                src = src.rearrange("p k n -> p (k n)")
            elif len(src.shape) == 4:
                src = src.rearrange("p w k n -> p (w k n)")
            loads.append(ld_tail[i].mark(sp.dma_start(dst, src)))
        w1_st, w2_st, gw_st, bw_st, la, lb, crep = (v[0] for v in views)
        for _ in range(3):
            yield
        wait(dve, *place_free, *loads)
        wait(act, *place_free, *loads)
        wait(pe, *loads)
        for b in range(B):
            m = e_vec.mark(dve.tensor_scalar(lbw[b][:, :], lb, crep[:, b:b + 1], 2.0, ALU.mult, ALU.mult))
            yield
            wait(pe, m)
            i, bank = b_work.take(pe)
            for k in range(KD):
                last = pe.matmul(bank[:, k * D:(k + 1) * D], la[:, k * P:(k + 1) * P], lbw[b][:, :], start=True, stop=True)
            t = e_mm.mark(last)
            wait(dve, t)
            t = e_vec.mark(dve.tensor_tensor(bwF[b][:, :, :].rearrange("p k n -> p (k n)"), bank, bw_st, ALU.add))
            b_work.release(i, t)
            base_w.append(split_rows(bwH[b][:, :, :], bwL[b][:, :, :], bwF[b][:, :, :], (t,)))
            yield
        gru_w.append(split_weights(gwH[:, :, :, :].rearrange("p w k n -> p (w k n)"), gwL[:, :, :, :].rearrange("p w k n -> p (w k n)"), gw_st, (loads[4],)))
        Q = W // 4
        stats = []
        for n, st in enumerate((w1_st, w2_st)):
            sums = tiny[:, 200 + 8 * n:204 + 8 * n]
            for q in range(4):
                qs = slice(q * Q, (q + 1) * Q)
                v_step(dve.scalar_tensor_tensor(below[:, qs], st[:, qs], -1.0, st[:, qs], ALU.mult, ALU.max))
                m = v_step(dve.tensor_reduce(sums[:, q:q + 1], below[:, qs], AX.X, ALU.add))
                if q % 2:
                    yield
            stats.append((sums, m))
        for n, (st, tw) in enumerate(((w1_st, t1w), (w2_st, t2w))):
            sums, m = stats[n]
            half_, neg = (tiny[:, 204 + 8 * n + a:205 + 8 * n + a] for a in range(2))
            wait(pe, m)
            i, bank = b_work.take(pe)
            for q in range(4):
                last = pe.matmul(bank[:, 0:1], ones32[:, :], sums[:, q:q + 1], start=(q == 0), stop=(q == 3))
            t = e_mm.mark(last)
            wait(dve, t)
            t = v_step(dve.tensor_scalar(half_, bank[:, 0:1], 1.0 / (FF * D), 1e-8, ALU.mult, ALU.max))
            b_work.release(i, t)
            v_step(dve.tensor_scalar(neg, half_, -0.5, None, ALU.mult))
            v_step(dve.tensor_scalar(half_, half_, 0.5, None, ALU.mult))
            flat = tw[:, :, :].rearrange("p k n -> p (k n)")
            for q in range(4):
                qs = slice(q * Q, (q + 1) * Q)
                v_step(dve.tensor_scalar(below[:, qs], st[:, qs], neg, None, ALU.is_lt))
                m = v_step(dve.scalar_tensor_tensor(flat[:, qs], st[:, qs], half_, below[:, qs], ALU.is_gt, ALU.subtract))
                if q % 2:
                    yield
            tern.append(m)

    def combine_tile(tt):
        i, _ = r_y12.take(pool)
        for k, (buf, ev) in enumerate(((y1, ld_y1), (y2, ld_y2))):
            fetched = ev[i].mark(pool.indirect_dma_start(buf[i][:, :], None, rows_out, bass.IndirectOffsetOnAxis(ap=rows[:, k, tt:tt + 1], axis=0)))
            wait(dve, fetched)
        yield
        g0 = v_step(dve.tensor_scalar(y1[i][:, :], y1[i][:, :], gates[:, 0, tt:tt + 1], None, ALU.mult))
        a = e_comb.mark(dve.scalar_tensor_tensor(y1[i][:, :], y2[i][:, :], gates[:, 1, tt:tt + 1], y1[i][:, :], ALU.mult, ALU.add))
        yield
        wait(pe, a)
        bi, bank = b_work.take(pe)
        for k in range(KD):
            last = pe.transpose(bank[:, k * P:(k + 1) * P], y1[i][:, k * P:(k + 1) * P], ident[:, :])
        m = e_t.mark(last)
        r_y12.release(i, m)
        wait(dve, m)
        s = slice(tt * P, (tt + 1) * P)
        x = e_x.mark(dve.tensor_tensor(xT[:, :, s], bank[:, 0:D].rearrange("p (k t) -> p k t", k=KD), xT[:, :, s], ALU.add))
        b_work.release(bi, x)
        in_x[tt // QT] = split_rows(inH[:, :, s], inL[:, :, s], xT[:, :, s], (x,))

    def combine_tiles(first, end):
        live = []
        for tt in range(first, end + 2):
            if tt < end:
                live.append(combine_tile(tt))
            live = [g for g in live if next(g, "ended") != "ended"]
            yield

    acc_free = [tuple(m for ring in (b_turn, b_down) for marks in ring.free for m in marks)] * CPB
    run_all(combine_tiles(0, QT))
    loaded = fetch_mlp(0, 1, *stD_free)
    combining = combine_tiles(QT, NT)
    w_m = w_next
    mlp_down = []

    def down_unit():
        b, j, c, i, hi_, z, s = mlp_down.pop(0)
        wait(pe, z)
        dh, dl = parts(wDh[s], I1)[2], parts(wDl[s], I1)[2]
        first, final = (j == 0 and i == 0), (j == 2 and i == IT1 - 1)
        if first:
            wait(pe, *acc_free[c])
        for m in range(KD):
            ms = slice(m * P, (m + 1) * P)
            o = banks[:, 4 + 2 * c + m, :]
            pe.matmul(o, dh[:, i, ms], hiD[hi_][:, :], start=first, stop=False)
            pe.matmul(o, dh[:, i, ms], loD[hi_][:, :], start=False, stop=False)
            last = pe.matmul(o, dl[:, i, ms], hiD[hi_][:, :], start=False, stop=final)
        m = e_mm.mark(last)
        r_h.release(hi_, m)
        if final:
            cc = b * CPB + c
            ts = slice(cc * CH, (cc + 1) * CH)
            for k in range(KD):
                in_x[cc] = evacuate(inH[:, k, ts], inL[:, k, ts], banks[:, 4 + 2 * c + k, :], None, m, ())
            acc_free[c] = (in_x[cc],)
        return m

    for n in range(3 * B):
        b, j = n // 3, n % 3
        s = n % 2
        gh, uh, _ = parts(wDh[s], I1)
        gl, ul, _ = parts(wDl[s], I1)
        wait(pe, w_m)
        for u in range(CPB * IT1):
            c, i = u // IT1, u % IT1
            cc = b * CPB + c
            ts = slice(cc * CH, (cc + 1) * CH)
            if i == 0:
                wait(pe, in_x[cc])
            ms = slice(i * P, (i + 1) * P)
            gate = work(CH, [(gh[:, k, ms], gl[:, k, ms], inH[:, k, ts], inL[:, k, ts]) for k in range(KD)])
            up = work(CH, [(uh[:, k, ms], ul[:, k, ms], inH[:, k, ts], inL[:, k, ts]) for k in range(KD)])
            hi_, _ = r_h.take(act)
            weight = wsel[:, b, j:j + 1] if j < 2 else None
            z = gated_unit(gate, up, ACT.Gelu_apprx_tanh, 0.0, weight, None, CH, hiD[hi_][:, :], loD[hi_][:, :])
            m = up[2]
            mlp_down.append((b, j, c, i, hi_, z, s))
            if len(mlp_down) > 2:
                m = down_unit()
            if u == 2:
                following = split_mlp(n + 1, loaded, (m,)) if n + 1 < 3 * B else tail_weights(stD_free, (m,))
            if u > (6 if n + 1 < 3 * B else 2):
                next(following, None)
            if u == CPB * IT1 - 1 and n + 2 < 3 * B:
                loaded = fetch_mlp((n + 2) // 3, (n + 2) % 3, *stD_free)
            next(combining, None)
        w_m = w_next
    run_all(following)

    top[0] = middle_top
    FT = FF // P
    gate_t = [sb("gates", [P, CH]) for _ in range(2)]
    cand_t = [sb("candidates", [P, CH]) for _ in range(2)]
    state = [sb("state", [P, CH]) for _ in range(4)]
    act_out = [sb("gelu", [P, CH]) for _ in range(3)]
    hiE = [sb("hidden_hi", [P, CH], F32R) for _ in range(4)]
    loE = [sb("hidden_lo", [P, CH], F32R) for _ in range(4)]
    outb = [sb("out", [P, CH]) for _ in range(4)]

    assert top[0] <= last_top
    b_any = b_work

    r_gate, r_state = Ring([0, 1]), Ring(state)
    e_gate = Event(nc, "gru_gates")
    e_scan = Event(nc, "gru_states")
    wait(pe, *gru_w)

    def gru_chunk(c, carry):
        s = slice(c * CH, (c + 1) * CH)
        wait(pe, in_x[c])
        new = []
        for m_ in range(KD):
            ms = slice(m_ * P, (m_ + 1) * P)
            gi, _ = r_gate.take(act)
            for w, (dst, func) in enumerate(((gate_t[gi], ACT.Sigmoid), (cand_t[gi], ACT.Tanh))):
                i, bank = b_any.take(pe)
                t = e_mm.mark(products(bank, [(gwH[:, w, k, ms], gwL[:, w, k, ms], inH[:, k, s], inL[:, k, s]) for k in range(KD)]))
                wait(act, t)
                a = e_gate.mark(act.activation(dst[:, :], bank, func, bias=bias_g[:, w, m_:m_ + 1]))
                b_any.release(i, a)
            si, st = r_state.take(dve)
            wait(dve, a)
            init = 0.0 if carry is None else carry[m_]
            h = e_scan.mark(dve.tensor_tensor_scan(st[:, :], gate_t[gi][:, :], cand_t[gi][:, :], init, ALU.mult, ALU.add))
            r_gate.release(gi, h)
            new.append(st[:, CH - 1:CH])
            wait(dve, h)
            x = e_x.mark(dve.tensor_tensor(xT[:, m_, s], st[:, :], xT[:, m_, s], ALU.add))
            r_state.release(si, x)
        wait(act, t)
        in_x[c] = split_input(c, x)
        return new

    b_out = b_any
    r_gelu, r_he2 = Ring(act_out), Ring([0, 1, 2, 3])
    r_outb = Ring(outb)
    st_out = [dma_event(f"st_out{i}") for i in range(4)]

    def ffn_down(c, i, hi_, z):
        acc = 4 + 2 * (c % 2)
        s = slice(c * CH, (c + 1) * CH)
        wait(pe, z)
        if i == 0:
            wait(pe, *acc_free[c % 2])
        for m in range(KD):
            ms = slice(m * P, (m + 1) * P)
            pe.matmul(banks[:, acc + m, :], t2w[:, i, ms], hiE[hi_][:, :], start=(i == 0), stop=False)
            last = pe.matmul(banks[:, acc + m, :], t2w[:, i, ms], loE[hi_][:, :], start=False, stop=(i == FT - 1))
        m = e_mm.mark(last)
        r_he2.release(hi_, m)
        if i == FT - 1:
            wait(dve, m)
            for k in range(KD):
                oi, o = r_outb.take(dve)
                y = e_x.mark(dve.scalar_tensor_tensor(o[:, :], banks[:, acc + k, :], bias_2[:, k:k + 1], xT[:, k, s], ALU.add, ALU.add))
                wait(sp, y)
                r_outb.release(oi, st_out[oi].mark(sp.dma_start(out[:, k, s], o[:, :])))
            acc_free[c % 2] = (y,)

    under_way = []

    def ffn_chunk(c):
        s = slice(c * CH, (c + 1) * CH)
        wait(pe, in_x[c], *tern)
        for i in range(FT):
            bi, bank = b_any.take(pe)
            ms = slice(i * P, (i + 1) * P)
            for k in range(KD):
                pe.matmul(bank, t1w[:, k, ms], inH[:, k, s], start=(k == 0), stop=False)
                last = pe.matmul(bank, t1w[:, k, ms], inL[:, k, s], start=False, stop=(k == KD - 1))
            m = e_mm.mark(last)
            ai, a = r_gelu.take(act)
            wait(act, m)
            x = e_act.mark(act.activation(a[:, :], bank, ACT.Gelu, bias=bias_1[:, i:i + 1]))
            b_any.release(bi, x)
            hi_, _ = r_he2.take(act)
            z = split_rows(hiE[hi_][:, :], loE[hi_][:, :], a[:, :], (x,))
            r_gelu.release(ai, z)
            under_way.append((c, i, hi_, z))
            if len(under_way) > 2:
                ffn_down(*under_way.pop(0))

    def adapted(c):
        in_x[c] = linear(c, bwH[c // CPB], bwL[c // CPB], bias_b, (base_w[c // CPB], in_x[c]))

    carry = gru_chunk(0, None)
    while mlp_down:
        down_unit()
    gru_chunk(1, carry)
    carry = gru_chunk(2, None)
    adapted(0)
    gru_chunk(3, carry)
    for c in range(1, NCH):
        adapted(c)
    for c in range(NCH):
        ffn_chunk(c)
    while under_way:
        ffn_down(*under_way.pop(0))
    for ev in st_out:
        wait(sp, (ev, ev.count))


def kernel(**inputs):
    import concourse.bacc as _bacc
    from concourse.bass_utils import run_bass_kernel_spmd as _run
    a = {k: np.asarray(v) for k, v in inputs.items()}

    def cols(w, k):
        return w.reshape(k, P, -1).transpose(1, 0, 2)

    def heads(w):
        return w.transpose(1, 0, 2).reshape(D, NH * DH)

    half = HR
    freq = np.power(np.float32(10000.0), (-np.arange(half).astype(np.float32) / np.float32(half)))
    rad = freq[:, None] * np.arange(T, dtype=np.float32)[None, :]
    cos, sin = np.cos(rad), np.sin(rad)
    arrays = {
        "xT": a["x"].reshape(N, D).T.reshape(KD, P, N).transpose(1, 0, 2),
        "cond_8": a["cond_8"],
        "cond_w": a["L0_cond_weight"].transpose(2, 0, 1).reshape(KD, P, G, D).transpose(1, 0, 2, 3),
        "cond_mask": cols(a["L0_cond_mask"].T, KD),
        "cond_bias": a["L0_cond_bias"].reshape(KD, P).T,
        "attn_w": np.stack([cols(heads(a["L0_attn_wq"]), KD), cols(heads(a["L0_attn_wk"]), KD),
                            cols(heads(a["L0_attn_wv"]), KD), cols(a["L0_attn_wo"], KD)], axis=1),
        "ropeC": np.concatenate([cos, cos, np.ones((P - 2 * HR, T), np.float32)]),
        "ropeS": np.concatenate([sin, -sin]),
        "cond_rep": np.repeat(a["cond_8"].T, R, axis=0),
        "pack0": np.concatenate([
            a["L0_cond2_W_up"].transpose(0, 2, 1).reshape(G, KD, P, H0).transpose(0, 2, 1, 3).reshape(G, P, -1),
            a["L0_cond2_W_gate"].transpose(0, 2, 1).reshape(G, KD, P, H0).transpose(0, 2, 1, 3).reshape(G, P, -1),
            a["L0_cond2_W_down"].transpose(0, 2, 1).reshape(G, H0 // P, P, D).transpose(0, 2, 1, 3).reshape(G, P, -1),
            a["L0_cond2_b_up"].reshape(G, H0 // P, P).transpose(0, 2, 1),
            a["L0_cond2_b_gate"].reshape(G, H0 // P, P).transpose(0, 2, 1)], axis=2).reshape(G * P, PK0),
        "b_down": a["L0_cond2_b_down"],
        "WgT": cols(a["L0_ffn_Wg"].T, KD),
        "packF": np.concatenate([
            a["L0_ffn_W1"].reshape(G, KD, P, 2 * I0).transpose(0, 2, 1, 3).reshape(G, P, -1),
            a["L0_ffn_W2"].reshape(G, I0 // P, P, D).transpose(0, 2, 1, 3).reshape(G, P, -1)], axis=2),
        "pack1": np.concatenate([
            a["L1_cond_skill_gate"].reshape(G, KD, P, I1).transpose(0, 2, 1, 3).reshape(G, P, -1),
            a["L1_cond_skill_up"].reshape(G, KD, P, I1).transpose(0, 2, 1, 3).reshape(G, P, -1),
            a["L1_cond_skill_down"].reshape(G, I1 // P, P, D).transpose(0, 2, 1, 3).reshape(G, P, -1)], axis=2).reshape(G * P, PK1),
        "shared": np.concatenate([cols(a["L1_cond_shared_gate"], KD).reshape(P, -1), cols(a["L1_cond_shared_up"], KD).reshape(P, -1),
                                  cols(a["L1_cond_shared_down"], I1 // P).reshape(P, -1)], axis=1),
        "gru_w": np.stack([cols(a["L1_attn_Wg"].T, KD), cols(a["L1_attn_Wc"].T, KD)], axis=1),
        "gru_b": np.stack([a["L1_attn_bg"].reshape(KD, P).T, a["L1_attn_bc"].reshape(KD, P).T], axis=1),
        "base_w": cols(a["L1_cond2_W_base"].T, KD),
        "base_bias": a["L1_cond2_b_base"].reshape(KD, P).T,
        "lora_a": a["L1_cond2_As"].reshape(G * R, D),
        "lora_b": a["L1_cond2_Bs"].transpose(0, 2, 1).reshape(G * R, D),
        "ffn_w1": cols(a["L1_ffn_W1"].T, KD),
        "ffn_b1": a["L1_ffn_b1"].reshape(FF // P, P).T,
        "ffn_w2": cols(a["L1_ffn_W2"].T, FF // P),
        "ffn_b2": a["L1_ffn_b2"].reshape(KD, P).T,
    }
    arrays = {k: np.ascontiguousarray(v) for k, v in arrays.items()}
    nc = _bacc.Bacc("TRN2", target_bir_lowering=False, num_devices=1)
    A = {k: nc.dram_tensor(f"in_{k}", v.shape, mybir.dt.from_np(v.dtype), kind="ExternalInput").ap() for k, v in arrays.items()}
    out = nc.dram_tensor("out_xT", (P, KD, N), F32, kind="ExternalOutput").ap()
    program(nc, A, out)
    r = _run(nc, [{f"in_{k}": v for k, v in arrays.items()}], core_ids=[0])
    got = r.results[0]["out_xT"]
    return np.ascontiguousarray(got.transpose(1, 0, 2).reshape(D, N).T.reshape(B, T, D))
```

```python
import numpy as np
import concourse.bass as bass
from concourse import mybir
from concourse.alu_op_type import AluOpType as ALU

F32 = mybir.dt.float32
F32R = mybir.dt.float32r
BF16 = mybir.dt.bfloat16
I32 = mybir.dt.int32
ACT = mybir.ActivationFunctionType
AX = mybir.AxisListType

P = 128
B, T, D = 2, 1024, 256
N = B * T
KD = D // P
CH = 512
NCH = N // CH
CPB = T // CH
G = 8
NH, DH = 2, 128
HR = 32
H0 = 512
I0 = 512
CAP = int(N * 2 * 1.25 / 8)
ST = CAP // P
HALF = CAP // 2
NT = N // P
TPB = T // P
I1 = 1024
R = 16
FF = 4 * D
LOW = 32
HIGH = CAP // LOW
MASK = -1.0e30
PK0 = 2 * KD * H0 + (H0 // P) * D + 2 * (H0 // P)
PKF = KD * 2 * I0 + (I0 // P) * D
PK1 = 2 * KD * I1 + (I1 // P) * D


class Event:

    def __init__(self, nc, name, by=1):
        self.sem, self.count, self.by = nc.alloc_semaphore(name), 0, by

    def mark(self, ins):
        ins.then_inc(self.sem, self.by)
        self.count += self.by
        return (self, self.count)


def wait(eng, *marks):
    for m in marks:
        if m is not None:
            eng.wait_ge(m[0].sem, m[1])


class Ring:

    def __init__(self, slots):
        self.slots, self.free, self.at = slots, [() for _ in slots], -1

    def take(self, eng):
        self.at = (self.at + 1) % len(self.slots)
        assert self.free[self.at] is not None, "its last users are not known yet"
        wait(eng, *self.free[self.at])
        self.free[self.at] = None
        return self.at, self.slots[self.at]

    def release(self, i, *marks):
        self.free[i] = marks

    def idle(self):
        return self.free[(self.at + 1) % len(self.slots)] is not None


def run_all(steps):
    while True:
        try:
            next(steps)
        except StopIteration as end:
            return end.value


def one_behind_another(tasks):
    live, tasks = [], list(tasks)
    while live or tasks:
        if tasks:
            live.append(tasks.pop(0))
        live = [g for g in live if next(g, "ended") != "ended"]
        yield


def interleave_steps(main, side, every=1):
    for n, _ in enumerate(main, 1):
        if n % every == 0:
            next(side, None)
        yield
    for _ in side:
        yield


def interleave(main, side, every=1):
    for _ in interleave_steps(main, side, every):
        pass


def program(nc, A, out):
    pe, act, dve, pool, sp = nc.tensor, nc.scalar, nc.vector, nc.gpsimd, nc.sync

    def f(ap):
        return ap.bitcast(F32)

    base0 = (nc.sbuf_base + 63) // 64 * 64
    top = [base0]
    serial = [0]

    def sb(name, shape, dt=F32):
        size = int(np.prod(shape[1:])) * (2 if dt == BF16 else 4)
        serial[0] += 1
        t = nc.alloc_sbuf_tensor_at(f"{name}_{serial[0]}", shape, dt, offset=top[0])
        top[0] += (size + 31) // 32 * 32
        assert top[0] <= nc.sbuf_usable_end, (name, top[0])
        return t

    banks = nc.alloc_psum_tensor("banks", [P, 8, CH], F32)

    def dma_event(name):
        return Event(nc, name, 16)

    xT = sb("residual", [P, KD, N])
    inH = sb("input_hi", [P, KD, N], F32R)
    inL = sb("input_lo", [P, KD, N], F32R)
    stage = sb("weight_stage", [P, 6160])
    ident = sb("identity", [P, P])
    ident16 = sb("identity_bf16", [P, P], BF16)
    causal = sb("causal_mask", [P, P], BF16)
    before = sb("earlier_token", [P, P], BF16)
    ones16 = sb("ones_bf16", [P, P], BF16)
    ones32 = sb("ones", [P, P])
    rev = sb("eight_minus_expert", [P, G])
    cond = sb("conditioning", [P, B, G])
    dyn0 = sb("rows_of_L0_cond2", [P, B], I32)
    dynb = sb("expert_of_L0_cond2", [P, B], I32)
    dyn1 = sb("rows_of_L1_cond", [P, B * 2], I32)
    wsel = sb("L1_expert_weight", [P, B, 2])
    lane = sb("partition_number", [P, 1])
    bias_c = sb("cond_bias", [P, KD])
    bias_g = sb("gru_biases", [P, 2, KD])
    bias_b = sb("base_bias", [P, KD])
    bias_1 = sb("ffn_bias_1", [P, FF // P])
    bias_2 = sb("ffn_bias_2", [P, KD])
    tiny = sb("tiny", [P, 224])
    QT = CH // P
    K = 2
    gates = sb("route_gates", [P, NCH, K, QT])
    rows = sb("route_rows", [P, NCH, K, QT], I32)
    slot_token = sb("token_of_slot", [P, G * ST], I32)
    all_top2, all_places, all_first_rows, raw_gates, kept = (sb(n, [P, NCH, K, QT]) for n in
        ("two_largest", "place", "first_row", "raw_gates", "kept"))
    diff = sb("largest_difference", [P, NCH, QT])
    phase_top = top[0]

    rows_in = nc.dram_tensor("routed_input", [N, D], F32, kind="Internal").ap()
    rows_out = nc.dram_tensor("expert_output", [G * CAP, D], F32, kind="Internal").ap()

    e_const = Event(nc, "constants")
    e_vec = Event(nc, "dve_small_step")
    e_acs = Event(nc, "act_small_step")
    e_hi = Event(nc, "hi_written")
    e_lo = Event(nc, "lo_written")
    e_wlo = Event(nc, "weight_lo_by_pool")
    e_mm = Event(nc, "product_in_psum")

    def v_step(ins):
        m = e_vec.mark(ins)
        wait(dve, m)
        return m

    def products(bank, terms):
        n = len(terms)
        for i, (wh, wl, dh, dl) in enumerate(terms):
            pe.matmul(bank, wh, dh, start=(i == 0), stop=False)
            pe.matmul(bank, wh, dl, start=False, stop=False)
            last = pe.matmul(bank, wl, dh, start=False, stop=(i == n - 1))
        return last

    def split_weights(hi, lo, src, ready, lo_eng=None, lo_event=None):
        lo_eng = lo_eng or pool
        lo_event = lo_event or (e_wlo if lo_eng is pool else e_lo)
        wait(act, *ready)
        h = e_hi.mark(act.copy(hi, src))
        wait(lo_eng, h)
        return lo_event.mark(lo_eng.tensor_tensor(lo, src, f(hi), ALU.subtract))

    def evacuate(hi, lo, bank, bias, ready, free):
        wait(act, ready, *free)
        if bias is None:
            h = e_hi.mark(act.copy(hi, bank))
        else:
            h = e_hi.mark(act.activation(hi, bank, ACT.Identity, bias=bias))
        wait(dve, h)
        if bias is None:
            return e_lo.mark(dve.tensor_tensor(lo, bank, f(hi), ALU.subtract))
        return e_lo.mark(dve.scalar_tensor_tensor(lo, bank, bias, f(hi), ALU.add, ALU.subtract))

    def split_rows(hi, lo, src, ready):
        wait(act, *ready)
        h = e_hi.mark(act.copy(hi, src))
        wait(dve, h)
        return e_lo.mark(dve.tensor_tensor(lo, src, f(hi), ALU.subtract))

    def load(eng, dst, src, name, *after):
        wait(eng, *after)
        ev = dma_event(name)
        return ev.mark(eng.dma_start(dst, src))

    ld_cond = load(act, cond[:, :, :], A["cond_8"].rearrange("b g -> (b g)").rearrange("(a n) -> a n", a=1).broadcast_to((P, B * G)).rearrange("p (b g) -> p b g", b=B), "ld_cond")

    for t, v in ((ident, 0.0), (ident16, 0.0), (causal, 0.0), (before, 1.0), (ones16, 1.0), (ones32, 1.0)):
        c0 = e_const.mark(pool.memset(t[:, :], v))
    wait(pool, c0)
    pool.affine_select(out=ident[:, :], in_=ident[:, :], compare_op=ALU.not_equal, fill=1.0, base=0, pattern=[[-1, P]], channel_multiplier=1)
    pool.affine_select(out=ident16[:, :], in_=ident16[:, :], compare_op=ALU.not_equal, fill=1.0, base=0, pattern=[[-1, P]], channel_multiplier=1)
    pool.affine_select(out=causal[:, :], in_=causal[:, :], compare_op=ALU.is_ge, fill=MASK, base=0, pattern=[[-1, P]], channel_multiplier=1)
    pool.affine_select(out=before[:, :], in_=before[:, :], compare_op=ALU.is_gt, fill=0.0, base=0, pattern=[[1, P]], channel_multiplier=-1)
    pool.iota(rev[:, :], [[-1, G]], base=G, channel_multiplier=0, allow_small_or_imprecise_dtypes=True)
    consts = e_const.mark(pool.iota(lane[:, :], [[0, 1]], base=0, channel_multiplier=1, allow_small_or_imprecise_dtypes=True))
    wait(dve, consts)
    wait(pe, consts)

    def first_max(vals, groups, m, onehot, tmp, tmp1):
        def wide(ap):
            return ap.rearrange("p (g a) -> p g a", a=1).broadcast_to((P, groups, G))
        revb = rev[:, :].rearrange("p (a g) -> p a g", a=1).broadcast_to((P, groups, G))
        v_step(dve.tensor_reduce(m, vals, AX.X, ALU.max))
        v_step(dve.tensor_tensor(tmp, vals, wide(m), ALU.is_equal))
        v_step(dve.tensor_tensor(tmp, tmp, revb, ALU.mult))
        v_step(dve.tensor_reduce(tmp1, tmp, AX.X, ALU.max))
        v_step(dve.tensor_tensor(onehot, revb, wide(tmp1), ALU.is_equal))

    def second_input(dst, vals, onehot):
        v_step(dve.scalar_tensor_tensor(dst, onehot, -3.0e38, vals, ALU.mult, ALU.add))

    def expert_number(dst, onehot, groups, tmp):
        revb = rev[:, :].rearrange("p (a g) -> p a g", a=1).broadcast_to((P, groups, G))
        v_step(dve.tensor_tensor(tmp, onehot, revb, ALU.mult))
        v_step(dve.tensor_reduce(dst, tmp, AX.X, ALU.add))
        v_step(dve.tensor_scalar(dst, dst, -1.0, float(G), ALU.mult, ALU.add))

    def t3(at, g):
        return tiny[:, at:at + g * G].rearrange("p (g e) -> p g e", e=G)
    pick_wide = [t3(16 * i, B) for i in range(5)]
    pick_thin = [tiny[:, 80 + 2 * i:82 + 2 * i] for i in range(4)]

    def pick_L0_cond2():
        _, oh, tm, _, _ = pick_wide
        m1, _, s1, ex = pick_thin
        wait(dve, ld_cond)
        first_max(cond[:, :, :], B, m1, oh, tm, s1)
        expert_number(ex, oh, B, tm)
        v_step(dve.tensor_copy(dynb[:, :], ex))
        return v_step(dve.tensor_scalar(dyn0[:, :], ex, float(P), lane[:, 0:1], ALU.mult, ALU.add))

    def pick_L1_cond():
        nonlocal picked1
        v0, oh, tm, rw, v2 = pick_wide
        m1, m2, s1, ex = pick_thin
        m1w = m1.rearrange("p (g a) -> p g a", a=1).broadcast_to((P, B, G))
        d0 = v_step(dve.tensor_tensor(v0, cond[:, :, :], m1w, ALU.subtract))
        wait(act, d0)
        x0 = e_acs.mark(act.activation(rw, v0, ACT.Exp))
        wait(dve, x0)
        v_step(dve.tensor_reduce(s1, rw, AX.X, ALU.add))
        v_step(dve.reciprocal(s1, s1))
        v_step(dve.tensor_tensor(rw, rw, s1.rearrange("p (g a) -> p g a", a=1).broadcast_to((P, B, G)), ALU.mult))
        yield
        first_max(rw, B, m1, oh, tm, s1)
        yield
        expert_number(ex, oh, B, tm)
        d1 = dyn1[:, :].rearrange("p (b k) -> p b k", k=2)
        v_step(dve.tensor_scalar(d1[:, :, 0], ex, float(P), lane[:, 0:1], ALU.mult, ALU.add))
        yield
        second_input(v2, rw, oh)
        first_max(v2, B, m2, oh, tm, s1)
        yield
        expert_number(ex, oh, B, tm)
        v_step(dve.tensor_scalar(d1[:, :, 1], ex, float(P), lane[:, 0:1], ALU.mult, ALU.add))
        yield
        v_step(dve.tensor_tensor(s1, m1, m2, ALU.add))
        v_step(dve.reciprocal(s1, s1))
        a0, a1 = tiny[:, 104:106], tiny[:, 106:108]
        for k, m in enumerate((m1, m2)):
            v_step(dve.tensor_tensor(a0, m, s1, ALU.mult))
            v_step(dve.tensor_scalar(a1, a0, 1.0 - 1.0 / 12, None, ALU.mult))
            picked1 = v_step(dve.scalar_tensor_tensor(wsel[:, :, k], a0, 1.0 / 12, a1, ALU.mult, ALU.add))

    picked1 = None

    cwH = [sb("cond_weight_hi", [P, KD, D], F32R) for _ in range(B)]
    cwL = [sb("cond_weight_lo", [P, KD, D], F32R) for _ in range(B)]
    cwF = [sb("cond_weight", [P, KD, D]) for _ in range(B)]
    term = sb("cond_term", [P, D])
    cmask = sb("cond_mask", [P, KD, D])
    ropeC = sb("rope_cos", [P, T])
    ropeS = sb("rope_sin", [2 * HR, T])
    cross = [sb("rope_cross", [2 * HR, CH]) for _ in range(2)]
    rot = [sb("rotated", [P, CH]) for _ in range(2)]
    projected_top = top[0]
    aW = sb("attention_weights_hi", [P, 4, KD, D], F32R)
    aWl = sb("attention_weights_lo", [P, 4, KD, D], F32R)
    kH = sb("key_hi", [P, NH, T], F32R)
    kL = sb("key_lo", [P, NH, T], F32R)
    qH = [sb("query_hi", [P, NH, CH], F32R) for _ in range(2)]
    qL = [sb("query_lo", [P, NH, CH], F32R) for _ in range(2)]
    scored_top = top[0]
    vH = sb("value_hi", [P, TPB, D], F32R)
    vL = sb("value_lo", [P, TPB, D], F32R)
    PAIR = 2 * P
    ptH = [sb("probT_hi", [P, TPB, PAIR], F32R) for _ in range(2)]
    ptL = [sb("probT_lo", [P, TPB, PAIR], F32R) for _ in range(2)]
    prob = [sb("probabilities", [P, T])] + [stage[:, PK0 + T * i:PK0 + T * (i + 1)] for i in (1, 2, 0)]
    stat = sb("softmax_stats", [P, 4 * 16])

    cond_stage = stage[:, 0:2048 * KD].rearrange("p (k g o) -> p k g o", k=KD, g=G)
    aw_st = stage[:, 4096:6144].rearrange("p (w k o) -> p w k o", w=4, k=KD)

    def load_x(c, eng=sp):
        return load(eng, xT[:, :, c * CH:(c + 1) * CH], A["xT"][:, :, c * CH:(c + 1) * CH], f"ld_x{c}")
    ld_cw = [load(sp, cond_stage[:, k, :, :], A["cond_w"][:, k, :, :], f"ld_cond_w{k}") for k in range(KD)]
    ld_x = [load_x(0)]
    ld_mask = load(act, cmask[:, :, :], A["cond_mask"], "ld_cond_mask")
    ld_small = Event(nc, "ld_small", 16)
    small = ld_small.mark(act.dma_start(bias_c[:, :], A["cond_bias"]))
    ld_aw = load(act, aw_st, A["attn_w"], "ld_attn_w")
    small = ld_small.mark(sp.dma_start(ropeC[:, :], A["ropeC"]))
    small = ld_small.mark(sp.dma_start(ropeS[:, :], A["ropeS"]))
    for dst, src in ((bias_b, "base_bias"), (bias_1, "ffn_b1"), (bias_2, "ffn_b2")):
        small = ld_small.mark(sp.dma_start(dst[:, :], A[src]))
    small = ld_small.mark(sp.dma_start(bias_g[:, :, :], A["gru_b"]))
    ld_x += [load_x(c) for c in range(1, NCH)]

    def split_input(c, ready):
        s = slice(c * CH, (c + 1) * CH)
        return split_rows(inH[:, :, s], inL[:, :, s], xT[:, :, s], (ready,))

    e_cwp = Event(nc, "cond_weight_by_pool")

    def conditioned_weights():
        w, at = cwF[0], [None] * KD
        lead = 3
        for step in range(G + lead):
            for k, g in ((0, step), (1, step - lead)):
                if g == 0:
                    wait(dve, ld_cw[k])
                    at[k] = e_vec.mark(dve.tensor_scalar(w[:, k, :], cond_stage[:, k, 0, :], cond[:, 0, 0:1], None, ALU.mult))
                elif 0 < g < G:
                    wait(dve, at[k])
                    at[k] = e_vec.mark(dve.scalar_tensor_tensor(w[:, k, :], cond_stage[:, k, g, :], cond[:, 0, g:g + 1], w[:, k, :], ALU.mult, ALU.add))
        wait(dve, *at, ld_mask)
        return v_step(dve.tensor_tensor(w[:, :, :], w[:, :, :], cmask[:, :, :], ALU.mult))

    def conditioned_half(k):
        w = cwF[1][:, k, :]
        wait(pool, ld_cond, ld_cw[k], ld_mask)
        m = e_cwp.mark(pool.tensor_scalar(w, cond_stage[:, k, 0, :], cond[:, 1, 0:1], 1.0, ALU.mult, ALU.mult))
        for g in range(1, G):
            t = e_cwp.mark(pool.tensor_scalar(term[:, :], cond_stage[:, k, g, :], cond[:, 1, g:g + 1], 1.0, ALU.mult, ALU.mult))
            wait(pool, t)
            m = e_cwp.mark(pool.tensor_tensor(w, w, term[:, :], ALU.add))
            wait(pool, m)
            yield
        cw_half[k] = e_cwp.mark(pool.tensor_tensor(w, w, cmask[:, k, :], ALU.mult))

    cw_half = [None] * KD
    run_all(conditioned_half(1))
    picked = pick_L0_cond2()
    in_x = [None] * NCH
    weights_0 = conditioned_weights()
    in_x[0] = split_input(0, ld_x[0])
    cw = [split_rows(cwH[0][:, :, :], cwL[0][:, :, :], cwF[0][:, :, :], (weights_0,)), None]
    attn_w = {w: split_weights(aW[:, w, :, :], aWl[:, w, :, :], aw_st[:, w, :, :], (ld_aw,), eng) for w, eng in ((1, dve), (0, dve), (2, pool), (3, pool))}
    wait(act, small)
    wait(dve, small)

    b_turn, b_out = Ring([banks[:, 4, :], banks[:, 5, :]]), Ring([banks[:, 6, :]])
    b_score, b_fill = Ring([banks[:, i:i + 1, :] for i in range(3)]), Ring([banks[:, 7, :], banks[:, 3, :]])
    r_prob = Ring(prob)
    r_prob.release(3, cw_half[1])
    r_prob.release(1, attn_w[3])
    r_prob.release(2, attn_w[3])
    r_rot = Ring(list(zip(rot, cross)))
    r_pt = Ring([0, 1])
    e_s = Event(nc, "scores")
    e_t = Event(nc, "probs_turned")
    e_exp = Event(nc, "exponentials")
    e_norm = Event(nc, "probs_normed")
    e_rope = Event(nc, "rope_by_pool")
    e_x = Event(nc, "residual_updated")
    q_free, k_free, v_free = [(), ()], (), ()
    k_ready, v_ready, q_ready = {}, [None] * NCH, {}
    tile = 0

    def linear(c, wh, wl, bias, ready, rings):
        s = slice(c * CH, (c + 1) * CH)
        got = []
        wait(pe, *ready)
        for m, ring in enumerate(rings):
            i, bank = ring.take(pe)
            t = e_mm.mark(products(bank, [(wh[:, k, m * P:(m + 1) * P], wl[:, k, m * P:(m + 1) * P], inH[:, k, s], inL[:, k, s]) for k in range(KD)]))
            got.append((i, bank, t))
        for m, (i, bank, t) in enumerate(got):
            lo = evacuate(inH[:, m, s], inL[:, m, s], bank, bias[:, m:m + 1], t, (got[-1][2],))
            rings[m].release(i, lo)
        return lo

    def conditioned(c):
        b = c // CPB
        if c == CPB:
            cw[1] = split_rows(cwH[1][:, :, :], cwL[1][:, :, :], cwF[1][:, :, :], cw_half)
        if c:
            in_x[c] = split_input(c, ld_x[c])
            yield
        in_x[c] = linear(c, cwH[b], cwL[b], bias_c, (cw[b], in_x[c]), (b_fill, b_out))

    def rotated(w, h, c, hi, lo, free, scale=None):
        s = slice(c * CH, (c + 1) * CH)
        pos = slice((c % CPB) * CH, (c % CPB + 1) * CH)
        wait(pe, in_x[c], attn_w[w])
        i, bank = b_fill.take(pe)
        hs = slice(h * DH, (h + 1) * DH)
        t = e_mm.mark(products(bank, [(aW[:, w, k, hs], aWl[:, w, k, hs], inH[:, k, s], inL[:, k, s]) for k in range(KD)]))
        yield
        wait(dve, t)
        j, (r, x) = r_rot.take(dve)
        dve.tensor_tensor(r[:, :], bank, ropeC[:, pos], ALU.mult)
        dve.tensor_tensor(x[0:HR, :], bank[HR:2 * HR, :], ropeS[HR:2 * HR, pos], ALU.mult)
        u = e_vec.mark(dve.tensor_tensor(x[HR:2 * HR, :], bank[0:HR, :], ropeS[0:HR, pos], ALU.mult))
        b_fill.release(i, u)
        wait(pool, u)
        v = e_rope.mark(pool.tensor_tensor(r[0:2 * HR, :], r[0:2 * HR, :], x[:, :], ALU.add))
        yield
        yield
        wait(act, *free)
        if scale is None:
            m = split_rows(hi, lo, r[:, :], (v,))
        else:
            wait(act, v)
            y = e_hi.mark(act.activation(hi, r[:, :], ACT.Identity, scale=scale))
            wait(dve, y)
            m = e_lo.mark(dve.scalar_tensor_tensor(lo, r[:, :], scale, f(hi), ALU.mult, ALU.subtract))
        r_rot.release(j, m)
        return m

    def key_head(c, h):
        s = slice((c % CPB) * CH, (c % CPB + 1) * CH)
        k_ready[c, h] = yield from rotated(1, h, c, kH[:, h, s], kL[:, h, s], k_free)

    def query_head(c, h):
        q_ready[c, h] = yield from rotated(0, h, c, qH[c % 2][:, h, :], qL[c % 2][:, h, :], q_free[c % 2], 1.0 / DH)

    def value_tiles(c, t):
        tt = (c % CPB) * QT + t
        wait(pe, in_x[c], attn_w[2])
        i, bank = b_fill.take(pe)
        for u in range(2):
            ts = slice(c * CH + (t + u) * P, c * CH + (t + u + 1) * P)
            last = products(bank[:, u * D:(u + 1) * D], [(inH[:, k, ts], inL[:, k, ts], aW[:, 2, k, :], aWl[:, 2, k, :]) for k in range(KD)])
        m = e_mm.mark(last)
        yield
        v_ready[c] = evacuate(vH[:, tt:tt + 2, :], vL[:, tt:tt + 2, :], bank.rearrange("p (t d) -> p t d", d=D), None, m, v_free)
        b_fill.release(i, v_ready[c])

    def keys(c):
        return [key_head(c, h) for h in range(NH)]

    def queries(c):
        return [query_head(c, h) for h in range(NH)]

    def values(c):
        return [value_tiles(c, t) for t in range(0, QT, 2)]

    def scores(c, h, i):
        nonlocal tile
        qt = (c % CPB) * QT + i
        width = (qt + 1) * P
        qs = slice(i * P, (i + 1) * P)
        q_h, q_l = qH[c % 2][:, h, qs], qL[c % 2][:, h, qs]
        wait(pe, q_ready[c, h], k_ready[c, h])
        si, sc = b_score.take(pe)
        flat = sc.rearrange("p a n -> p (a n)")
        for n0 in range(0, width, CH):
            n1 = min(n0 + CH, width)
            o = flat[:, n0:n1]
            pe.matmul(o, q_h, kH[:, h, n0:n1], start=True, stop=False)
            pe.matmul(o, q_h, kL[:, h, n0:n1], start=False, stop=False)
            pe.matmul(o, q_l, kH[:, h, n0:n1], start=False, stop=(n1 < width))
        m = e_s.mark(pe.matmul(flat[:, width - P:width], ident16[:, :], causal[:, :], start=False, stop=True))
        so = 4 * (tile % 16)
        tile += 1
        nb, l, r = (stat[:, so + a:so + a + 1] for a in range(3))
        wait(dve, m)
        u = e_vec.mark(dve.tensor_reduce(nb, flat[:, 0:width], AX.X, ALU.max, negate=True))
        return c, h, i, qt, si, flat, u, nb, l, r

    def exponentials(c, h, i, qt, si, flat, u, nb, l, r):
        width = (qt + 1) * P
        pi, pr = r_prob.take(act)
        wait(act, u)
        x = e_exp.mark(act.activation(pr[:, 0:width], flat[:, 0:width], ACT.Exp, bias=nb, scale=1.0, accum_out=l))
        b_score.release(si, x)
        return (c, h, i, qt, pi, pr, x, l, r)

    def norm(c, h, i, qt, pi, pr, x, l, r):
        width = (qt + 1) * P
        wait(dve, x)
        u = e_vec.mark(dve.reciprocal(r, l))
        wait(pool, u)
        n = e_norm.mark(pool.tensor_scalar(pr[:, 0:width], pr[:, 0:width], r, 1.0, ALU.mult, ALU.mult))
        return (c, h, i, qt, pi, pr, n)

    pair_at = None

    def turn(c, h, i, qt, pi, pr, n):
        nonlocal pair_at
        if i % 2 == 0:
            pair_at, _ = r_pt.take(act)
        half = slice((i % 2) * P, (i % 2 + 1) * P)
        parts_ = []
        wait(pe, n)
        for k0 in range(0, qt + 1, 4):
            k1 = min(k0 + 4, qt + 1)
            ti, bank = b_turn.take(pe)
            for k in range(k0, k1):
                last = pe.transpose(bank[:, (k - k0) * P:(k - k0 + 1) * P], pr[:, k * P:(k + 1) * P], ident[:, :])
            m = e_t.mark(last)
            src = bank[:, 0:(k1 - k0) * P].rearrange("p (k q) -> p k q", q=P)
            hi, lo = ptH[pair_at][:, k0:k1, half], ptL[pair_at][:, k0:k1, half]
            wait(act, m)
            parts_.append((ti, hi, lo, src, e_hi.mark(act.copy(hi, src))))
        r_prob.release(pi, m)
        return c, h, i, parts_

    def turned_lo(c, h, i, parts_):
        for ti, hi, lo, src, m in parts_:
            wait(dve, m)
            m = e_lo.mark(dve.tensor_tensor(lo, src, f(hi), ALU.subtract))
            b_turn.release(ti, m)
        if i % 2:
            turned.append((c, h, i, pair_at, m))

    def weighted(c, h, i, at, ready):
        qt = (c % CPB) * QT + i
        assert v_ready[c]
        wait(pe, ready, v_ready[c])
        oi, bank = b_out.take(pe)
        hs = slice(h * DH, (h + 1) * DH)
        for k in range(qt + 1):
            q0 = P if k == qt else 0
            a, p_h, p_l = bank[:, q0:PAIR], ptH[at][:, k, q0:PAIR], ptL[at][:, k, q0:PAIR]
            pe.matmul(a, vH[:, k, hs], p_h, start=(k == 0), stop=False)
            pe.matmul(a, vH[:, k, hs], p_l, start=False, stop=False)
            last = pe.matmul(a, vL[:, k, hs], p_h, start=False, stop=(k == qt))
        m = e_mm.mark(last)
        r_pt.release(at, m)
        s = slice(c * CH + (i - 1) * P, c * CH + (i + 1) * P)
        lo = evacuate(inH[:, h, s], inL[:, h, s], bank[:, 0:PAIR], None, m, ())
        b_out.release(oi, lo)
        return lo

    def project_out(c, ready):
        s = slice(c * CH, (c + 1) * CH)
        wait(pe, ready, attn_w[3])
        for m_ in range(KD):
            ring = b_fill if m_ and b_fill.idle() else b_out
            oi, bank = ring.take(pe)
            ms = slice(m_ * P, (m_ + 1) * P)
            m = e_mm.mark(products(bank, [(aW[:, 3, k, ms], aWl[:, 3, k, ms], inH[:, k, s], inL[:, k, s]) for k in range(KD)]))
            wait(dve, m)
            x = e_x.mark(dve.tensor_tensor(xT[:, m_, s], bank, xT[:, m_, s], ALU.add))
            ring.release(oi, x)
        wait(act, m)
        in_x[c] = split_input(c, x)

    def share_banks(long):
        nonlocal b_score, b_fill
        before_ = tuple(m for ring in (b_score, b_fill) for marks in ring.free for m in marks)
        if long:
            b_score, b_fill = Ring([banks[:, 0:2, :], banks[:, 2:4, :]]), Ring([banks[:, 7, :]])
        else:
            b_score, b_fill = Ring([banks[:, i:i + 1, :] for i in range(3)]), Ring([banks[:, 7, :], banks[:, 3, :]])
        for ring in (b_score, b_fill):
            for i in range(len(ring.slots)):
                ring.release(i, *before_)

    scored, normed, turned, project = [], [], [], []

    def attention(c):
        for h in range(NH):
            for i in range(QT):
                yield from advance((c, h, i))
        q_free[c % 2] = ((e_s, e_s.count),)

    def advance(new=None):
        nonlocal v_free
        ready_pairs, ready_chunks = turned[:], project[:]
        old = turn(*normed.pop(0)) if len(normed) > (1 if new else 0) else None
        if new:
            new = scores(*new)
        if old:
            turned_lo(*old)
        if new:
            new = exponentials(*new)
        if scored:
            normed.append(norm(*scored.pop(0)))
        if new:
            scored.append(new)
        yield
        for c, h, i, at, lo in ready_pairs:
            turned.pop(0)
            ready = weighted(c, h, i, at, lo)
            v_free = ((e_mm, e_mm.count),)
            if h == NH - 1 and i == QT - 1:
                project.append((c, ready))
            yield
        for c, ready in ready_chunks:
            project.pop(0)
            project_out(c, ready)
            yield

    def flush():
        while scored or normed or turned or project:
            yield from advance()

    def some(steps, n):
        for _ in range(n):
            next(steps)
            yield

    def chain(*steps):
        for s in steps:
            yield from s

    run_all(one_behind_another([conditioned(0), key_head(0, 0), query_head(0, 0)]))
    chunk_0 = interleave_steps(attention(0), conditioned_half(0))
    interleave(some(chunk_0, 2), one_behind_another([key_head(0, 1), query_head(0, 1)] + values(0)))
    interleave(chunk_0, one_behind_another([conditioned(1)] + keys(1) + queries(1) + values(1)), every=2)
    wait(pool, picked, cw_half[0])
    ld_pack0 = [dma_event("ld_pack0_0").mark(pool.indirect_dma_start(
        stage[:, 0:PK0], None, A["pack0"], bass.IndirectOffsetOnAxis(ap=dyn0[:, 0:1], axis=0)))]
    share_banks(True)
    interleave(attention(1), one_behind_another([conditioned(2), conditioned(3)] + queries(2)), every=2)
    k_free = q_free[1]
    share_banks(False)
    interleave(flush(), one_behind_another(keys(2)))
    interleave(attention(2), one_behind_another(values(2) + keys(3) + values(3) + queries(3)), every=2)
    share_banks(True)

    top[0] = phase_top
    HT = H0 // P
    wBh, wBl, bB = [], [], []
    for b in range(B):
        wBh.append(sb("expert0_hi", [P, PK0 - 2 * HT], F32R))
        wBl.append(sb("expert0_lo", [P, PK0 - 2 * HT], F32R))
        bB.append(sb("expert0_biases", [P, 2, HT]))
        if not b:
            assert top[0] <= projected_top
    downB = [sb("expert0_bias_down", [P, D]) for _ in range(B)]
    wgT = sb("router_weights", [P, KD, G])
    act_out = [sb("silu", [P, CH]) for _ in range(2)]
    prod = [sb("hidden", [P, CH]) for _ in range(2)]
    hidH, hidL = [], []
    for _ in range(2):
        hidH.append(sb("hidden_hi", [P, HT, CH], F32R))
        hidL.append(sb("hidden_lo", [P, HT, CH], F32R))
        if len(hidH) == 1:
            assert top[0] <= scored_top
    xrow = [sb("x_rows", [P, D]) for _ in range(6)]
    xcol = [sb("x_columns", [P, KD, P]) for _ in range(2)]
    GH = G * HIGH
    lg = [sb("logits", [P, QT, G]) for _ in range(2)]
    lg2, pos = (sb(n, [P, QT, G]) for n in ("logits_but_first", "position"))
    oh, tmp = (sb(n, [P, K, QT, G]) for n in ("expert_onehots", "route_tmp"))
    M16 = [sb("routed_bf16", [P, QT, G], BF16) for _ in range(2)]
    counts = [sb("routed_before", [P, G]) for _ in range(2)]
    eight_less, row = (sb(n, [P, K, QT]) for n in ("eight_minus_picked", "row"))
    row_int = sb("row_int", [P, K, QT], I32)
    digits_int = sb("column_and_low_int", [P, 2, K, QT], I32)
    digits = sb("column_and_low", [P, 2, K, QT])
    ramp = sb("ramp", [P, GH])
    ramp_low = sb("ramp_low", [P, P // LOW, LOW])
    tok = sb("token_number", [P, NT])
    at_col = [sb("token_at_column", [P, GH], F32R) for _ in range(K * QT)]
    at_low = [sb("at_low", [P, P], F32R) for _ in range(K * QT)]

    def parts(ap, n):
        return (ap[:, 0:KD * n].rearrange("p (k n) -> p k n", k=KD), ap[:, KD * n:2 * KD * n].rearrange("p (k n) -> p k n", k=KD),
                ap[:, 2 * KD * n:2 * KD * n + (n // P) * D].rearrange("p (k n) -> p k n", n=D))

    w_ready = [[None, None, ld_pack0[0]], [None, None, None]]

    def fetch_down_bias(b):
        w_ready[b][1] = dma_event(f"ld_bdown_{b}").mark(pool.indirect_dma_start(
            downB[b][:, :], None, A["b_down"], bass.IndirectOffsetOnAxis(ap=dynb[:, b:b + 1], axis=0)))

    def prepare0(b, *free):
        a = w_ready[b][2]
        st = stage[:, b * PK0:(b + 1) * PK0]
        n = PK0 - 2 * HT
        wait(act, *free)
        wait(dve, *free)
        pieces = 6
        for q in range(pieces):
            qs = slice(q * n // pieces, (q + 1) * n // pieces)
            m = split_weights(wBh[b][:, qs], wBl[b][:, qs], st[:, qs], (a,), dve)
            if q < pieces - 1:
                yield
        w_ready[b][0] = m
        w_ready[b][2] = e_acs.mark(act.copy(bB[b][:, :, :], st[:, n:n + 2 * HT].rearrange("p (a h) -> p a h", a=2)))
        yield

    b_work = Ring([banks[:, i, :] for i in range(3)])
    b_down = Ring([banks[:, 3, :], banks[:, 4, :]])
    inverse = banks[:, 7, 0:GH]
    r_act, r_prod, r_hid = Ring(act_out), Ring(prod), Ring([0, 1])
    r_xrow, r_xcol, r_at = Ring(xrow), Ring(xcol), Ring(list(range(2 * QT)))
    e_act = Event(nc, "activated")
    e_prod = Event(nc, "hidden_product")
    e_row = Event(nc, "x_row_written")
    e_col = Event(nc, "x_column_written")
    e_log = Event(nc, "logits_in_psum")
    e_cnt = Event(nc, "counts_in_psum")
    e_inv = Event(nc, "slots_in_psum")
    e_at = Event(nc, "slot_onehots")
    st_x = [dma_event(f"st_x{i}") for i in range(6)]

    def gated_unit(first, second, func, bias, scale, gate_bias, width, hi, lo):
        i0, b0, ready0 = first
        i1, b1, ready1 = second
        ai, s = r_act.take(act)
        wait(act, ready0)
        x = e_act.mark(act.activation(s[:, 0:width], b0, func, bias=bias))
        b_work.release(i0, x)
        hi_, h = r_prod.take(dve)
        wait(dve, x, ready1)
        if gate_bias is not None:
            y = e_prod.mark(dve.scalar_tensor_tensor(h[:, 0:width], b1, gate_bias, s[:, 0:width], ALU.add, ALU.mult))
        elif scale is not None:
            y = e_prod.mark(dve.scalar_tensor_tensor(h[:, 0:width], b1, scale, s[:, 0:width], ALU.mult, ALU.mult))
        else:
            y = e_prod.mark(dve.tensor_tensor(h[:, 0:width], b1, s[:, 0:width], ALU.mult))
        b_work.release(i1, y)
        r_act.release(ai, y)
        z = split_rows(hi, lo, h[:, 0:width], (y,))
        r_prod.release(hi_, z)
        return z

    def work(width, terms):
        i, bank = b_work.take(pe)
        return i, bank[:, 0:width], e_mm.mark(products(bank[:, 0:width], terms))

    hidden = {}

    def up_chunk(c):
        b = c // CPB
        s = slice(c * CH, (c + 1) * CH)
        uh, gh, _ = parts(wBh[b], H0)
        ul, gl, _ = parts(wBl[b], H0)
        wait(pe, in_x[c], w_ready[b][0])
        wait(act, w_ready[b][2])
        hi_, _ = r_hid.take(act)
        for i in range(HT):
            ms = slice(i * P, (i + 1) * P)
            up = work(CH, [(uh[:, k, ms], ul[:, k, ms], inH[:, k, s], inL[:, k, s]) for k in range(KD)])
            yield
            gate = work(CH, [(gh[:, k, ms], gl[:, k, ms], inH[:, k, s], inL[:, k, s]) for k in range(KD)])
            z = gated_unit(up, gate, ACT.Silu, bB[b][:, 0, i:i + 1], None, bB[b][:, 1, i:i + 1], CH,
                           hidH[hi_][:, i, :], hidL[hi_][:, i, :])
            hidden[c] = (hi_, z)
            yield

    x_rows = {}

    def down_chunk(c):
        b = c // CPB
        hi_, z = hidden[c]
        dh, dl = parts(wBh[b], H0)[2], parts(wBl[b], H0)[2]
        wait(pe, z)
        wait(dve, w_ready[b][1])
        for t in range(QT):
            ts = slice(t * P, (t + 1) * P)
            bi, bank = b_down.take(pe)
            m = e_mm.mark(products(bank[:, 0:D], [(hidH[hi_][:, k, ts], hidL[hi_][:, k, ts], dh[:, k, :], dl[:, k, :]) for k in range(HT)]))
            xi, xr = r_xrow.take(dve)
            wait(dve, m)
            y = e_row.mark(dve.tensor_tensor(xr[:, :], bank[:, 0:D], downB[b][:, :], ALU.add))
            b_down.release(bi, y)
            tt = c * QT + t
            wait(sp, y)
            stored = st_x[xi].mark(sp.dma_start(rows_in[tt * P:(tt + 1) * P, :], xr[:, :]))
            x_rows[tt] = (xi, xr, y, stored)
            yield
        r_hid.release(hi_, m)

    def chunk_logits(c):
        columns = None

        def logits(t, xc, ci, y):
            wait(pe, y, ld_wg)
            ti, bank = b_turn.take(pe)
            for k in range(KD):
                last = pe.matmul(bank[:, 0:G], xc[:, k, :], wgT[:, k, :], start=(k == 0), stop=(k == KD - 1))
            m = e_log.mark(last)
            r_xcol.release(ci, m)
            wait(dve, m)
            y = e_vec.mark(dve.tensor_copy(lg[c % 2][:, t, :], bank[:, 0:G]))
            b_turn.release(ti, y)
            return y

        for t in range(QT):
            tt = c * QT + t
            while min(tt + 1, NT - 1) not in x_rows and (t + 1 < QT or tt not in x_rows):
                yield
            xi, xr, y, stored = x_rows[tt]
            wait(pe, y)
            ti, bank = b_turn.take(pe)
            for k in range(KD):
                last = pe.transpose(bank[:, k * P:(k + 1) * P], xr[:, k * P:(k + 1) * P], ident[:, :])
            m = e_t.mark(last)
            r_xrow.release(xi, m, stored)
            ci, xc = r_xcol.take(act)
            wait(act, m)
            y = e_col.mark(act.copy(xc[:, :, :], bank[:, 0:D].rearrange("p (k t) -> p k t", k=KD)))
            b_turn.release(ti, y)
            if columns:
                logits(*columns)
            columns = (t, xc, ci, y)
            yield
        logits_ready[c] = logits(*columns)
        yield

    logits_ready = {}

    def route_chunk(c):
        nonlocal slot_mark
        while c not in logits_ready:
            yield
        wait(dve, logits_ready[c])
        top2, place, first_row = all_top2[:, c, :, :], all_places[:, c, :, :], all_first_rows[:, c, :, :]
        first_max(lg[c % 2][:, :, :], QT, top2[:, 0, :], oh[:, 0, :, :], tmp[:, 0, :, :], eight_less[:, 0, :])
        yield
        second_input(lg2[:, :, :], lg[c % 2][:, :, :], oh[:, 0, :, :])
        yield
        first_max(lg2[:, :, :], QT, top2[:, 1, :], oh[:, 1, :, :], tmp[:, 1, :, :], eight_less[:, 1, :])
        r_m = v_step(dve.tensor_tensor(M16[c % 2][:, :, :], oh[:, 0, :, :], oh[:, 1, :, :], ALU.add))
        yield
        v_step(dve.tensor_scalar(first_row[:, :, :], eight_less[:, :, :], -float(CAP), float(G * CAP), ALU.mult, ALU.add))
        yield
        wait(pe, r_m)
        ti, bank = b_turn.take(pe)
        for t in range(QT):
            ranks = bank[:, t * G:(t + 1) * G]
            for u in range(t):
                pe.matmul(ranks, ones16[:, :], M16[c % 2][:, u, :], start=(u == 0), stop=False)
            pe.matmul(ranks, before[:, :], M16[c % 2][:, t, :], start=(t == 0), stop=True)
        for u in range(QT):
            last = pe.matmul(bank[:, QT * G:(QT + 1) * G], ones16[:, :], M16[c % 2][:, u, :], start=(u == 0), stop=(u == QT - 1))
        mt = e_cnt.mark(last)
        wait(dve, mt, ramps)
        cnt = counts[c % 2][:, :].rearrange("p (a g) -> p a g", a=1).broadcast_to((P, QT, G))
        both = pos[:, :, :].rearrange("p t g -> p (t g)").rearrange("p (a n) -> p a n", a=1).broadcast_to((P, K, QT * G))
        v_step(dve.tensor_tensor(pos[:, :, :], bank[:, 0:QT * G].rearrange("p (t e) -> p t e", e=G), cnt, ALU.add))
        y = v_step(dve.tensor_tensor(counts[1 - c % 2][:, :], bank[:, QT * G:(QT + 1) * G], counts[c % 2][:, :], ALU.add))
        b_turn.release(ti, y)
        yield
        v_step(dve.tensor_tensor(tmp[:, :, :, :].rearrange("p k t g -> p k (t g)"), oh[:, :, :, :].rearrange("p k t g -> p k (t g)"), both, ALU.mult))
        v_step(dve.tensor_reduce(place[:, :, :].rearrange("p k t -> p (k t)"), tmp[:, :, :, :].rearrange("p k t g -> p (k t) g"), AX.X, ALU.add))
        yield
        v_step(dve.tensor_scalar(row[:, :, :], place[:, :, :], float(CAP), float(4 * N * LOW), ALU.is_ge, ALU.mult))
        v_step(dve.tensor_tensor(row[:, :, :], row[:, :, :], place[:, :, :], ALU.add))
        v_step(dve.tensor_tensor(row_int[:, :, :], row[:, :, :], first_row[:, :, :], ALU.add))
        e_vec.mark(dve.tensor_single_scalar(digits_int[:, 0, :, :], row_int[:, :, :], LOW.bit_length() - 1, ALU.logical_shift_right))
        v_step(dve.tensor_single_scalar(digits_int[:, 1, :, :], row_int[:, :, :], LOW - 1, ALU.bitwise_and))
        v_step(dve.tensor_copy(digits[:, :, :, :], digits_int[:, :, :, :]))
        yield
        for k in range(K):
            ready = []
            for t in range(QT):
                ai, _ = r_at.take(dve)
                tt = c * QT + t
                dve.tensor_scalar(at_col[ai][:, :], ramp[:, :], digits[:, 0, k, t:t + 1], tok[:, tt:tt + 1], ALU.is_equal, ALU.mult)
                ready.append((ai, t, e_at.mark(dve.tensor_scalar(at_low[ai][:, :], ramp_low[:, :, :].rearrange("p q l -> p (q l)"),
                                                                 digits[:, 1, k, t:t + 1], None, ALU.is_equal))))
            yield
            for ai, t, y in ready:
                wait(pe, y)
                slot_mark = e_inv.mark(pe.matmul(inverse, at_low[ai][:, :], at_col[ai][:, :], start=(c == 0 and k == 0 and t == 0),
                                                 stop=(c == NCH - 1 and k == 1 and t == QT - 1)))
                r_at.release(ai, slot_mark)

    def way_back():
        nonlocal rows_ready
        d = v_step(dve.tensor_tensor(diff[:, :, :], all_top2[:, :, 1, :], all_top2[:, :, 0, :], ALU.subtract))
        wait(act, d)
        x = e_acs.mark(act.activation(raw_gates[:, :, 1, :], diff[:, :, :], ACT.Exp))
        picks = pick_L1_cond()
        next(picks)
        v_step(dve.tensor_scalar(kept[:, :, :, :], all_places[:, :, :, :], float(CAP - 1), None, ALU.min))
        v_step(dve.tensor_tensor(rows[:, :, :, :], kept[:, :, :, :], all_first_rows[:, :, :, :], ALU.add))
        yield
        v_step(dve.tensor_scalar(kept[:, :, :, :], all_places[:, :, :, :], float(CAP), None, ALU.is_lt))
        wait(dve, x)
        v_step(dve.tensor_scalar(diff[:, :, :], raw_gates[:, :, 1, :], 1.0, None, ALU.add))
        v_step(dve.reciprocal(raw_gates[:, :, 0, :], diff[:, :, :]))
        yield
        v_step(dve.tensor_tensor(raw_gates[:, :, 1, :], raw_gates[:, :, 1, :], raw_gates[:, :, 0, :], ALU.mult))
        rows_ready = v_step(dve.tensor_tensor(gates[:, :, :, :], kept[:, :, :, :], raw_gates[:, :, :, :], ALU.mult))
        yield
        yield from picks

    projected = ((e_mm, e_mm.count), (e_lo, e_lo.count), (e_rope, e_rope.count))
    interleave(attention(3), prepare0(0, *projected), 3)
    for i in range(3):
        b_work.release(i, *(m for marks in b_score.free for m in marks))
    ups = [up_chunk(c) for c in range(NCH)]
    interleave(flush(), some(ups[0], 3))

    attention_done = ((e_mm, e_mm.count), (e_lo, e_lo.count))
    wait(pool, *attention_done)
    wait(sp, *attention_done)
    ld_wg = load(sp, wgT[:, :, :], A["WgT"], "ld_wg")
    w_ready[1][2] = dma_event("ld_pack0_1").mark(pool.indirect_dma_start(
        stage[:, PK0:2 * PK0], None, A["pack0"], bass.IndirectOffsetOnAxis(ap=dyn0[:, 1:2], axis=0)))
    fetch_down_bias(0)
    fetch_down_bias(1)
    b_turn = Ring([banks[:, 5, :], banks[:, 6, :]])
    e_cst2 = Event(nc, "route_constants")
    e_cst2.mark(pool.memset(counts[0][:, :], 0.0))
    e_cst2.mark(pool.iota(ramp[:, :], [[1, GH]], base=0, channel_multiplier=0, allow_small_or_imprecise_dtypes=True))
    e_cst2.mark(pool.iota(ramp_low[:, :, :], [[0, P // LOW], [1, LOW]], base=0, channel_multiplier=0, allow_small_or_imprecise_dtypes=True))
    ramps = e_cst2.mark(pool.iota(tok[:, :], [[P, NT]], base=0, channel_multiplier=1, allow_small_or_imprecise_dtypes=True))

    rows_ready = slot_mark = None

    beside = top[0]
    top[0] = phase_top
    IT = I0 // P
    w1H, w1L, w2H, w2L = [], [], [], []
    for _ in range(2):
        w1H.append(sb("ffn_w1_hi", [P, KD, 2 * I0], F32R))
        w1L.append(sb("ffn_w1_lo", [P, KD, 2 * I0], F32R))
        w2H.append(sb("ffn_w2_hi", [P, IT, D], F32R))
        w2L.append(sb("ffn_w2_lo", [P, IT, D], F32R))
    ffn_top = top[0]
    top[0] = beside
    ld_f = [dma_event(f"ld_packF{i}") for i in range(2)]
    w1_free, w2_free, stage_free = [(), ()], [(), ()], [(), ()]

    def fetch_weights(e):
        s = e % 2
        wait(sp, *stage_free[s])
        return ld_f[s].mark(sp.dma_start(stage[:, s * PK0:s * PK0 + PKF], A["packF"][e]))

    def split_expert(e, loaded):
        s = e % 2
        st = stage[:, s * PK0:s * PK0 + PKF]
        n1 = KD * 2 * I0
        for k in range(KD):
            for part in range(2):
                ps, a = slice(part * I0, (part + 1) * I0), (2 * k + part) * I0
                m1_ = split_weights(w1H[s][:, k, ps], w1L[s][:, k, ps], st[:, a:a + I0], (loaded, *w1_free[s]))
                yield
        for k in range(0, IT, 2):
            a = n1 + k * D
            m2_ = split_weights(w2H[s][:, k:k + 2, :], w2L[s][:, k:k + 2, :], st[:, a:a + 2 * D].rearrange("p (k n) -> p k n", n=D), (loaded, *w2_free[s]))
            if k + 2 < IT:
                yield
        stage_free[s] = (m2_,)
        return m1_, m2_

    loaded, first_split = [], []

    def expert_0_weights():
        w1_free[0] = w2_free[0] = ((e_mm, e_mm.count),)
        first_split.append((yield from split_expert(0, loaded[0])))

    def all_chunks():
        yield from ups[0]
        loaded.append(fetch_weights_when(0))
        weights = chain([None] * 4, prepare0(1))
        for c in range(NCH):
            if c == CPB:
                loaded.append(fetch_weights_when(1))
                weights = expert_0_weights()
            steps = chain(some(ups[c + 1], HT + 1), down_chunk(c), ups[c + 1]) if c + 1 < NCH else chain([None] * 3, down_chunk(c))
            yield from interleave_steps(steps, weights)

    def fetch_weights_when(e):
        stage_free[e] = (w_ready[e][0], w_ready[e][2])
        return fetch_weights(e)

    interleave(interleave_steps(all_chunks(), chain(*[chunk_logits(c) for c in range(NCH)])),
               chain(*[route_chunk(c) for c in range(NCH)]))
    w1_free[1] = w2_free[1] = ((e_mm, e_mm.count),)
    wait(act, slot_mark)
    inv = inverse.rearrange("p (e h) -> p e h", e=G)
    for q in range(P // LOW):
        qs = slice(q * LOW, (q + 1) * LOW)
        slots_ready = e_acs.mark(act.copy(slot_token[qs, :].rearrange("p (e j) -> p e j", e=G),
                                          inv[qs, :, :].rearrange("p e (j q) -> p e j q", q=P // LOW)[:, :, :, q]))

    top[0] = ffn_top
    IT1 = I1 // P
    heH, heL = sb("expert_hidden_hi", [P, IT, CAP], F32R), sb("expert_hidden_lo", [P, IT, CAP], F32R)
    xeH = [sb("expert_in_hi", [P, KD, CAP], F32R) for _ in range(2)]
    xeL = [sb("expert_in_lo", [P, KD, CAP], F32R) for _ in range(2)]
    got_at = top[0]
    got = [sb("gathered", [P, D]) for _ in range(ST + 1)]
    act_out = [sb("gelu", [P, CH]) for _ in range(2)]
    prod = [sb("hidden", [P, CH]) for _ in range(2)]
    yrow = [sb("y_rows", [P, D]) for _ in range(4)]
    last_top = nc.sbuf_usable_end // 32 * 32 - 4 * PK1
    assert top[0] <= last_top
    top[0] = last_top
    wDl = [sb("mlp_lo", [P, PK1], F32R)]
    top[0] = phase_top
    wDh = [sb("mlp_hi", [P, PK1], F32R) for _ in range(2)]
    wDl.append(sb("mlp_lo", [P, PK1], F32R))
    hiD = [sb("hidden_hi", [P, CH], F32R) for _ in range(4)]
    loD = [sb("hidden_lo", [P, CH], F32R) for _ in range(4)]
    assert top[0] <= got_at
    top[0] = got_at
    y1 = [sb("y_first", [P, D]) for _ in range(3)]
    y2 = [sb("y_second", [P, D]) for _ in range(3)]
    r_act, r_prod = Ring(act_out), Ring(prod)
    b_work = Ring([banks[:, i, :] for i in range(4)])
    b_turn = Ring([banks[:, 4, :], banks[:, 5, :]])
    b_down = Ring([banks[:, 6, :], banks[:, 7, :]])
    r_got, r_xe, r_he, r_y = Ring(got), Ring([0, 1]), Ring([0]), Ring(yrow)
    ld_got = [dma_event(f"gather{i}") for i in range(ST + 1)]
    st_y = [dma_event(f"st_y{i}") for i in range(4)]
    e_y = Event(nc, "y_row_written")
    wait(pool, slots_ready)
    for i in range(6):
        wait(pool, (st_x[i], st_x[i].count))

    def gather(e):
        res = []
        for j in range(ST):
            gi, g = r_got.take(pool)
            n = e * ST + j
            res.append((gi, g, ld_got[gi].mark(pool.indirect_dma_start(g[:, :], None, rows_in, bass.IndirectOffsetOnAxis(ap=slot_token[:, n:n + 1], axis=0)))))
        return res

    def turn_in(e, tiles):
        xi, _ = r_xe.take(act)
        for j, (gi, g, m) in enumerate(tiles):
            wait(pe, m)
            ti, bank = b_turn.take(pe)
            for k in range(KD):
                last = pe.transpose(bank[:, k * P:(k + 1) * P], g[:, k * P:(k + 1) * P], ident[:, :])
            t = e_t.mark(last)
            r_got.release(gi, t)
            js = slice(j * P, (j + 1) * P)
            lo = evacuate(xeH[xi][:, :, js], xeL[xi][:, :, js], bank[:, 0:D].rearrange("p (k t) -> p k t", k=KD), None, t, ())
            b_turn.release(ti, lo)
            yield
        return xi, lo

    def coming_expert(e):
        weights = first_split[0] if e == 0 else (yield from split_expert(e, loaded[e]))
        if e + 2 < G:
            loaded.append(fetch_weights(e + 2))
        elif e + 1 == G:
            loaded.append(fetch_mlp(0, 0, *stage_free[0], *stage_free[1]))
        yield
        rows_turned = yield from turn_in(e, tiles)
        coming[e] = (*rows_turned, weights)

    def up_expert(e, xi, ready, wm):
        s = e % 2
        hi_, _ = r_he.take(act)
        wait(pe, ready, wm[0])
        halves = []
        for h in range(2):
            hs = slice(h * HALF, (h + 1) * HALF)
            for i in range(IT):
                both = []
                for part in range(2):
                    ms = slice(part * I0 + i * P, part * I0 + (i + 1) * P)
                    both.append(work(HALF, [(w1H[s][:, k, ms], w1L[s][:, k, ms], xeH[xi][:, k, hs], xeL[xi][:, k, hs]) for k in range(KD)]))
                m = both[1][2]
                z = gated_unit(*both, ACT.Gelu, 0.0, None, None, HALF, heH[:, i, hs], heL[:, i, hs])
                yield
            halves.append(z)
        w1_free[s] = (m,)
        r_xe.release(xi, m)
        return hi_, halves

    def down_expert(e, hi_, ready, wm):
        s = e % 2
        wait(pe, wm[1])
        for j in range(ST):
            wait(pe, ready[0 if (j + 1) * P <= HALF else 1])
            js = slice(j * P, (j + 1) * P)
            bi, bank = b_down.take(pe)
            m = e_mm.mark(products(bank[:, 0:D], [(heH[:, k, js], heL[:, k, js], w2H[s][:, k, :], w2L[s][:, k, :]) for k in range(IT)]))
            yi, y = r_y.take(dve)
            wait(dve, m)
            c = e_y.mark(dve.tensor_copy(y[:, :], bank[:, 0:D]))
            b_down.release(bi, c)
            wait(sp, c)
            r0 = e * CAP + j * P
            r_y.release(yi, st_y[yi].mark(sp.dma_start(rows_out[r0:r0 + P, :], y[:, :])))
            yield
        w2_free[s] = (m,)
        r_he.release(hi_, m)

    ld_d, ld_dyn = dma_event("ld_mlp"), dma_event("ld_picked_mlp")
    stD_free = ()
    PIECES = 8
    PIECE = PK1 // PIECES

    def fetch_mlp(b, j, *free):
        if j < 2:
            n = 2 * b + j
            wait(pool, picked1, *free)
            return ld_dyn.mark(pool.indirect_dma_start(stage[:, 0:PK1], None, A["pack1"], bass.IndirectOffsetOnAxis(ap=dyn1[:, n:n + 1], axis=0)))
        wait(sp, *free)
        return ld_d.mark(sp.dma_start(stage[:, 0:PK1], A["shared"]))

    def split_mlp(n, ready, free):
        nonlocal stD_free, w_next
        s = n % 2
        wait(act, *free)
        for q in range(PIECES):
            qs = slice(q * PIECE, (q + 1) * PIECE)
            w_next = split_weights(wDh[s][:, qs], wDl[s][:, qs], stage[:, qs], (ready,), dve if n == 1 else pool)
            stD_free = (w_next,)
            yield

    w_next = None
    tiles = gather(0)
    coming = {}
    run_all(coming_expert(0))

    def expert(e):
        xi, ready, weights = coming[e]
        hid = yield from up_expert(e, xi, ready, weights)
        yield from down_expert(e, *hid, weights)

    for e in range(G):
        if e + 1 < G:
            tiles = gather(e + 1)
            steps = interleave_steps(expert(e), way_back()) if e == 1 else expert(e)
            interleave(steps, coming_expert(e + 1))
        else:
            interleave(expert(e), split_mlp(0, loaded[G], (*w1_free[0], *w2_free[0])))

    r_y12, r_h = Ring([0, 1, 2]), Ring([0, 1, 2, 3])
    ld_y1 = [dma_event(f"ld_y1_{i}") for i in range(3)]
    ld_y2 = [dma_event(f"ld_y2_{i}") for i in range(3)]
    e_comb = Event(nc, "rows_combined")
    for i in range(4):
        wait(pool, (st_y[i], st_y[i].count))
    wait(pool, rows_ready)
    wait(dve, rows_ready)

    middle_top = phase_top + 4 * PK1
    top[0] = phase_top
    t1w = sb("ternary_w1", [P, KD, FF], F32R)
    t2w = sb("ternary_w2", [P, FF // P, D], F32R)
    below = sb("below_minus_half", [P, KD * FF])
    assert top[0] <= middle_top
    top[0] = last_top
    gwH = sb("gru_weights_hi", [P, 2, KD, D], F32R)
    gwL = sb("gru_weights_lo", [P, 2, KD, D], F32R)
    lbw = [sb("lora_b_weighted", [P, D]) for _ in range(B)]
    bwF = [sb("adapted_weights", [P, KD, D]) for _ in range(B)]
    bwH = [sb("adapted_weights_hi", [P, KD, D], F32R) for _ in range(B)]
    bwL = [sb("adapted_weights_lo", [P, KD, D], F32R) for _ in range(B)]
    ld_tail = [dma_event(f"ld_{k}") for k in ("ffn_w1", "ffn_w2", "gru_w", "base_w", "lora_a", "lora_b", "cond_rep")]
    tern, base_w, gru_w = [], [], []

    def tail_weights(free, place_free):
        W = KD * FF
        views, at = [], 0
        for k in ("ffn_w1", "ffn_w2", "gru_w", "base_w", "lora_a", "lora_b", "cond_rep"):
            src = A[k]
            n = int(np.prod(src.shape[1:]))
            views.append((stage[:, at:at + n], src))
            at += n
        loads = []
        wait(sp, *free)
        for i in (4, 5, 6, 3, 2, 0, 1):
            dst, src = views[i]
            if len(src.shape) == 3:
                src = src.rearrange("p k n -> p (k n)")
            elif len(src.shape) == 4:
                src = src.rearrange("p w k n -> p (w k n)")
            loads.append(ld_tail[i].mark(sp.dma_start(dst, src)))
        w1_st, w2_st, gw_st, bw_st, la, lb, crep = (v[0] for v in views)
        yield
        wait(dve, *place_free, *loads)
        wait(act, *place_free, *loads)
        wait(pe, *loads)
        for b in range(B):
            m = e_vec.mark(dve.tensor_scalar(lbw[b][:, :], lb, crep[:, b:b + 1], 2.0, ALU.mult, ALU.mult))
            yield
            wait(pe, m)
            i, bank = b_work.take(pe)
            for k in range(KD):
                last = pe.matmul(bank[:, k * D:(k + 1) * D], la[:, k * P:(k + 1) * P], lbw[b][:, :], start=True, stop=True)
            t = e_mm.mark(last)
            wait(dve, t)
            t = e_vec.mark(dve.tensor_tensor(bwF[b][:, :, :].rearrange("p k n -> p (k n)"), bank, bw_st, ALU.add))
            b_work.release(i, t)
            base_w.append(split_rows(bwH[b][:, :, :], bwL[b][:, :, :], bwF[b][:, :, :], (t,)))
            yield
        gru_w.append(split_weights(gwH[:, :, :, :].rearrange("p w k n -> p (w k n)"), gwL[:, :, :, :].rearrange("p w k n -> p (w k n)"), gw_st, (loads[4],)))
        Q = W // 4
        stats = []
        for n, st in enumerate((w1_st, w2_st)):
            sums = tiny[:, 200 + 8 * n:204 + 8 * n]
            for q in range(4):
                qs = slice(q * Q, (q + 1) * Q)
                v_step(dve.scalar_tensor_tensor(below[:, qs], st[:, qs], -1.0, st[:, qs], ALU.mult, ALU.max))
                m = v_step(dve.tensor_reduce(sums[:, q:q + 1], below[:, qs], AX.X, ALU.add))
                if q % 2:
                    yield
            stats.append((sums, m))
        for n, (st, tw) in enumerate(((w1_st, t1w), (w2_st, t2w))):
            sums, m = stats[n]
            half_, neg = (tiny[:, 204 + 8 * n + a:205 + 8 * n + a] for a in range(2))
            wait(pe, m)
            i, bank = b_work.take(pe)
            for q in range(4):
                last = pe.matmul(bank[:, 0:1], ones32[:, :], sums[:, q:q + 1], start=(q == 0), stop=(q == 3))
            t = e_mm.mark(last)
            wait(dve, t)
            t = v_step(dve.tensor_scalar(half_, bank[:, 0:1], 1.0 / (FF * D), 1e-8, ALU.mult, ALU.max))
            b_work.release(i, t)
            v_step(dve.tensor_scalar(neg, half_, -0.5, None, ALU.mult))
            v_step(dve.tensor_scalar(half_, half_, 0.5, None, ALU.mult))
            flat = tw[:, :, :].rearrange("p k n -> p (k n)")
            for q in range(4):
                qs = slice(q * Q, (q + 1) * Q)
                v_step(dve.tensor_scalar(below[:, qs], st[:, qs], neg, None, ALU.is_lt))
                m = v_step(dve.scalar_tensor_tensor(flat[:, qs], st[:, qs], half_, below[:, qs], ALU.is_gt, ALU.subtract))
                if q % 2:
                    yield
            tern.append(m)

    def combine_tile(tt):
        i, _ = r_y12.take(pool)
        fetched = [ev[i].mark(pool.indirect_dma_start(buf[i][:, :], None, rows_out, bass.IndirectOffsetOnAxis(ap=rows[:, tt // QT, k, tt % QT:tt % QT + 1], axis=0)))
                   for k, (buf, ev) in enumerate(((y1, ld_y1), (y2, ld_y2)))]
        yield
        wait(dve, fetched[0])
        v_step(dve.tensor_scalar(y1[i][:, :], y1[i][:, :], gates[:, tt // QT, 0, tt % QT:tt % QT + 1], None, ALU.mult))
        wait(dve, fetched[1])
        a = e_comb.mark(dve.scalar_tensor_tensor(y1[i][:, :], y2[i][:, :], gates[:, tt // QT, 1, tt % QT:tt % QT + 1], y1[i][:, :], ALU.mult, ALU.add))
        yield
        wait(pe, a)
        bi, bank = b_work.take(pe)
        for k in range(KD):
            last = pe.transpose(bank[:, k * P:(k + 1) * P], y1[i][:, k * P:(k + 1) * P], ident[:, :])
        m = e_t.mark(last)
        r_y12.release(i, m)
        wait(dve, m)
        s = slice(tt * P, (tt + 1) * P)
        x = e_x.mark(dve.tensor_tensor(xT[:, :, s], bank[:, 0:D].rearrange("p (k t) -> p k t", k=KD), xT[:, :, s], ALU.add))
        b_work.release(bi, x)
        in_x[tt // QT] = split_rows(inH[:, :, s], inL[:, :, s], xT[:, :, s], (x,))

    def combine_tiles(first, end):
        live = []
        for tt in range(first, end + 2):
            if tt < end:
                live.append(combine_tile(tt))
            live = [g for g in live if next(g, "ended") != "ended"]
            yield

    acc_free = [tuple(m for ring in (b_turn, b_down) for marks in ring.free for m in marks)] * CPB
    run_all(combine_tiles(0, QT))
    loaded = fetch_mlp(0, 1, *stD_free)
    combining = combine_tiles(QT, NT)
    w_m = w_next
    mlp_down = []

    def down_unit():
        b, j, c, i, hi_, z, s = mlp_down.pop(0)
        wait(pe, z)
        dh, dl = parts(wDh[s], I1)[2], parts(wDl[s], I1)[2]
        first, final = (j == 0 and i == 0), (j == 2 and i == IT1 - 1)
        if first:
            wait(pe, *acc_free[c])
        for m in range(KD):
            ms = slice(m * P, (m + 1) * P)
            o = banks[:, 4 + 2 * c + m, :]
            pe.matmul(o, dh[:, i, ms], hiD[hi_][:, :], start=first, stop=False)
            pe.matmul(o, dh[:, i, ms], loD[hi_][:, :], start=False, stop=False)
            last = pe.matmul(o, dl[:, i, ms], hiD[hi_][:, :], start=False, stop=final)
        m = e_mm.mark(last)
        r_h.release(hi_, m)
        if final:
            cc = b * CPB + c
            ts = slice(cc * CH, (cc + 1) * CH)
            for k in range(KD):
                in_x[cc] = evacuate(inH[:, k, ts], inL[:, k, ts], banks[:, 4 + 2 * c + k, :], None, m, ())
            acc_free[c] = (in_x[cc],)
        return m

    for n in range(3 * B):
        b, j = n // 3, n % 3
        s = n % 2
        gh, uh, _ = parts(wDh[s], I1)
        gl, ul, _ = parts(wDl[s], I1)
        wait(pe, w_m)
        for u in range(CPB * IT1):
            c, i = u // IT1, u % IT1
            cc = b * CPB + c
            ts = slice(cc * CH, (cc + 1) * CH)
            if i == 0:
                wait(pe, in_x[cc])
            ms = slice(i * P, (i + 1) * P)
            gate = work(CH, [(gh[:, k, ms], gl[:, k, ms], inH[:, k, ts], inL[:, k, ts]) for k in range(KD)])
            up = work(CH, [(uh[:, k, ms], ul[:, k, ms], inH[:, k, ts], inL[:, k, ts]) for k in range(KD)])
            hi_, _ = r_h.take(act)
            weight = wsel[:, b, j:j + 1] if j < 2 else None
            z = gated_unit(gate, up, ACT.Gelu_apprx_tanh, 0.0, weight, None, CH, hiD[hi_][:, :], loD[hi_][:, :])
            m = up[2]
            mlp_down.append((b, j, c, i, hi_, z, s))
            if len(mlp_down) > 2:
                m = down_unit()
            if u == 2:
                following = split_mlp(n + 1, loaded, (m,)) if n + 1 < 3 * B else tail_weights(stD_free, (m,))
            if u > (6 if n + 1 < 3 * B else 2):
                next(following, None)
            if u == CPB * IT1 - 1 and n + 2 < 3 * B:
                loaded = fetch_mlp((n + 2) // 3, (n + 2) % 3, *stD_free)
            next(combining, None)
        w_m = w_next
    run_all(following)

    top[0] = middle_top
    FT = FF // P
    gate_t = [sb("gates", [P, CH]) for _ in range(2)]
    cand_t = [sb("candidates", [P, CH]) for _ in range(2)]
    state = [sb("state", [P, CH]) for _ in range(4)]
    act_out = [sb("gelu", [P, CH]) for _ in range(3)]
    hiE = [sb("hidden_hi", [P, CH], F32R) for _ in range(4)]
    loE = [sb("hidden_lo", [P, CH], F32R) for _ in range(4)]
    outb = [sb("out", [P, CH]) for _ in range(4)]

    assert top[0] <= last_top
    b_any = b_work

    r_gate, r_state = Ring([0, 1]), Ring(state)
    e_gate = Event(nc, "gru_gates")
    e_scan = Event(nc, "gru_states")
    wait(pe, *gru_w)

    def gru_chunk(c, carry):
        s = slice(c * CH, (c + 1) * CH)
        wait(pe, in_x[c])
        new = []
        for m_ in range(KD):
            ms = slice(m_ * P, (m_ + 1) * P)
            gi, _ = r_gate.take(act)
            for w, (dst, func) in enumerate(((gate_t[gi], ACT.Sigmoid), (cand_t[gi], ACT.Tanh))):
                i, bank = b_any.take(pe)
                t = e_mm.mark(products(bank, [(gwH[:, w, k, ms], gwL[:, w, k, ms], inH[:, k, s], inL[:, k, s]) for k in range(KD)]))
                wait(act, t)
                a = e_gate.mark(act.activation(dst[:, :], bank, func, bias=bias_g[:, w, m_:m_ + 1]))
                b_any.release(i, a)
            si, st = r_state.take(dve)
            wait(dve, a)
            init = 0.0 if carry is None else carry[m_]
            h = e_scan.mark(dve.tensor_tensor_scan(st[:, :], gate_t[gi][:, :], cand_t[gi][:, :], init, ALU.mult, ALU.add))
            r_gate.release(gi, h)
            new.append(st[:, CH - 1:CH])
            wait(dve, h)
            x = e_x.mark(dve.tensor_tensor(xT[:, m_, s], st[:, :], xT[:, m_, s], ALU.add))
            r_state.release(si, x)
        wait(act, t)
        in_x[c] = split_input(c, x)
        return new

    r_gelu, r_he2 = Ring(act_out), Ring([0, 1, 2, 3])
    r_outb = Ring(outb)
    st_out = [dma_event(f"st_out{i}") for i in range(4)]

    def ffn_down(c, i, hi_, z):
        acc = 4 + 2 * (c % 2)
        s = slice(c * CH, (c + 1) * CH)
        wait(pe, z)
        if i == 0:
            wait(pe, *acc_free[c % 2])
        for m in range(KD):
            ms = slice(m * P, (m + 1) * P)
            pe.matmul(banks[:, acc + m, :], t2w[:, i, ms], hiE[hi_][:, :], start=(i == 0), stop=False)
            last = pe.matmul(banks[:, acc + m, :], t2w[:, i, ms], loE[hi_][:, :], start=False, stop=(i == FT - 1))
        m = e_mm.mark(last)
        r_he2.release(hi_, m)
        if i == FT - 1:
            wait(dve, m)
            for k in range(KD):
                oi, o = r_outb.take(dve)
                y = e_x.mark(dve.scalar_tensor_tensor(o[:, :], banks[:, acc + k, :], bias_2[:, k:k + 1], xT[:, k, s], ALU.add, ALU.add))
                wait(sp, y)
                r_outb.release(oi, st_out[oi].mark(sp.dma_start(out[:, k, s], o[:, :])))
            acc_free[c % 2] = (y,)

    under_way = []

    def ffn_chunk(c):
        s = slice(c * CH, (c + 1) * CH)
        wait(pe, in_x[c], *tern)
        for i in range(FT):
            bi, bank = b_any.take(pe)
            ms = slice(i * P, (i + 1) * P)
            for k in range(KD):
                pe.matmul(bank, t1w[:, k, ms], inH[:, k, s], start=(k == 0), stop=False)
                last = pe.matmul(bank, t1w[:, k, ms], inL[:, k, s], start=False, stop=(k == KD - 1))
            m = e_mm.mark(last)
            ai, a = r_gelu.take(act)
            wait(act, m)
            x = e_act.mark(act.activation(a[:, :], bank, ACT.Gelu, bias=bias_1[:, i:i + 1]))
            b_any.release(bi, x)
            hi_, _ = r_he2.take(act)
            z = split_rows(hiE[hi_][:, :], loE[hi_][:, :], a[:, :], (x,))
            r_gelu.release(ai, z)
            under_way.append((c, i, hi_, z))
            if len(under_way) > 3:
                ffn_down(*under_way.pop(0))

    def adapted(c):
        in_x[c] = linear(c, bwH[c // CPB], bwL[c // CPB], bias_b, (base_w[c // CPB], in_x[c]), (b_any, b_any))

    carry = gru_chunk(0, None)
    while mlp_down:
        down_unit()
    gru_chunk(1, carry)
    carry = gru_chunk(2, None)
    adapted(0)
    gru_chunk(3, carry)
    for c in range(1, NCH):
        adapted(c)
    for c in range(NCH):
        ffn_chunk(c)
    while under_way:
        ffn_down(*under_way.pop(0))
    for ev in st_out:
        wait(sp, (ev, ev.count))


def kernel(**inputs):
    import concourse.bacc as _bacc
    from concourse.bass_utils import run_bass_kernel_spmd as _run
    a = {k: np.asarray(v) for k, v in inputs.items()}

    def cols(w, k):
        return w.reshape(k, P, -1).transpose(1, 0, 2)

    def heads(w):
        return w.transpose(1, 0, 2).reshape(D, NH * DH)

    half = HR
    freq = np.power(np.float32(10000.0), (-np.arange(half).astype(np.float32) / np.float32(half)))
    rad = freq[:, None] * np.arange(T, dtype=np.float32)[None, :]
    cos, sin = np.cos(rad), np.sin(rad)
    arrays = {
        "xT": a["x"].reshape(N, D).T.reshape(KD, P, N).transpose(1, 0, 2),
        "cond_8": a["cond_8"],
        "cond_w": a["L0_cond_weight"].transpose(2, 0, 1).reshape(KD, P, G, D).transpose(1, 0, 2, 3),
        "cond_mask": cols(a["L0_cond_mask"].T, KD),
        "cond_bias": a["L0_cond_bias"].reshape(KD, P).T,
        "attn_w": np.stack([cols(heads(a["L0_attn_wq"]), KD), cols(heads(a["L0_attn_wk"]), KD),
                            cols(heads(a["L0_attn_wv"]), KD), cols(a["L0_attn_wo"], KD)], axis=1),
        "ropeC": np.concatenate([cos, cos, np.ones((P - 2 * HR, T), np.float32)]),
        "ropeS": np.concatenate([sin, -sin]),
        "cond_rep": np.repeat(a["cond_8"].T, R, axis=0),
        "pack0": np.concatenate([
            a["L0_cond2_W_up"].transpose(0, 2, 1).reshape(G, KD, P, H0).transpose(0, 2, 1, 3).reshape(G, P, -1),
            a["L0_cond2_W_gate"].transpose(0, 2, 1).reshape(G, KD, P, H0).transpose(0, 2, 1, 3).reshape(G, P, -1),
            a["L0_cond2_W_down"].transpose(0, 2, 1).reshape(G, H0 // P, P, D).transpose(0, 2, 1, 3).reshape(G, P, -1),
            a["L0_cond2_b_up"].reshape(G, H0 // P, P).transpose(0, 2, 1),
            a["L0_cond2_b_gate"].reshape(G, H0 // P, P).transpose(0, 2, 1)], axis=2).reshape(G * P, PK0),
        "b_down": a["L0_cond2_b_down"],
        "WgT": cols(a["L0_ffn_Wg"].T, KD),
        "packF": np.concatenate([
            a["L0_ffn_W1"].reshape(G, KD, P, 2 * I0).transpose(0, 2, 1, 3).reshape(G, P, -1),
            a["L0_ffn_W2"].reshape(G, I0 // P, P, D).transpose(0, 2, 1, 3).reshape(G, P, -1)], axis=2),
        "pack1": np.concatenate([
            a["L1_cond_skill_gate"].reshape(G, KD, P, I1).transpose(0, 2, 1, 3).reshape(G, P, -1),
            a["L1_cond_skill_up"].reshape(G, KD, P, I1).transpose(0, 2, 1, 3).reshape(G, P, -1),
            a["L1_cond_skill_down"].reshape(G, I1 // P, P, D).transpose(0, 2, 1, 3).reshape(G, P, -1)], axis=2).reshape(G * P, PK1),
        "shared": np.concatenate([cols(a["L1_cond_shared_gate"], KD).reshape(P, -1), cols(a["L1_cond_shared_up"], KD).reshape(P, -1),
                                  cols(a["L1_cond_shared_down"], I1 // P).reshape(P, -1)], axis=1),
        "gru_w": np.stack([cols(a["L1_attn_Wg"].T, KD), cols(a["L1_attn_Wc"].T, KD)], axis=1),
        "gru_b": np.stack([a["L1_attn_bg"].reshape(KD, P).T, a["L1_attn_bc"].reshape(KD, P).T], axis=1),
        "base_w": cols(a["L1_cond2_W_base"].T, KD),
        "base_bias": a["L1_cond2_b_base"].reshape(KD, P).T,
        "lora_a": a["L1_cond2_As"].reshape(G * R, D),
        "lora_b": a["L1_cond2_Bs"].transpose(0, 2, 1).reshape(G * R, D),
        "ffn_w1": cols(a["L1_ffn_W1"].T, KD),
        "ffn_b1": a["L1_ffn_b1"].reshape(FF // P, P).T,
        "ffn_w2": cols(a["L1_ffn_W2"].T, FF // P),
        "ffn_b2": a["L1_ffn_b2"].reshape(KD, P).T,
    }
    arrays = {k: np.ascontiguousarray(v) for k, v in arrays.items()}
    nc = _bacc.Bacc("TRN2", target_bir_lowering=False, num_devices=1)
    A = {k: nc.dram_tensor(f"in_{k}", v.shape, mybir.dt.from_np(v.dtype), kind="ExternalInput").ap() for k, v in arrays.items()}
    out = nc.dram_tensor("out_xT", (P, KD, N), F32, kind="ExternalOutput").ap()
    program(nc, A, out)
    r = _run(nc, [{f"in_{k}": v for k, v in arrays.items()}], core_ids=[0])
    got = r.results[0]["out_xT"]
    return np.ascontiguousarray(got.transpose(1, 0, 2).reshape(D, N).T.reshape(B, T, D))
```
